# Optimizing a Trainium2 kernel written in Bass

```python
import numpy as np
import jax
import jax.numpy as jnp

def _softmax(x, axis=-1):
    return jax.nn.softmax(x, axis=axis)

def _gelu(x):
    return jax.nn.gelu(x, approximate=True)

def _silu(x):
    return jax.nn.silu(x)

def _sigmoid(x):
    return jax.nn.sigmoid(x)

def _layernorm(x, axis=-1, eps=1e-05):
    m = jnp.mean(x, axis=axis, keepdims=True)
    v = jnp.var(x, axis=axis, keepdims=True)
    return (x - m) / jnp.sqrt(v + eps)

def _scatter_add(tgt, idx, src, axis=0):
    return tgt.at[idx].add(src)

def _segment_sum(src, seg, n):
    return jax.ops.segment_sum(src, seg, n)
kernel_name = 'mk_recurrent_d2_jaxref_r8_cf61c7'

def setup_inputs(seed: int=0):
    np.random.seed(seed)
    _w = jnp.asarray

    def _L0_attn_setup():
        import jax, jax.numpy as jnp
        import numpy as np
        B, N, D = (8, 128, 512)
        H = 8
        HEAD_DIM = D // H
        E = HEAD_DIM // H
        key = jax.random.key(seed)
        ks = jax.random.split(key, 7)
        s = 0.02
        return {'x': jax.random.normal(ks[0], (B, N, D), dtype=jnp.float32), 'Wqk_w': jax.random.normal(ks[1], (2 * HEAD_DIM, D), dtype=jnp.float32) * s, 'Wqk_b': jnp.zeros((2 * HEAD_DIM,), dtype=jnp.float32), 'Wv_w': jax.random.normal(ks[2], (HEAD_DIM, D), dtype=jnp.float32) * s, 'Wv_b': jnp.zeros((HEAD_DIM,), dtype=jnp.float32), 'Wo_w': jax.random.normal(ks[3], (D, HEAD_DIM), dtype=jnp.float32) * s, 'Wo_b': jnp.zeros((D,), dtype=jnp.float32)}
    _L0_attn_in = _L0_attn_setup()

    def _L0_ffn_setup():
        import jax, jax.numpy as jnp
        import numpy as np
        R = 16
        NUM_EXPERTS = 8
        TOP_K = 2
        LORA_ALPHA = 32
        SCALING = LORA_ALPHA / R
        key = jax.random.key(seed)
        ks = jax.random.split(key, 6)
        d_in, d_out = (512, 512)
        x = jax.random.normal(ks[0], (4, 256, d_in), dtype=jnp.float32)
        W_base = jax.random.normal(ks[1], (d_out, d_in), dtype=jnp.float32) * 0.02
        b_base = jax.random.normal(ks[2], (d_out,), dtype=jnp.float32) * 0.02
        W_router = jax.random.normal(ks[3], (NUM_EXPERTS, d_in), dtype=jnp.float32) * 0.01
        A = jax.random.normal(ks[4], (NUM_EXPERTS, R, d_in), dtype=jnp.float32) * 0.02
        B = jax.random.normal(ks[5], (NUM_EXPERTS, d_out, R), dtype=jnp.float32) * 0.02
        return {'x': x, 'W_base': W_base, 'b_base': b_base, 'W_router': W_router, 'A': A, 'B': B}
    _L0_ffn_in = _L0_ffn_setup()

    def _L1_attn_setup():
        import jax, jax.numpy as jnp
        import numpy as np
        import math
        B, S, DM = (1, 256, 512)
        H, HKV, HD = (32, 8, 128)
        EPS = 1e-06
        NEG_INF = -1e+30

        def _alibi_slopes(n_heads: int) -> np.ndarray:
            start = 2 ** (-2 ** (-(math.log2(n_heads) - 3)))
            return np.array([start * start ** i for i in range(n_heads)], dtype=np.float32)

        def _rmsnorm(t, w):
            tf = t.astype(jnp.float32)
            inv = jax.lax.rsqrt(jnp.mean(tf * tf, axis=-1, keepdims=True) + EPS)
            return (tf * inv * w).astype(t.dtype)
        key = jax.random.key(seed)
        ks = jax.random.split(key, 5)
        std = 0.02
        return {'x': jax.random.normal(ks[0], (B, S, DM), dtype=jnp.float32), 'Wq': jax.random.normal(ks[1], (H * HD, DM), dtype=jnp.float32) * std, 'Wk': jax.random.normal(ks[2], (HKV * HD, DM), dtype=jnp.float32) * std, 'Wv': jax.random.normal(ks[3], (HKV * HD, DM), dtype=jnp.float32) * std, 'Wo': jax.random.normal(ks[4], (H * HD, DM), dtype=jnp.float32).T * (std / math.sqrt(2 * 32)), 'q_norm_w': jnp.ones((HD,), dtype=jnp.float32), 'k_norm_w': jnp.ones((HD,), dtype=jnp.float32)}
    _L1_attn_in = _L1_attn_setup()

    def _L1_ffn_setup():
        import jax, jax.numpy as jnp
        import numpy as np
        NF4 = jnp.array([-1.0, -0.6961928009986877, -0.5250730514526367, -0.39491748809814453, -0.28444138169288635, -0.18477343022823334, -0.09105003625154495, 0.0, 0.07958029955625534, 0.16093020141124725, 0.24611230194568634, 0.33791524171829224, 0.44070982933044434, 0.5626170039176941, 0.7229568362236023, 1.0], dtype=jnp.float32)
        BLOCK = 64
        B, S, D, H, R = (2, 256, 512, 1376, 16)

        def dequant_nf4(codes, absmax, shape):
            vals = NF4[codes] * jnp.repeat(absmax, BLOCK)
            return vals.reshape(shape)
        key = jax.random.key(seed)
        ks = jax.random.split(key, 11)
        n_w = H * D
        return {'x1': jax.random.normal(ks[0], (B, S, D), dtype=jnp.float32), 'w_up_codes': jax.random.randint(ks[1], (n_w,), 0, 16, dtype=jnp.int32), 'w_up_absmax': jax.random.uniform(ks[2], (n_w // BLOCK,), dtype=jnp.float32) * 0.05, 'b_up': jax.random.normal(ks[3], (H,), dtype=jnp.float32) * 0.02, 'w_up_lora_a': jax.random.normal(ks[4], (D, R), dtype=jnp.float32) * 0.02, 'w_up_lora_b': jax.random.normal(ks[5], (R, H), dtype=jnp.float32) * 0.02, 'w_down_codes': jax.random.randint(ks[6], (n_w,), 0, 16, dtype=jnp.int32), 'w_down_absmax': jax.random.uniform(ks[7], (n_w // BLOCK,), dtype=jnp.float32) * 0.05, 'b_down': jax.random.normal(ks[8], (D,), dtype=jnp.float32) * 0.02, 'w_down_lora_a': jax.random.normal(ks[9], (H, R), dtype=jnp.float32) * 0.02, 'w_down_lora_b': jax.random.normal(ks[10], (R, D), dtype=jnp.float32) * 0.02}
    _L1_ffn_in = _L1_ffn_setup()
    _d = {'L0_attn_x': _L0_attn_in['x'], 'L0_attn_Wqk_w': _L0_attn_in['Wqk_w'], 'L0_attn_Wqk_b': _L0_attn_in['Wqk_b'], 'L0_attn_Wv_w': _L0_attn_in['Wv_w'], 'L0_attn_Wv_b': _L0_attn_in['Wv_b'], 'L0_attn_Wo_w': _L0_attn_in['Wo_w'], 'L0_attn_Wo_b': _L0_attn_in['Wo_b'], 'L0_ffn_W_base': _L0_ffn_in['W_base'], 'L0_ffn_b_base': _L0_ffn_in['b_base'], 'L0_ffn_W_router': _L0_ffn_in['W_router'], 'L0_ffn_A': _L0_ffn_in['A'], 'L0_ffn_B': _L0_ffn_in['B'], 'L1_attn_Wq': _L1_attn_in['Wq'], 'L1_attn_Wk': _L1_attn_in['Wk'], 'L1_attn_Wv': _L1_attn_in['Wv'], 'L1_attn_Wo': _L1_attn_in['Wo'], 'L1_attn_q_norm_w': _L1_attn_in['q_norm_w'], 'L1_attn_k_norm_w': _L1_attn_in['k_norm_w'], 'L1_ffn_w_up_codes': _L1_ffn_in['w_up_codes'], 'L1_ffn_w_up_absmax': _L1_ffn_in['w_up_absmax'], 'L1_ffn_b_up': _L1_ffn_in['b_up'], 'L1_ffn_w_up_lora_a': _L1_ffn_in['w_up_lora_a'], 'L1_ffn_w_up_lora_b': _L1_ffn_in['w_up_lora_b'], 'L1_ffn_w_down_codes': _L1_ffn_in['w_down_codes'], 'L1_ffn_w_down_absmax': _L1_ffn_in['w_down_absmax'], 'L1_ffn_b_down': _L1_ffn_in['b_down'], 'L1_ffn_w_down_lora_a': _L1_ffn_in['w_down_lora_a'], 'L1_ffn_w_down_lora_b': _L1_ffn_in['w_down_lora_b']}
    _x0 = _d['L0_attn_x']
    _d['L0_attn_x'] = jax.random.normal(jax.random.fold_in(jax.random.key(seed), 1), (1, 1024, 512), dtype=_x0.dtype)
    del _x0
    return _d

def reference(L0_attn_x, L0_attn_Wqk_w, L0_attn_Wqk_b, L0_attn_Wv_w, L0_attn_Wv_b, L0_attn_Wo_w, L0_attn_Wo_b, L0_ffn_W_base, L0_ffn_b_base, L0_ffn_W_router, L0_ffn_A, L0_ffn_B, L1_attn_Wq, L1_attn_Wk, L1_attn_Wv, L1_attn_Wo, L1_attn_q_norm_w, L1_attn_k_norm_w, L1_ffn_w_up_codes, L1_ffn_w_up_absmax, L1_ffn_b_up, L1_ffn_w_up_lora_a, L1_ffn_w_up_lora_b, L1_ffn_w_down_codes, L1_ffn_w_down_absmax, L1_ffn_b_down, L1_ffn_w_down_lora_a, L1_ffn_w_down_lora_b):

    def _L0_attn_ref(x, Wqk_w, Wqk_b, Wv_w, Wv_b, Wo_w, Wo_b):
        import jax, jax.numpy as jnp
        import numpy as np
        B, N, D = (8, 128, 512)
        H = 8
        HEAD_DIM = D // H
        E = HEAD_DIM // H
        b, n, _ = x.shape
        qk = (x @ Wqk_w.T + Wqk_b).reshape(b, n, H, E, 2)
        q = jnp.transpose(qk[..., 0], (0, 2, 1, 3))
        k = jnp.transpose(qk[..., 1], (0, 2, 1, 3))
        v = (x @ Wv_w.T + Wv_b).reshape(b, n, H, E)
        v = jnp.transpose(v, (0, 2, 1, 3))
        scores = jnp.einsum('bhqd,bhkd->bhqk', q, k)
        attn = jax.nn.softmax(scores, axis=-1) / jnp.asarray(HEAD_DIM ** 0.5, x.dtype)
        out = jnp.einsum('bhsl,bhlv->bhsv', attn, v)
        out = jnp.transpose(out, (0, 2, 1, 3)).reshape(b, n, H * E)
        return out @ Wo_w.T + Wo_b

    def _L0_ffn_ref(x, W_base, b_base, W_router, A, B):
        import jax, jax.numpy as jnp
        import numpy as np
        R = 16
        NUM_EXPERTS = 8
        TOP_K = 2
        LORA_ALPHA = 32
        SCALING = LORA_ALPHA / R
        orig_shape = x.shape
        d_in = x.shape[-1]
        x_flat = x.reshape(-1, d_in)
        logits = x_flat @ W_router.T
        probs = jax.nn.softmax(logits, axis=-1)
        topk_probs, topk_idx = jax.lax.top_k(probs, TOP_K)
        topk_probs = topk_probs / jnp.sum(topk_probs, axis=-1, keepdims=True)
        onehot = jax.nn.one_hot(topk_idx, NUM_EXPERTS, dtype=x.dtype)
        combine = jnp.einsum('nk,nke->ne', topk_probs, onehot)
        h = jnp.einsum('nd,erd->ner', x_flat, A)
        hw = h * combine[:, :, None]
        expert_out = jnp.einsum('ner,eor->no', hw, B) * SCALING
        base_out = x_flat @ W_base.T + b_base
        out = base_out + expert_out
        return out.reshape(*orig_shape[:-1], W_base.shape[0])

    def _L1_attn_ref(x, Wq, Wk, Wv, Wo, q_norm_w, k_norm_w):
        import jax, jax.numpy as jnp
        import numpy as np
        import math
        B, S, DM = (1, 256, 512)
        H, HKV, HD = (32, 8, 128)
        EPS = 1e-06
        NEG_INF = -1e+30

        def _alibi_slopes(n_heads: int) -> np.ndarray:
            start = 2 ** (-2 ** (-(math.log2(n_heads) - 3)))
            return np.array([start * start ** i for i in range(n_heads)], dtype=np.float32)

        def _rmsnorm(t, w):
            tf = t.astype(jnp.float32)
            inv = jax.lax.rsqrt(jnp.mean(tf * tf, axis=-1, keepdims=True) + EPS)
            return (tf * inv * w).astype(t.dtype)
        b, s, _ = x.shape
        G = H // HKV
        q = (x @ Wq.T).reshape(b, s, H, HD).transpose(0, 2, 1, 3)
        k = (x @ Wk.T).reshape(b, s, HKV, HD).transpose(0, 2, 1, 3)
        v = (x @ Wv.T).reshape(b, s, HKV, HD).transpose(0, 2, 1, 3)
        q = _rmsnorm(q, q_norm_w)
        k = _rmsnorm(k, k_norm_w)
        qg = q.reshape(b, HKV, G, s, HD)
        scores = jnp.einsum('bkgqd,bksd->bkgqs', qg, k) / math.sqrt(HD)
        slopes = jnp.asarray(_alibi_slopes(H)).reshape(HKV, G)
        pos = jnp.arange(s, dtype=jnp.float32)
        rel = pos[None, :] - pos[:, None]
        bias = jnp.where(rel > 0, NEG_INF, slopes[:, :, None, None] * rel)
        attn = jax.nn.softmax(scores + bias[None], axis=-1)
        out = jnp.einsum('bkgqs,bksd->bkgqd', attn, v)
        out = out.reshape(b, H, s, HD).transpose(0, 2, 1, 3).reshape(b, s, H * HD)
        return out @ Wo.T

    def _L1_ffn_ref(x1, w_up_codes, w_up_absmax, b_up, w_up_lora_a, w_up_lora_b, w_down_codes, w_down_absmax, b_down, w_down_lora_a, w_down_lora_b):
        import jax, jax.numpy as jnp
        import numpy as np
        NF4 = jnp.array([-1.0, -0.6961928009986877, -0.5250730514526367, -0.39491748809814453, -0.28444138169288635, -0.18477343022823334, -0.09105003625154495, 0.0, 0.07958029955625534, 0.16093020141124725, 0.24611230194568634, 0.33791524171829224, 0.44070982933044434, 0.5626170039176941, 0.7229568362236023, 1.0], dtype=jnp.float32)
        BLOCK = 64
        B, S, D, H, R = (2, 256, 512, 1376, 16)

        def dequant_nf4(codes, absmax, shape):
            vals = NF4[codes] * jnp.repeat(absmax, BLOCK)
            return vals.reshape(shape)
        w_up = dequant_nf4(w_up_codes, w_up_absmax, (H, D)).T
        y1 = x1 @ w_up + b_up + x1 @ w_up_lora_a @ w_up_lora_b
        x2 = jax.nn.relu(y1)
        w_down = dequant_nf4(w_down_codes, w_down_absmax, (D, H)).T
        y2 = x2 @ w_down + b_down + x2 @ w_down_lora_a @ w_down_lora_b
        return y2
    x = L0_attn_x
    xn = _layernorm(x, axis=-1)
    s = _L0_attn_ref(xn, L0_attn_Wqk_w, L0_attn_Wqk_b, L0_attn_Wv_w, L0_attn_Wv_b, L0_attn_Wo_w, L0_attn_Wo_b)
    g = _silu(_L0_ffn_ref(xn, L0_ffn_W_base, L0_ffn_b_base, L0_ffn_W_router, L0_ffn_A, L0_ffn_B))
    x = x + s * g
    xn = _layernorm(x, axis=-1)
    s = _L1_attn_ref(xn, L1_attn_Wq, L1_attn_Wk, L1_attn_Wv, L1_attn_Wo, L1_attn_q_norm_w, L1_attn_k_norm_w)
    g = _silu(_L1_ffn_ref(xn, L1_ffn_w_up_codes, L1_ffn_w_up_absmax, L1_ffn_b_up, L1_ffn_w_up_lora_a, L1_ffn_w_up_lora_b, L1_ffn_w_down_codes, L1_ffn_w_down_absmax, L1_ffn_b_down, L1_ffn_w_down_lora_a, L1_ffn_w_down_lora_b))
    x = x + s * g
    return x

_drawn_inputs = setup_inputs


def setup_inputs(seed=0):
    import zlib

    import numpy as np

    out = dict(_drawn_inputs(seed))
    spreads = {'L0_attn_Wqk_b': (0.0, 0.8),
     'L0_attn_Wv_b': (0.0, 0.8),
     'L0_attn_Wo_b': (0.0, 0.1),
     'L1_attn_q_norm_w': (1.0, 0.6),
     'L1_attn_k_norm_w': (1.0, 0.6)}
    factors = {'L0_attn_Wqk_w': 8.0,
     'L0_attn_Wv_w': 8.0,
     'L0_attn_Wo_w': 8.0,
     'L0_ffn_b_base': 8.0,
     'L0_ffn_W_router': 8.0,
     'L0_ffn_A': 8.0,
     'L0_ffn_B': 8.0,
     'L1_attn_Wq': 8.0,
     'L1_attn_Wk': 8.0,
     'L1_attn_Wv': 8.0,
     'L1_attn_Wo': 8.0,
     'L1_ffn_w_up_absmax': 8.0,
     'L1_ffn_b_up': 8.0,
     'L1_ffn_w_up_lora_a': 8.0,
     'L1_ffn_w_up_lora_b': 8.0,
     'L1_ffn_w_down_absmax': 8.0,
     'L1_ffn_b_down': 56.056,
     'L1_ffn_w_down_lora_a': 8.0,
     'L1_ffn_w_down_lora_b': 8.0}
    for name, (base, spread) in spreads.items():
        noise = np.random.default_rng([zlib.crc32(name.encode()), seed]).standard_normal(out[name].shape)
        drawn = base * np.exp(spread * noise) if base else spread * noise
        out[name] = jnp.asarray(drawn.astype(out[name].dtype))
    for name, factor in factors.items():
        out[name] = (out[name] * factor).astype(out[name].dtype)
    return out
```

```python
import math
import numpy as np
import concourse.bass as bass
from concourse import mybir
from contextlib import ExitStack

F32 = mybir.dt.float32
F32R = mybir.dt.float32r
I32 = mybir.dt.int32
ALU = mybir.AluOpType
ACT = mybir.ActivationFunctionType
AX = mybir.AxisListType

P = 128
TOK, D = 1024, 512
NT, KT = TOK // P, D // P
H0, E0 = 8, 8
NEXP, RANK0 = 8, 16
HKV, GRP, HD = 8, 4, 128
FF, RANK1 = 1376, 16
FT = -(-FF // P)
LN_EPS, RMS_EPS = 1e-5, 1e-6

WQK_H, WQK_L = 0, 2048
WBASE_H, WBASE_L = 4096, 6144
WVAR_H, WVAR_L = 8192, 8992
WEXP_H, WEXP_L = 9792, 10304
WO0_H, WO0_L = 10816, 11328
QS, KS = 11840, 13888
VPAD = 0
W_H, W_L = 0, 5120
WOUT = KT * 768
QT = 10240
KTR = 12288
VN = 14336
PT = 16384
OT = 19456
ARENA = 21504
FW = 0
X2 = 6144
LA_H, LA_L = 8192, 8704
LB_H, LB_L = 9216, 10624
DLA_H, DLA_L = 12032, 13440
DLB_H, DLB_L = 14848, 15360
XLA = 15872
ZT = 16896

C_ID = 0
C_TRI = C_ID + P
C_MASK = C_TRI + NEXP * NEXP
C_BQK = C_MASK + 4
C_QKW = C_BQK + 4
C_BUP = C_QKW + 2
C_SLOPE = C_BUP + FT
C_ISL = C_SLOPE + HKV * GRP
C_EXP = C_ISL + HKV * 5
C_BD = C_EXP + 9
NCONST = C_BD + D
R_BV, R_BO, R_BB = 0, 64, 64 + D
NROWS = 64 + 2 * D

NF4 = [-1.0, -0.6961928009986877, -0.5250730514526367, -0.39491748809814453, -0.28444138169288635,
       -0.18477343022823334, -0.09105003625154495, 0.0, 0.07958029955625534, 0.16093020141124725,
       0.24611230194568634, 0.33791524171829224, 0.44070982933044434, 0.5626170039176941,
       0.7229568362236023, 1.0]
LINES = [(NF4[2 * k + 1] - NF4[2 * k], NF4[2 * k] - 2 * k * (NF4[2 * k + 1] - NF4[2 * k])) for k in range(8)]
DQN = 704
NDQ = FT * 1024 // DQN

RAWC = 768


def _cut(src, hi, lo, n, step):
    return [(src + a, hi + a, lo + a, min(step, n - a)) for a in range(0, n, step)]


L0_CHUNKS = (_cut(0, WQK_H, WQK_L, 2048, RAWC) + _cut(2048, WVAR_H, WVAR_L, 800, 400)
             + _cut(2848, WBASE_H, WBASE_L, 2048, RAWC) + _cut(4896, WEXP_H, WEXP_L, 512, 512)
             + _cut(5408, WO0_H, WO0_L, 512, 512))
W0_QK, W0_VAR, W0_BASE, W0_EXP, W0_O = 3, 5, 8, 9, 10
NL0 = len(L0_CHUNKS)
QL1 = NL0
QFF = QL1 + 8 * HKV
FF_CHUNKS = ([(0, LA_H, LA_L, 512, P)] + [(512 + a, LB_H + a, LB_L + a, 704, RANK1) for a in (0, 704)]
             + [(1920 + a, DLA_H + a, DLA_L + a, 704, P) for a in (0, 704)] + [(3328, DLB_H, DLB_L, 512, RANK1)])
NFFC = len(FF_CHUNKS)

STEPS = NT * HKV


def slot_items(n):
    i = n % NT
    nk = i + 1
    group = {a: [kb for kb in range(nk) if 3 - (nk - 1 - kb) * 4 // nk == a] for a in range(4)}
    s1, s2 = n + 1 < STEPS, n + 2 < STEPS
    seq = []

    def put(*names, when=True):
        if when:
            seq.extend(names)

    put("V")
    for a in range(4):
        put(("S", a), when=s1)
        if a == 1:
            put("PQ", "PKV", when=s2)
        if a == 2:
            put("QN", when=s2)
        if a > 0:
            put(("NR", a - 1), when=s1)
        put(*[("T", kb) for kb in group[a]])
        if a == 0:
            put("WO", when=n > 0)
        put(("EX", a), when=s1)
        if a == 1:
            put("DA")
    put("QK", when=s2)
    put(("NR", 3), when=s1)
    put("E", "DB")
    return seq


T_LN0, T_QK, T_VAR, T_HW, T_ATT = 0, 8, 16, 24, 32
T_LN1 = T_ATT + 2 * H0 * NT
T_PRO = T_LN1 + NT
T_BASE = T_PRO + 6
S_ATT, S_PRO = NT, NT + 2 * H0 * 4
S_BASE = S_PRO + 4
W_PRO = NT
W_BASE = W_PRO + 2
PV_BASE = 2 * H0 * NT
OT_BASE = 2
EX_PRO = 2 * H0 * 4
EX_BASE = EX_PRO + 4
P_PER, V_PER = 64, 3


def _tables():
    t, s, w, pv = T_BASE, S_BASE, W_BASE, PV_BASE
    at = {}
    for n in range(STEPS):
        for x in slot_items(n):
            if x in ("PKV",) or x[0] == "T":
                at[n, x] = t
                t += 1
            elif x == "QK":
                at[n, "QT"], at[n, "KT"] = t, t + 1
                t += 2
            elif x[0] == "S":
                at[n, x] = s
                s += 1
            elif x in ("PQ", "WO"):
                at[n, x] = w
                w += 1
        at[n, "last"] = t - 1
        for kb in range(n % NT + 1):
            at[n, ("PV", kb)] = pv
            pv += 1
    at[STEPS, "WO"] = w
    return at, t, s, w + 1, pv


AT, T_END, S_END, W_END, PV_END = _tables()


def at(g, i, name):
    if isinstance(g, int):
        return AT[8 * g + i, name]
    return g * (AT[8 + i, name] - AT[i, name]) + AT[i, name]


def hold(eng, sem, value, passed):
    eng.wait_ge(sem, value)
    if not isinstance(value, int):
        eng.sem_inc(passed, 1)


class Tally:

    def __init__(self, eng, sem, passed):
        self.eng, self.sem, self.passed, self.base, self.n = eng, sem, passed, 0, 0

    def done(self, ins):
        ins.then_inc(self.sem, 1)
        self.n += 1

    def settle(self):
        hold(self.eng, self.sem, self.base + self.n, self.passed)

    def link(self, ins):
        self.done(ins)
        self.settle()


def slots(eng, tallies, slot):
    slot(0, 0)
    start = [t.n for t in tallies]
    probe = []
    with eng.Fori(0, HKV - 1) as g:
        for t in tallies:
            t.n = 0
            t.base = t.per * g + start[tallies.index(t)]
        for i in range(1, NT + 1):
            slot(g, i)
        for t in tallies:
            assert t.n == t.per, (t.n, t.per)
            probe.append(t.n)
    for t, s in zip(tallies, start):
        t.base, t.n = 0, s + (HKV - 1) * t.per
    for i in range(1, NT):
        slot(HKV - 1, i)


def program(nc, x, w0, w1, codes, absmax, lora, consts, rows, rel, out):
    with ExitStack() as ctx:
        def sb(name, shape, dt=F32):
            return ctx.enter_context(nc.sbuf_tensor(name, shape, dt))

        def sem(name):
            return ctx.enter_context(nc.semaphore(name))

        x1_dram = nc.dram_tensor("x1_scratch", (TOK, D), F32, kind="Internal").ap()
        wd_dram = nc.dram_tensor("dequantised", (P, FT * 1024), F32, kind="Internal").ap()

        XT = sb("XT", [P, 2, KT, TOK], F32R)
        R = sb("R", [P, ARENA], F32R)
        G = sb("G", [P, NT * D])
        PB = sb("PB", [P, 2, 4, TOK])
        REL = sb("REL", [P, TOK])
        RAW = sb("RAW", [P, 2, RAWC])
        QN = sb("QN", [P, 5 * HD])
        VS = sb("VS", [P, 4, HD])
        DQ = sb("DQ", [P, 4, DQN])
        C = sb("C", [P, NCONST])
        JUNK = sb("JUNK", [P, 10, HD], mybir.dt.bfloat16)
        MX = sb("MX", [P, 8])
        NM = sb("NM", [P, 8])
        SM = sb("SM", [P, 8])
        RI = sb("RI", [P, 8])
        SQ = sb("SQ", [P, 2, 5])
        SQB = sb("SQB", [P, 2, 5])
        SQC = sb("SQC", [P, 2, 5])
        INV = sb("INV", [P, 2, 5])
        SLC = sb("SLC", [P, 4])
        QKW = sb("QKW", [P, 2])
        ST = sb("ST", [P, 2, 6])
        MV = sb("MV", [P, 2, 2])
        VE = sb("VE", [P, 2])
        RSTD = sb("RSTD", [P, 2])
        CMP = sb("CMP", [P, 2, 512])
        RT = sb("RT", [P, 8, 64])

        LA = DQ[:, :, :].rearrange("p a n -> p (a n)")
        HN = LA[:, 0:1024]
        VN0 = LA[:, 1024:1536]
        ROWS = LA[:, 1536:1536 + NROWS]
        PBF = PB[:, :, :, :].rearrange("p a b n -> p (a b n)")
        XS = [PBF[:, t * D:(t + 1) * D] for t in range(4)]
        XN = [PBF[:, (4 + t) * D:(5 + t) * D] for t in range(4)]
        TMP = [PBF[:, (8 + t) * D:(9 + t) * D] for t in range(6)]
        CODES = DQ[:, 0, :].bitcast(I32)
        IDENT = C[:, C_ID:C_ID + P]

        S = [ctx.enter_context(nc.psum_tensor(f"S{k}", [P, 1024], F32)) for k in range(2)]
        T = [ctx.enter_context(nc.psum_tensor(f"T{k}", [P, 512], F32)) for k in range(2)]
        VB = ctx.enter_context(nc.psum_tensor("VB", [P, 512], F32))
        WB = ctx.enter_context(nc.psum_tensor("WB", [P, 512], F32))

        in_const = sem("in_const")
        in_rows = sem("in_rows")
        in_x = [sem(f"in_x{k}") for k in range(4)]
        in_raw = [sem(f"in_raw{k}") for k in range(2)]
        in_codes = sem("in_codes")
        in_absmax = sem("in_absmax")
        in_fw = [sem(f"in_fw{k}") for k in range(2)]
        in_x1 = [sem(f"in_x1{k}") for k in range(4)]
        out_x1 = [sem(f"out_x1{k}") for k in range(4)]
        out_dq = sem("out_dq")
        out_y = [sem(f"out_y{k}") for k in range(4)]
        t_full = sem("t_full")
        t_act = sem("t_act")
        t_free = sem("t_free")
        s_full = sem("s_full")
        s_free = sem("s_free")
        w_full = sem("w_full")
        w_free = sem("w_free")
        pv_done = sem("pv_done")
        ot_high = sem("ot_high")
        ot_low = sem("ot_low")
        max_ready = sem("max_ready")
        neg_ready = sem("neg_ready")
        exp_done = sem("exp_done")
        probs_ready = sem("probs_ready")
        split = sem("split")
        vpad_ready = sem("vpad_ready")
        v_split = sem("v_split")
        squares = sem("squares")
        inv_ready = sem("inv_ready")
        qk_ready = sem("qk_ready")
        var_ready = sem("var_ready")
        rstd_ready = sem("rstd_ready")
        xn_ready = sem("xn_ready")
        x1_ready = sem("x1_ready")
        row_ready = sem("row_ready")
        row_exp = sem("row_exp")
        hw_ready = sem("hw_ready")
        y_ready = sem("y_ready")
        y_tanh = sem("y_tanh")
        gate_done = sem("gate_done")
        line = sem("line")
        line_used = sem("line_used")
        dq_selected = sem("dq_selected")
        dq_scaled = sem("dq_scaled")
        fw_split = sem("fw_split")
        x2_ready = sem("x2_ready")
        z_high = sem("z_high")
        z_low = sem("z_low")
        d_full = sem("d_full")
        d_free = sem("d_free")
        out_done = sem("out_done")
        a_chain = sem("a_chain")
        v_chain = sem("v_chain")
        p_chain = sem("p_chain")
        v_passed = sem("v_passed")
        p_passed = sem("p_passed")

        block = ctx.enter_context(nc.Block())

        def r(off, n, p=P):
            return R[0:p, off:off + n]

        def rf(off, n, p=P):
            return R[0:p, off:off + n].bitcast(F32)

        @block.sync
        def _(sp):
            sp.dma_start(C[:, :], consts).then_inc(in_const, 16)
            for t in range(4):
                sp.dma_start(XS[t], x[t * P:(t + 1) * P, :]).then_inc(in_x[t], 16)

            def raw(q, src, rows_=P):
                if q >= 2:
                    sp.wait_ge(split, q - 1)
                n = src.shape[-1]
                sp.dma_start(RAW[0:rows_, q % 2, 0:n], src).then_inc(in_raw[q % 2], 16)

            for q in range(2):
                src, _, _, n = L0_CHUNKS[q]
                raw(q, w0[:, src:src + n])
            sp.dma_start(ROWS, rows).then_inc(in_rows, 16)
            for t in range(4, NT):
                sp.wait_ge(xn_ready, t - 3)
                sp.dma_start(XS[t % 4], x[t * P:(t + 1) * P, :]).then_inc(in_x[t % 4], 16)
            sp.dma_start(REL[:, :], rel).then_inc(out_dq, 16)
            for q in range(2, NL0):
                src, _, _, n = L0_CHUNKS[q]
                raw(q, w0[:, src:src + n])

            def w1_chunk(g, c):
                q = QL1 + c
                a, n = (c * 768, 768) if c < 4 else (WOUT + (c - 4) * 512, 512)
                if isinstance(g, int):
                    raw(q + 8 * g, w1[g * P:(g + 1) * P, a:a + n])
                else:
                    sp.wait_ge(split, g * 8 + q - 1)
                    sp.dma_start(RAW[:, q % 2, 0:n], w1[bass.ds(g * P, P), a:a + n]).then_inc(in_raw[q % 2], 16)

            sp.wait_ge(t_full, T_ATT + (2 * H0 - 1) * NT)
            for t in range(4):
                sp.dma_start(XS[t], x[t * P:(t + 1) * P, :]).then_inc(in_x[t], 16)
            w1_chunk(0, 0)
            w1_chunk(0, 1)
            for t in range(NT):
                sp.wait_ge(x1_ready, t + 1)
                sp.dma_start(x1_dram[t * P:(t + 1) * P, :], XS[t % 4]).then_inc(out_x1[t % 4], 16)
                if t + 4 < NT:
                    sp.wait_ge(xn_ready, NT + t + 1)
                    sp.wait_ge(out_x1[t % 4], 16)
                    sp.dma_start(XS[t % 4], x[(t + 4) * P:(t + 5) * P, :]).then_inc(in_x[t % 4], 16)
            for c in range(2, 8):
                w1_chunk(0, c)

            def load_codes(g, i):
                if isinstance(g, int):
                    cc = (8 * g + i) // 4
                    if cc:
                        sp.wait_ge(dq_selected, cc)
                    else:
                        sp.wait_ge(xn_ready, 2 * NT)
                        sp.wait_ge(t_free, T_LN1 + NT)
                    sp.dma_start(CODES, codes[cc * P:(cc + 1) * P, :]).then_inc(in_codes, 16)
                else:
                    sp.wait_ge(dq_selected, g * 2 + i // 4)
                    sp.dma_start(CODES, codes[bass.ds(g * (2 * P) + i // 4 * P, P), :]).then_inc(in_codes, 16)

            def slot(g, i):
                jj = i % 4
                if jj == 0:
                    load_codes(g, i)
                if not (isinstance(g, int) and g == HKV - 1):
                    if i == 1:
                        w1_chunk(g + 1, 0)
                        w1_chunk(g + 1, 1)
                    if i == 5:
                        w1_chunk(g + 1, 2)
                        w1_chunk(g + 1, 3)
                    if i == 6:
                        w1_chunk(g + 1, 4)
                        w1_chunk(g + 1, 5)
                    if i == 8:
                        w1_chunk(g + 1, 6)
                        w1_chunk(g + 1, 7)
                if jj == 0 and not (isinstance(g, int) and 8 * g + i == 0):
                    sp.wait_ge(dq_scaled, g * 2 + (i // 4 + 1))
                    sp.dma_start(wd_dram[:, bass.ds(g * (2 * DQN) + (i // 4 - 1) * DQN, DQN)], DQ[:, 1, :])\
                        .then_inc(out_dq, 16)
                if jj == 3:
                    sp.wait_ge(dq_selected, g * 2 + i // 4 + 1)
                    sp.dma_start(DQ[:, 3, :], absmax[bass.ds(g * (2 * P) + i // 4 * P, P), :]).then_inc(in_absmax, 16)

            slots(sp, [], slot)
            sp.wait_ge(dq_scaled, NDQ + 1)
            sp.dma_start(wd_dram[:, (NDQ - 1) * DQN:NDQ * DQN], DQ[:, 1, :]).then_inc(out_dq, 16)
            for q, (src, _, _, n, np_) in enumerate(FF_CHUNKS):
                raw(QFF + q, lora[0:np_, src:src + n], np_)
            sp.wait_ge(out_dq, 16 * (NDQ + 1))
            for u in range(2 * FT):
                if u >= 2:
                    sp.wait_ge(fw_split, u - 1)
                else:
                    sp.wait_ge(t_full, AT[STEPS - 1, "last"] + 1)
                sp.dma_start(PBF[:, u % 2 * 1024:(u % 2 + 1) * 1024],
                             wd_dram[:, u % FT * 1024:(u % FT + 1) * 1024]).then_inc(in_fw[u % 2], 16)
                if u in (0, FT + 5):
                    for tt in range(4):
                        t = u // FT * 4 + tt
                        if t >= 4:
                            sp.wait_ge(out_y[tt], 16)
                        sp.dma_start(PBF[:, (8 + tt) * D:(9 + tt) * D], x1_dram[t * P:(t + 1) * P, :])\
                            .then_inc(in_x1[tt], 16)
                if u == FT + 3 or u == 2 * FT - 1:
                    for tt in range(4):
                        t = u // (2 * FT - 1) * 4 + tt
                        sp.wait_ge(out_done, t + 1)
                        sp.dma_start(out[t * P:(t + 1) * P, :], PBF[:, (8 + tt) * D:(9 + tt) * D])\
                            .then_inc(out_y[tt], 16)
            for tt in range(4):
                sp.wait_ge(out_y[tt], 32)

        @block.gpsimd
        def _(pool):
            e = nc.gpsimd
            ch = Tally(pool, p_chain, p_passed)
            ch.per = P_PER

            def split_raw(q, hi, lo, n, np_=P, parity=None, first=None):
                k = q % 2 if parity is None else parity
                hold(pool, in_raw[k], 16 * (q // 2 + 1) if first is None else first, p_passed)
                ch.link(e.tensor_copy(r(hi, n, np_), RAW[0:np_, k, 0:n]))
                e.tensor_tensor(r(lo, n, np_), RAW[0:np_, k, 0:n], rf(hi, n, np_), ALU.subtract).then_inc(split, 1)

            def rstd(t):
                k = t % 2
                hold(pool, var_ready, t + 1, p_passed)
                ch.link(e.tensor_scalar(VE[:, k:k + 1], MV[:, k, 1:2], 1.0, LN_EPS, ALU.mult, ALU.add))
                e.tensor_tensor(RSTD[:, k:k + 1], VE[:, k:k + 1], C[:, C_EXP:C_EXP + 1], ALU.pow).then_inc(rstd_ready, 1)

            def divide(m, a, L, count, scale):
                k = m % 2 * 4 + a
                hold(pool, exp_done, count, p_passed)
                ch.link(e.tensor_tensor(RI[:, k:k + 1], SM[:, k:k + 1], C[:, C_EXP + 5:C_EXP + 6], ALU.pow))
                e.tensor_scalar(PB[:, m % 2, a, 0:L], PB[:, m % 2, a, 0:L], RI[:, k:k + 1], scale,
                                ALU.mult, ALU.mult).then_inc(probs_ready, 1)

            def negate(m, a, count):
                k = m % 2 * 4 + a
                hold(pool, s_free, count, p_passed)
                e.tensor_scalar(NM[:, k:k + 1], MX[:, k:k + 1], -1.0, 0.0, ALU.mult, ALU.add).then_inc(neg_ready, 1)

            def inverse_rms(g, m, count):
                k = m % 2
                hold(pool, squares, count, p_passed)
                ch.link(e.tensor_scalar(SQB[:, k, :], SQ[:, k, :], 1.0 / HD, RMS_EPS, ALU.mult, ALU.add))
                ch.link(e.tensor_tensor(SQC[:, k, :], SQB[:, k, :], C[:, C_EXP:C_EXP + 5], ALU.pow))
                e.tensor_tensor(INV[:, k, :], SQC[:, k, :], C[:, bass.ds(g * 5 + C_ISL, 5)], ALU.mult)\
                    .then_inc(inv_ready, 1)

            hold(pool, in_const, 16, p_passed)
            rstd(0)
            rstd(1)
            for q in range(NL0):
                src, hi, lo, n = L0_CHUNKS[q]
                split_raw(q, hi, lo, n)
                if 2 + q < NT:
                    rstd(2 + q)
            hold(pool, s_full, NT, p_passed)
            ch.link(e.memset(rf(VPAD, 8192), 0.0))
            hold(pool, t_free, T_VAR + NT, p_passed)
            src = VN0.rearrange("p (b h e) -> p b h e", b=NT, h=H0)

            whole = r(VPAD, 8192).rearrange("p (b n) -> p b n", b=NT)
            for h in range(H0):
                o = h * P + 2 * E0 * h
                hi_ap, lo_ap = whole[:, :, o:o + E0], whole[:, :, o + E0:o + 2 * E0]
                ch.link(e.tensor_copy(hi_ap, src[:, :, h, :]))
                e.tensor_tensor(lo_ap, src[:, :, h, :], hi_ap.bitcast(F32), ALU.subtract).then_inc(vpad_ready, 1)
            for n in range(2 * H0):
                for a in range(4):
                    divide(n, a, TOK, n * 4 + a + 1, 1.0 / math.sqrt(H0 * E0))
            for t in range(NT):
                rstd(NT + t)

            def w1_split(g, c):
                if isinstance(g, int):
                    q = QL1 + 8 * g + c
                    first = None
                else:
                    q = QL1 + c
                    first = g * 64 + 16 * (q // 2 + 1)
                off, n = (c * 768, 768) if c < 4 else (WOUT + (c - 4) * 512, 512)
                split_raw(q, W_H + off, W_L + off, n, parity=q % 2, first=first)

            hold(pool, w_full, NT, p_passed)
            for c in range(4):
                w1_split(0, c)
            inverse_rms(0, 0, 5)
            w1_split(0, 4)
            inverse_rms(0, 1, 10)
            for c in range(5, 8):
                w1_split(0, c)
            for a in range(4):
                negate(0, a, a + 1)
                divide(0, a, P, EX_PRO + a + 1, 1.0)

            def slot(g, i):
                n0 = g * 8 + i
                known = 8 * g + i if isinstance(g, int) else i
                last = isinstance(g, int) and g == HKV - 1
                L = (i + 1) % NT * P + P
                for it in slot_items(known if isinstance(g, int) else i):
                    if it == "V":
                        b = i % NT
                        if i < 2:
                            hold(pool, t_act, T_PRO + 3 * i + 1, p_passed)
                        if i >= 2:
                            hold(pool, t_act, at(g, i - 2, "PKV") + 1, p_passed)
                        elif i == 1:
                            hold(pool, t_act, g * 60 + (AT[NT - 1, "PKV"] - 60 + 1), p_passed)
                        if i == NT:
                            hold(pool, pv_done, at(g, NT - 1, ("PV", 0)) + 1, p_passed)
                        elif i:
                            hold(pool, pv_done, g * 36 + (AT[NT - 1, ("PV", b)] - 36 + 1), p_passed)
                        k = i % 4
                        ch.link(e.tensor_copy(r(VN + b * P, P), VS[:, k, :]))
                        e.tensor_tensor(r(VN + TOK + b * P, P), VS[:, k, :], rf(VN + b * P, P), ALU.subtract)\
                            .then_inc(v_split, 1)
                    elif it[0] == "S":
                        a = it[1]
                        negate(i + 1, a, at(g, i, it) + (1 - S_PRO))
                        if i == 6 and a == 0 and not last:
                            w1_split(g + 1, 3)
                        if i == 8 and a == 1:
                            w1_split(g + 1, 5)
                        if i == 8 and a == 2:
                            w1_split(g + 1, 7)
                    elif it[0] == "NR":
                        a = it[1]
                        divide(i + 1, a, L, n0 * 4 + (EX_BASE + a + 1), 1.0)
                    elif it == "PKV":
                        inverse_rms(g + (i + 2) // 8, i + 2, n0 * 5 + 15)
                    elif it == "QN" and i == 5 and not last:
                        hold(pool, t_full, at(g, 5, "PKV") + 1, p_passed)
                        w1_split(g + 1, 0)
                    elif it[0] == "EX" and i == 5 and not last and it[1] in (2, 3):
                        w1_split(g + 1, it[1] - 1)
                    elif it[0] == "EX" and i == 8 and it[1] == 1:
                        w1_split(g + 1, 6)
                    elif it == "WO" and i == 8:
                        hold(pool, w_full, at(g, 8, "WO") + 1, p_passed)
                        w1_split(g + 1, 4)

            slots(pool, [ch], slot)
            hold(pool, w_full, W_END, p_passed)
            for q, (_, hi, lo, n, np_) in enumerate(FF_CHUNKS):
                split_raw(QFF + q, hi, lo, n, np_)
            for u in range(2 * FT):
                hold(pool, in_fw[u % 2], 16 * (u // 2 + 1), p_passed)
                if u >= 3:
                    hold(pool, x2_ready, u - 2, p_passed)
                k = FW + u % 3 * 2048
                src = PBF[:, u % 2 * 1024:(u % 2 + 1) * 1024]
                ch.link(e.tensor_copy(r(k, 1024), src))
                e.tensor_tensor(r(k + 1024, 1024), src, rf(k, 1024), ALU.subtract).then_inc(fw_split, 1)

        @block.scalar
        def _(act):
            e = nc.scalar
            act.wait_ge(in_const, 16)

            def high_xt(k, t):
                act.wait_ge(t_full, k + 1)
                e.activation(XT[:, 0, :, t * P:(t + 1) * P], T[k % 2][:, :].rearrange("p (k n) -> p k n", k=KT),
                             ACT.Copy).then_inc(t_act, 1)

            for t in range(NT):
                high_xt(T_LN0 + t, t)
            for u in range(8):
                blk = u // 2
                k = T_QK + u
                act.wait_ge(t_full, k + 1)
                if u >= 2:
                    act.wait_ge(t_free, k - 1)
                e.activation(TMP[u % 2], T[k % 2][:, :], ACT.Identity, bias=C[:, C_BQK + blk:C_BQK + blk + 1])\
                    .then_inc(t_act, 1)
            for t in range(NT):
                k = T_VAR + t
                act.wait_ge(t_full, k + 1)
                e.activation(HN[:, t * P:(t + 1) * P], T[k % 2][:, 64:192], ACT.Copy).then_inc(t_act, 1)
            act.wait_ge(row_ready, 1)
            e.activation(RT[:, 2, :], RT[:, 1, :], ACT.Exp).then_inc(row_exp, 1)
            for t in range(NT):
                k = T_HW + t
                act.wait_ge(t_full, k + 1)
                if t >= 2:
                    act.wait_ge(s_full, t - 1)
                e.activation(r(OT + t % 2 * 256, P), T[k % 2][:, 0:P], ACT.Copy).then_inc(t_act, 1)
                if t >= 1:
                    act.wait_ge(y_ready, t)
                    if t >= 3:
                        act.wait_ge(gate_done, t - 2)
                    e.activation(TMP[2 + (t - 1) % 2], G[:, (t - 1) * D:t * D], ACT.Tanh, scale=0.5)\
                        .then_inc(y_tanh, 1)
            act.wait_ge(y_ready, NT)
            act.wait_ge(gate_done, NT - 2)
            e.activation(TMP[2 + (NT - 1) % 2], G[:, (NT - 1) * D:NT * D], ACT.Tanh, scale=0.5).then_inc(y_tanh, 1)

            def high_pt(k, c):
                act.wait_ge(t_full, k + 1)
                if isinstance(c, int) and c < 3:
                    pass
                else:
                    act.wait_ge(pv_done, c - 2)
                return T[k % 2]

            def exp0(n, a):
                u = n * 4 + a
                act.wait_ge(max_ready, u + 1)
                if n >= 2 and a == 0:
                    act.wait_ge(t_full, T_ATT + (n - 1) * NT)
                if u == 0:
                    act.wait_ge(gate_done, NT)
                k = n % 2 * 4 + a
                e.activation(PB[:, n % 2, a, :], S[u % 2][:, :], ACT.Exp, bias=NM[:, k:k + 1],
                             accum_out=SM[:, k:k + 1]).then_inc(exp_done, 1)

            for a in range(4):
                exp0(0, a)
            for n in range(2 * H0):
                for kb in range(NT):
                    c = n * NT + kb
                    k = T_ATT + c
                    act.wait_ge(t_full, k + 1)
                    if c >= 3:
                        act.wait_ge(pv_done, c - 2)
                    e.activation(r(PT + c % 3 * 1024, 512), T[k % 2][:, :], ACT.Copy).then_inc(t_act, 1)
                    if kb % 2 == 1 and n + 1 < 2 * H0:
                        exp0(n + 1, kb // 2)
                if n % H0 == H0 - 1:
                    qg = n // H0
                    act.wait_ge(pv_done, (n + 1) * NT)
                    e.activation(r(OT + qg * 1024, 512), VB[:, :], ACT.Copy).then_inc(ot_high, 1)
            for t in range(NT):
                high_xt(T_LN1 + t, t)

            def sum_squares(m, wcount, k):
                act.wait_ge(w_full, wcount)
                for a in range(4):
                    e.activation(JUNK[:, m % 2 * 5 + a, :], WB[:, a * HD:(a + 1) * HD], ACT.Square,
                                 accum_out=SQ[:, m % 2, a:a + 1]).then_inc(squares, 1)
                return k

            def squares_k(m, tcount, tk):
                act.wait_ge(t_full, tcount)
                e.activation(JUNK[:, m % 2 * 5 + 4, :], tk[:, 0:HD], ACT.Square, accum_out=SQ[:, m % 2, 4:5]).then_inc(squares, 1)
                e.activation(VS[:, m % 4, :], tk[:, HD:2 * HD], ACT.Copy).then_inc(t_act, 1)

            def high_qk(m, tq, tk, bq, bk):
                act.wait_ge(t_full, tq)
                e.activation(r(QT + m % 2 * 1024, 512), bq[:, :], ACT.Copy, scale=QKW[:, 0:1]).then_inc(t_act, 1)
                act.wait_ge(t_full, tk)
                e.activation(r(KTR + m % NT * P, P), bk[:, 0:P], ACT.Copy, scale=QKW[:, 1:2]).then_inc(t_act, 1)

            def exp1(m, a, L, count):
                act.wait_ge(neg_ready, count)
                k = m % 2 * 4 + a
                e.activation(PB[:, m % 2, a, 0:L], PB[:, m % 2, a, 0:L], ACT.Exp, bias=NM[:, k:k + 1],
                             accum_out=SM[:, k:k + 1]).then_inc(exp_done, 1)

            for m in range(2):
                sum_squares(m, W_PRO + m + 1, None)
                k = T_PRO + 3 * m
                squares_k(m, k + 1, T[k % 2])
                high_qk(m, k + 2, k + 3, T[(k + 1) % 2], T[k % 2])
            for a in range(4):
                exp1(0, a, P, a + 1)

            def lines(g, i, part):
                jj = i % 4
                todo = {(1, 0): (0, 1), (1, 1): (2,), (2, 0): (3, 4), (2, 1): (5,), (3, 0): (6,), (3, 1): (7,)}
                for ln in todo.get((jj, part), ()):
                    chunk = g * 2 + i // 4
                    to = {0: 1, 4: 2}.get(ln, 3)
                    if ln == 0:
                        act.wait_ge(in_codes, (chunk + 1) * 16)
                        act.wait_ge(out_dq, chunk * 16 + 16)
                    if ln > 1 and to == 3:
                        act.wait_ge(line_used, chunk * 6 + {2: 1, 3: 2, 5: 3, 6: 4, 7: 5}[ln])
                    if ln == 1:
                        act.wait_ge(dq_scaled, chunk + 1)
                    sc, bi = LINES[ln]
                    e.activation(DQ[:, to, :], CODES, ACT.Copy, scale=sc, bias=bi).then_inc(line, 1)

            def slot(g, i):
                known = 8 * g + i if isinstance(g, int) else i
                n0 = g * 8 + i
                L = (i + 1) % NT * P + P
                for it in slot_items(known):
                    if it[0] == "T":
                        kb = it[1]
                        c = at(g, i, ("PV", kb))
                        act.wait_ge(t_full, at(g, i, it) + 1)
                        act.wait_ge(pv_done, c - 2)
                        e.activation(r(PT + AT[i, ("PV", kb)] % 3 * 1024, 512), T[AT[known, it] % 2][:, :],
                                     ACT.Copy).then_inc(t_act, 1)
                    elif it[0] == "EX":
                        exp1(i + 1, it[1], L, n0 * 4 + it[1] + 5)
                    elif it == "PQ":
                        sum_squares(i + 2, at(g, i, "PQ") + 1, None)
                    elif it == "PKV":
                        squares_k(i + 2, at(g, i, "PKV") + 1, T[AT[known, "PKV"] % 2])
                    elif it == "QK":
                        high_qk(i + 2, at(g, i, "QT") + 1, at(g, i, "KT") + 1,
                                T[AT[known, "QT"] % 2], T[AT[known, "KT"] % 2])
                    elif it == "E":
                        act.wait_ge(pv_done, at(g, i, ("PV", i % NT)) + 1)
                        e.activation(r(OT + i % 2 * 1024, 512), VB[:, :], ACT.Copy).then_inc(ot_high, 1)
                    elif it == "DA":
                        lines(g, i, 0)
                    elif it == "DB":
                        lines(g, i, 1)

            slots(act, [], slot)
            for tg in range(2):
                k = T_END + tg * (FT + 1)
                act.wait_ge(t_full, k + 1)
                e.activation(r(XLA, 512, RANK1), T[k % 2][0:RANK1, :], ACT.Copy).then_inc(t_act, 1)
                for j in range(FT):
                    u = tg * FT + j
                    kk = k + 1 + j
                    act.wait_ge(t_full, kk + 1)
                    if u >= 2:
                        act.wait_ge(t_free, T_END + (u - 2) // FT * (FT + 1) + (u - 2) % FT + 2)
                    e.activation(PBF[:, 2048 + u % 2 * 512:2560 + u % 2 * 512], T[kk % 2][:, :], ACT.Relu,
                                 bias=C[:, C_BUP + j:C_BUP + j + 1]).then_inc(t_act, 1)
                act.wait_ge(x2_ready, (tg + 1) * FT)
                e.activation(r(ZT, 512, RANK1), VB[0:RANK1, :], ACT.Copy).then_inc(z_high, 1)
                for tt in range(4):
                    act.wait_ge(y_ready, NT + tg * 4 + tt + 1)
                    e.activation(PBF[:, (12 + tt % 2) * D:(13 + tt % 2) * D], PBF[:, (14 + tt % 2) * D:(15 + tt % 2) * D],
                                 ACT.Tanh, scale=0.5).then_inc(y_tanh, 1)

        @block.vector
        def _(dve):
            e = nc.vector
            ch = Tally(dve, v_chain, v_passed)
            ch.per = V_PER

            def normalise(t, src, slot_):
                k = t % 2
                ch.link(e.bn_stats(ST[:, k, :], src))
                e.bn_aggr(MV[:, k, :], ST[:, k, :]).then_inc(var_ready, 1)
                dve.wait_ge(var_ready, t + 1)
                dve.wait_ge(rstd_ready, t + 1)
                e.tensor_scalar(XN[slot_], src, MV[:, k, 0:1], RSTD[:, k:k + 1], ALU.subtract, ALU.mult)\
                    .then_inc(xn_ready, 1)

            def low_xt(k, t):
                dve.wait_ge(t_act, k + 1)
                e.tensor_tensor(XT[:, 1, :, t * P:(t + 1) * P], T[k % 2][:, :].rearrange("p (k n) -> p k n", k=KT),
                                XT[:, 0, :, t * P:(t + 1) * P].bitcast(F32), ALU.subtract).then_inc(t_free, 1)

            dve.wait_ge(in_const, 16)
            ch.done(e.tensor_scalar(QKW[:, 0:1], C[:, C_QKW:C_QKW + 1], 1.0 / math.sqrt(HD), None, ALU.mult))
            e.memset(CMP[:, 0, 0:8], 0.0).then_inc(dq_scaled, 1)
            ch.done(e.tensor_copy(QKW[:, 1:2], C[:, C_QKW + 1:C_QKW + 2]))
            ch.done(e.tensor_copy(SLC[:, :], C[:, C_SLOPE:C_SLOPE + 4]))
            for t in range(NT):
                dve.wait_ge(in_x[t % 4], 16 * (t // 4 + 1))
                if t >= 4:
                    dve.wait_ge(t_full, t - 3)
                normalise(t, XS[t % 4], t % 4)
                if t:
                    low_xt(t - 1, t - 1)
            low_xt(NT - 1, NT - 1)
            for u in range(8):
                blk, nt = u // 2, u % 2
                k = T_QK + u
                dve.wait_ge(t_act, k + 1)
                dve.wait_ge(t_free, k)
                m = C_MASK + 2 * (blk // 2)
                hi = r(PT + u % 2 * 512, 512)
                ch.done(e.tensor_copy(hi, TMP[u % 2]))
                ch.link(e.tensor_scalar(TMP[4], TMP[u % 2], C[:, m + 1:m + 2], None, ALU.mult))
                dst = (QS if blk < 2 else KS) + blk % 2 * 1024 + nt * 512
                e.scalar_tensor_tensor(r(dst, 512), hi.bitcast(F32), C[:, m:m + 1], TMP[4],
                                       ALU.mult, ALU.add).then_inc(t_free, 1)
            dve.wait_ge(in_rows, 16)
            for t in range(NT):
                k = T_VAR + t
                dve.wait_ge(t_act, k + 1)
                ch.done(e.tensor_copy(RT[:, 0, t * 8:t * 8 + 8], T[k % 2][:, 192:200]))
                e.tensor_tensor(VN0[:, t * 64:t * 64 + 64], T[k % 2][:, 0:64], ROWS[:, R_BV:R_BV + 64], ALU.add)\
                    .then_inc(t_free, 1)
            ch.settle()

            def by_e(k):
                return RT[:, k, :].rearrange("p (t e) -> p t e", e=NEXP)

            def over_e(a):
                return a.unsqueeze(2).to_broadcast([P, NT, NEXP])

            ch.link(e.tensor_reduce(RT[:, 3, 0:NT], by_e(0), AX.X, ALU.max))
            e.tensor_tensor(by_e(1), by_e(0), over_e(RT[:, 3, 0:NT]), ALU.subtract).then_inc(row_ready, 1)
            dve.wait_ge(row_exp, 1)
            ch.link(e.tensor_reduce(RT[:, 3, 8:16], by_e(2), AX.X, ALU.add))
            ch.link(e.reciprocal(RT[:, 3, 16:24], RT[:, 3, 8:16]))
            ch.link(e.tensor_tensor(by_e(4), by_e(2), over_e(RT[:, 3, 16:24]), ALU.mult))
            pj = by_e(4).unsqueeze(2).to_broadcast([P, NT, NEXP, NEXP])
            pe_ = by_e(4).unsqueeze(3).to_broadcast([P, NT, NEXP, NEXP])

            def cmp4(k):
                return CMP[:, k, :].rearrange("p (t e j) -> p t e j", e=NEXP, j=NEXP)

            ch.done(e.tensor_tensor(cmp4(0), pj, pe_, ALU.is_gt))
            ch.link(e.tensor_tensor(cmp4(1), pj, pe_, ALU.is_equal))
            tri = C[:, C_TRI:C_TRI + 64].unsqueeze(1).to_broadcast([P, NT, 64])
            c1 = CMP[:, 1, :].rearrange("p (t n) -> p t n", t=NT)
            ch.link(e.tensor_tensor(c1, c1, tri, ALU.mult))
            ch.link(e.tensor_tensor(CMP[:, 0, :], CMP[:, 0, :], CMP[:, 1, :], ALU.add))
            ch.link(e.tensor_reduce(RT[:, 5, :], CMP[:, 0, :].rearrange("p (n j) -> p n j", j=NEXP), AX.X, ALU.add))
            ch.link(e.scalar_tensor_tensor(RT[:, 6, :], RT[:, 5, :], 1.5, RT[:, 4, :], ALU.is_lt, ALU.mult))
            ch.link(e.tensor_reduce(RT[:, 3, 24:32], by_e(6), AX.X, ALU.add))
            ch.link(e.reciprocal(RT[:, 3, 32:40], RT[:, 3, 24:32]))
            ch.link(e.tensor_tensor(by_e(7), by_e(6), over_e(RT[:, 3, 32:40]), ALU.mult))
            ch.link(e.tensor_scalar(RT[:, 7, :], RT[:, 7, :], 2.0, None, ALU.mult))
            hn = HN.rearrange("p (n r) -> p n r", r=RANK0)
            e.tensor_tensor(hn, hn, RT[:, 7, :].unsqueeze(2).to_broadcast([P, 64, RANK0]), ALU.mult)\
                .then_inc(hw_ready, 1)

            def ffn0_out(t):
                dve.wait_ge(s_full, t + 1)
                e.tensor_tensor(G[:, t * D:(t + 1) * D], S[t % 2][:, 0:D], ROWS[:, R_BB:R_BB + D], ALU.add)\
                    .then_inc(y_ready, 1)

            def gate(t):
                dve.wait_ge(y_tanh, t + 1)
                e.scalar_tensor_tensor(G[:, t * D:(t + 1) * D], TMP[2 + t % 2], 1.0, G[:, t * D:(t + 1) * D],
                                       ALU.add, ALU.mult).then_inc(gate_done, 1)

            for t in range(NT):
                k = T_HW + t
                dve.wait_ge(t_act, k + 1)
                o = OT + t % 2 * 256
                e.tensor_tensor(r(o + P, P), T[k % 2][:, 0:P], rf(o, P), ALU.subtract).then_inc(t_free, 1)
                if t:
                    ffn0_out(t - 1)
                if t >= 2:
                    gate(t - 2)
            ffn0_out(NT - 1)
            gate(NT - 2)
            gate(NT - 1)

            def max0(n, a):
                u = n * 4 + a
                dve.wait_ge(s_full, S_ATT + u + 1)
                k = n % 2 * 4 + a
                if n >= 2:
                    dve.wait_ge(exp_done, u - 7)
                e.tensor_reduce(NM[:, k:k + 1], S[u % 2][:, :], AX.X, ALU.max, negate=True).then_inc(max_ready, 1)

            def low_pt(k, c, bank, kc):
                dve.wait_ge(t_act, k)
                o = PT + kc % 3 * 1024
                e.tensor_tensor(r(o + 512, 512), bank[:, :], rf(o, 512), ALU.subtract).then_inc(t_free, 1)

            for a in range(4):
                max0(0, a)
            for n in range(2 * H0):
                for kb in range(NT):
                    c = n * NT + kb
                    if kb % 2 == 0 and n + 1 < 2 * H0:
                        max0(n + 1, kb // 2)
                    low_pt(T_ATT + c + 1, c, T[(T_ATT + c) % 2], c)
                if n % H0 == H0 - 1:
                    o = OT + n // H0 * 1024
                    dve.wait_ge(ot_high, n // H0 + 1)
                    e.tensor_tensor(r(o + 512, 512), VB[:, :], rf(o, 512), ALU.subtract).then_inc(ot_low, 1)
            for t in range(NT):
                dve.wait_ge(w_full, t + 1)
                dve.wait_ge(in_x[t % 4], 16 * (t // 4 + 3))
                if t == 0:
                    dve.wait_ge(t_full, T_LN1)
                tmp = TMP[t % 2]
                e.tensor_tensor(tmp, WB[:, :], ROWS[:, R_BO:R_BO + D], ALU.add).then_inc(w_free, 1)
                dve.wait_ge(w_free, t + 1)
                ch.link(e.scalar_tensor_tensor(tmp, tmp, 0.5, G[:, t * D:(t + 1) * D], ALU.mult, ALU.mult))
                e.tensor_tensor(XS[t % 4], XS[t % 4], tmp, ALU.add).then_inc(x1_ready, 1)
                dve.wait_ge(x1_ready, t + 1)
                if t >= 4:
                    dve.wait_ge(t_full, T_LN1 + t - 3)
                normalise(NT + t, XS[t % 4], t % 4)
                if t:
                    low_xt(T_LN1 + t - 1, t - 1)
            low_xt(T_LN1 + NT - 1, NT - 1)
            ch.link(e.memset(G[:, :], 0.0))
            for k in range(4):
                dve.wait_ge(out_x1[k], 32)

            def copy_k(tcount, tk, tprev):
                dve.wait_ge(t_act, tcount)
                dve.wait_ge(t_full, tprev)
                e.tensor_copy(QN[:, 4 * HD:5 * HD], tk[:, 0:HD]).then_inc(t_free, 1)

            def scale_qk(m, icount, tcopy):
                dve.wait_ge(inv_ready, icount)
                dve.wait_ge(t_free, tcopy)
                k = m % 2
                e.tensor_tensor(QN[:, 0:4 * HD].rearrange("p (a n) -> p a n", a=4),
                                WB[:, :].rearrange("p (a n) -> p a n", a=4),
                                INV[:, k, 0:4].unsqueeze(2).to_broadcast([P, 4, HD]), ALU.mult).then_inc(w_free, 1)
                e.tensor_scalar(QN[:, 4 * HD:5 * HD], QN[:, 4 * HD:5 * HD], INV[:, k, 4:5], None, ALU.mult)\
                    .then_inc(qk_ready, 1)

            def low_qk(m, tq, tk, bq, bk):
                o = QT + m % 2 * 1024
                dve.wait_ge(t_act, tq)
                e.scalar_tensor_tensor(r(o + 512, 512), bq[:, :], QKW[:, 0:1], rf(o, 512), ALU.mult, ALU.subtract)\
                    .then_inc(t_free, 1)
                o = KTR + m % NT * P
                dve.wait_ge(t_act, tk)
                e.scalar_tensor_tensor(r(o + TOK, P), bk[:, 0:P], QKW[:, 1:2], rf(o, P), ALU.mult, ALU.subtract)\
                    .then_inc(t_free, 1)

            def bias_max(m, a, L, scount, bank):
                hold(dve, s_full, scount, v_passed)
                k = m % 2 * 4 + a
                e.tensor_tensor_reduce(out=PB[:, m % 2, a, 0:L], in0=bank[:, 0:L], in1=REL[:, TOK - L:TOK],
                                       scale=SLC[:, a:a + 1], scalar=-3.0e38, op0=ALU.add, op1=ALU.max,
                                       accum_out=MX[:, k:k + 1]).then_inc(s_free, 1)

            for m in range(2):
                k = T_PRO + 3 * m
                copy_k(k + 1, T[k % 2], k)
                scale_qk(m, m + 1, k + 1)
                low_qk(m, k + 2, k + 3, T[(k + 1) % 2], T[k % 2])
            for a in range(4):
                bias_max(0, a, P, S_PRO + a + 1, S[a % 2])

            def combine(g, i, part):
                jj = i % 4
                chunk = g * 2 + i // 4
                if jj == 0 and part == 0 and not (isinstance(g, int) and 8 * g + i == 0):
                    dve.wait_ge(in_absmax, chunk * 16)
                    e.tensor_tensor(DQ[:, 1, :], DQ[:, 1, :], DQ[:, 3, :], ALU.mult).then_inc(dq_scaled, 1)
                todo = {(1, 0): (1,), (1, 1): (2,), (2, 0): (3,), (2, 1): (5,), (3, 0): (6,), (3, 1): (7,)}
                for ln in todo.get((jj, part), ()):
                    dve.wait_ge(line, chunk * 8 + ln + 1)
                    b, op = (1, ALU.min) if ln < 4 else (2, ALU.max)
                    if ln not in (1, 5):
                        dve.wait_ge(line_used, chunk * 6 + {2: 1, 3: 2, 6: 4, 7: 5}[ln])
                    e.tensor_tensor(DQ[:, b, :], DQ[:, b, :], DQ[:, 3, :], op).then_inc(line_used, 1)
                if (jj, part) == (3, 1):
                    ch.link(e.tensor_scalar(CODES, CODES, 8, None, ALU.bitwise_and))
                    hold(dve, line_used, chunk * 6 + 6, v_passed)
                    e.copy_predicated(DQ[:, 1, :], CODES, DQ[:, 2, :]).then_inc(dq_selected, 1)
                    dve.wait_ge(dq_selected, chunk + 1)

            def slot(g, i):
                known = 8 * g + i if isinstance(g, int) else i
                n0 = g * 8 + i
                L = (i + 1) % NT * P + P
                for it in slot_items(known):
                    if it[0] == "S":
                        a = it[1]
                        if i == 7 and a == 0:
                            ch.link(e.tensor_copy(SLC[:, :], C[:, bass.ds(g * 4 + (C_SLOPE + 4), 4)]))
                        if a == 0 and i > 0:
                            prev = (at(g, i - 1, "last") + 1) if i >= 1 else None
                            dve.wait_ge(t_full, prev)
                        bias_max(i + 1, a, L, at(g, i, it) + 1, S[AT[known, it] % 2])
                    elif it[0] == "T":
                        low_pt(at(g, i, it) + 1, None, T[AT[known, it] % 2], AT[i, ("PV", it[1])])
                    elif it == "WO":
                        dve.wait_ge(w_full, at(g, i, "WO") + 1)
                        t = (i - 1) % NT
                        dve.wait_ge(w_free, at(g, i, "WO"))
                        e.tensor_tensor(G[:, t * D:(t + 1) * D], G[:, t * D:(t + 1) * D], WB[:, :], ALU.add)\
                            .then_inc(w_free, 1)
                    elif it == "PKV":
                        prev = T_BASE if known == 0 and isinstance(g, int) else at(g, i - 1, "KT") + 1
                        copy_k(at(g, i, "PKV") + 1, T[AT[known, "PKV"] % 2], prev)
                    elif it == "QN":
                        scale_qk(i + 2, n0 + 3, at(g, i, "PKV") + 1)
                    elif it == "QK":
                        low_qk(i + 2, at(g, i, "QT") + 1, at(g, i, "KT") + 1,
                               T[AT[known, "QT"] % 2], T[AT[known, "KT"] % 2])
                    elif it == "E":
                        o = OT + i % 2 * 1024
                        dve.wait_ge(ot_high, n0 + 3)
                        e.tensor_tensor(r(o + 512, 512), VB[:, :], rf(o, 512), ALU.subtract).then_inc(ot_low, 1)
                    elif it == "DA":
                        combine(g, i, 0)
                    elif it == "DB":
                        combine(g, i, 1)

            slots(dve, [ch], slot)
            dve.wait_ge(in_absmax, NDQ * 16)
            e.tensor_tensor(DQ[:, 1, :], DQ[:, 1, :], DQ[:, 3, :], ALU.mult).then_inc(dq_scaled, 1)
            dve.wait_ge(w_full, W_END)
            dve.wait_ge(w_free, W_END - 1)
            e.tensor_tensor(G[:, 7 * D:8 * D], G[:, 7 * D:8 * D], WB[:, :], ALU.add).then_inc(w_free, 1)
            for tg in range(2):
                k = T_END + tg * (FT + 1)
                dve.wait_ge(t_act, k + 1)
                e.tensor_tensor(r(XLA + 512, 512, RANK1), T[k % 2][0:RANK1, :], rf(XLA, 512, RANK1), ALU.subtract)\
                    .then_inc(t_free, 1)
                for j in range(FT):
                    u = tg * FT + j
                    kk = k + 1 + j
                    o = X2 + u % 2 * 1024
                    src = PBF[:, 2048 + u % 2 * 512:2560 + u % 2 * 512]
                    dve.wait_ge(t_act, kk + 1)
                    if u >= 2:
                        dve.wait_ge(x2_ready, u - 1)
                    ch.link(e.tensor_copy(r(o, 512), src))
                    e.tensor_tensor(r(o + 512, 512), src, rf(o, 512), ALU.subtract).then_inc(t_free, 1)
                dve.wait_ge(z_high, tg + 1)
                e.tensor_tensor(r(ZT + 512, 512, RANK1), VB[0:RANK1, :], rf(ZT, 512, RANK1), ALU.subtract)\
                    .then_inc(z_low, 1)

                def y_of(tt):
                    u = tg * 4 + tt
                    dve.wait_ge(d_full, u + 1)
                    y = PBF[:, (14 + tt % 2) * D:(15 + tt % 2) * D]
                    e.tensor_tensor(y, S[tt // 2][:, tt % 2 * D:(tt % 2 + 1) * D], C[:, C_BD:C_BD + D], ALU.add)\
                        .then_inc(y_ready, 1)
                    dve.wait_ge(y_ready, NT + u + 1)

                def result(tt):
                    u = tg * 4 + tt
                    dve.wait_ge(y_tanh, NT + u + 1)
                    y = PBF[:, (14 + tt % 2) * D:(15 + tt % 2) * D]
                    th = PBF[:, (12 + tt % 2) * D:(13 + tt % 2) * D]
                    ch.link(e.scalar_tensor_tensor(y, th, 1.0, y, ALU.add, ALU.mult))
                    ch.link(e.scalar_tensor_tensor(y, y, 0.5, G[:, u * D:(u + 1) * D], ALU.mult, ALU.mult))
                    dve.wait_ge(in_x1[tt], 16 * (tg + 1))
                    xx = PBF[:, (8 + tt) * D:(9 + tt) * D]
                    e.tensor_tensor(xx, xx, y, ALU.add).then_inc(out_done, 1)
                    dve.wait_ge(out_done, u + 1)

                y_of(0)
                for tt in range(4):
                    if tt < 3:
                        y_of(tt + 1)
                    result(tt)

        @block.tensor
        def _(pe):
            e = nc.tensor

            def mm3(dst, lh, ll, rh, rl, start, stop):
                e.matmul(dst, lh, rh, start=start, stop=False)
                e.matmul(dst, lh, rl, start=False, stop=False)
                return e.matmul(dst, ll, rh, start=False, stop=stop)

            def xt(half, kt, a, n):
                return XT[:, half, kt, a:a + n]

            def ring(k):
                if isinstance(k, int) and k < 2:
                    return
                pe.wait_ge(t_free, k - 1)

            def transpose_x(k, t, count):
                ring(k)
                pe.wait_ge(xn_ready, count)
                for kt in range(KT):
                    last = e.transpose(T[k % 2][:, kt * P:(kt + 1) * P], XN[t % 4][:, kt * P:(kt + 1) * P], IDENT)
                last.then_inc(t_full, 1)

            pe.wait_ge(in_const, 16)
            for t in range(NT):
                transpose_x(T_LN0 + t, t, t + 1)
            pe.wait_ge(split, W0_QK)
            pe.wait_ge(t_free, NT)
            for u in range(8):
                blk, nt = u // 2, u % 2
                k = T_QK + u
                ring(k)
                for kt in range(KT):
                    c = kt * 512 + blk * P
                    last = mm3(T[k % 2][:, :], r(WQK_H + c, P), r(WQK_L + c, P), xt(0, kt, nt * 512, 512),
                               xt(1, kt, nt * 512, 512), kt == 0, kt == KT - 1)
                last.then_inc(t_full, 1)
            pe.wait_ge(split, W0_VAR)
            for t in range(NT):
                k = T_VAR + t
                ring(k)
                for kt in range(KT):
                    c = kt * 200
                    last = mm3(T[k % 2][:, 0:200], xt(0, kt, t * P, P), xt(1, kt, t * P, P), r(WVAR_H + c, 200),
                               r(WVAR_L + c, 200), kt == 0, kt == KT - 1)
                last.then_inc(t_full, 1)
            pe.wait_ge(split, W0_BASE)

            def base(t):
                if t >= 2:
                    pe.wait_ge(y_ready, t - 1)
                for kt in range(KT):
                    c = kt * 512
                    mm3(S[t % 2][:, 0:D], xt(0, kt, t * P, P), xt(1, kt, t * P, P), r(WBASE_H + c, D),
                        r(WBASE_L + c, D), kt == 0, False)

            base(0)
            base(1)
            pe.wait_ge(hw_ready, 1)
            pe.wait_ge(split, W0_EXP)
            for t in range(NT):
                k = T_HW + t
                ring(k)
                e.transpose(T[k % 2][:, 0:P], HN[:, t * P:(t + 1) * P], IDENT).then_inc(t_full, 1)
                if t >= 2:
                    base(t)
                pe.wait_ge(t_free, k + 1)
                o = OT + t % 2 * 256
                mm3(S[t % 2][:, 0:D], r(o, P), r(o + P, P), r(WEXP_H, D), r(WEXP_L, D), False, True)\
                    .then_inc(s_full, 1)

            def scores0(n, a):
                qg, h = n // H0, n % H0
                u = n * 4 + a
                if u >= 2:
                    pe.wait_ge(exp_done, u - 1)
                else:
                    pe.wait_ge(y_ready, NT - 1 + u)
                b = h % 4 * 32
                qc = QS + h // 4 * 1024 + (qg * 4 + a) * P
                for c in range(2):
                    kc = KS + h // 4 * 1024 + c * 512
                    last = e.matmul(S[u % 2][:, c * 512:(c + 1) * 512], R[b:b + 32, qc:qc + P],
                                    R[b:b + 32, kc:kc + 512], start=True, stop=True)
                last.then_inc(s_full, 1)

            for a in range(4):
                scores0(0, a)
            pe.wait_ge(vpad_ready, H0)

            def values0(c):
                n, kb = c // NT, c % NT
                h = n % H0
                pe.wait_ge(t_free, T_ATT + c + 1)
                if n == H0 and kb == 0:
                    pe.wait_ge(ot_low, 1)
                v = r(VPAD + kb * 1024 + h * P, P)
                o = PT + c % 3 * 1024
                first, end = h == 0 and kb == 0, h == H0 - 1 and kb == NT - 1
                e.matmul(VB[:, :], v, r(o, 512), start=first, stop=False)
                e.matmul(VB[:, :], v, r(o + 512, 512), start=False, stop=end).then_inc(pv_done, 1)

            for n in range(2 * H0):
                for kb in range(NT):
                    c = n * NT + kb
                    k = T_ATT + c
                    if kb % 2 == 0 and n + 1 < 2 * H0:
                        scores0(n + 1, kb // 2)
                    if kb == 0:
                        pe.wait_ge(probs_ready, 4 * (n + 1))
                    ring(k)
                    for a in range(4):
                        last = e.transpose(T[k % 2][:, a * P:(a + 1) * P], PB[:, n % 2, a, kb * P:(kb + 1) * P], IDENT)
                    last.then_inc(t_full, 1)
                    if c >= 2:
                        values0(c - 2)
            values0(2 * H0 * NT - 2)
            values0(2 * H0 * NT - 1)
            for t in range(NT):
                qg = t // 4
                pe.wait_ge(ot_low, qg + 1)
                pe.wait_ge(split, W0_O)
                if t:
                    pe.wait_ge(w_free, t)
                o = OT + qg * 1024 + t % 4 * P
                mm3(WB[:, :], r(o, P), r(o + 512, P), r(WO0_H, D), r(WO0_L, D), True, True).then_inc(w_full, 1)
                if t:
                    transpose_x(T_LN1 + t - 1, t - 1, NT + t)
            transpose_x(T_LN1 + NT - 1, NT - 1, 2 * NT)

            def project_q(m, wait_w, chunks):
                pe.wait_ge(w_free, wait_w)
                for kt in range(KT):
                    pe.wait_ge(split, chunks + kt + 1)
                    c = kt * 768
                    last = mm3(WB[:, :], xt(0, kt, m % NT * P, P), xt(1, kt, m % NT * P, P), r(W_H + c, 512),
                               r(W_L + c, 512), kt == 0, kt == KT - 1)
                last.then_inc(w_full, 1)

            def project_kv(m, k, bank):
                ring(k)
                for kt in range(KT):
                    c = kt * 768 + 512
                    last = mm3(bank[:, 0:256], xt(0, kt, m % NT * P, P), xt(1, kt, m % NT * P, P), r(W_H + c, 256),
                               r(W_L + c, 256), kt == 0, kt == KT - 1)
                last.then_inc(t_full, 1)

            def transpose_qk(count, kq, kk, bq, bk):
                pe.wait_ge(qk_ready, count)
                ring(kq)
                for a in range(4):
                    last = e.transpose(bq[:, a * P:(a + 1) * P], QN[:, a * HD:(a + 1) * HD], IDENT)
                last.then_inc(t_full, 1)
                ring(kk)
                e.transpose(bk[:, 0:P], QN[:, 4 * HD:5 * HD], IDENT).then_inc(t_full, 1)

            def scores1(m, a, L, wait_s, wait_t, bank):
                if a == 0:
                    pe.wait_ge(t_free, wait_t)
                if wait_s is not None:
                    pe.wait_ge(s_free, wait_s)
                q = QT + m % 2 * 1024 + a * P
                for c in range(0, L, 512):
                    w = min(512, L - c)
                    last = mm3(bank[:, c:c + w], r(q, P), r(q + 512, P), r(KTR + c, w), r(KTR + TOK + c, w), True, True)
                last.then_inc(s_full, 1)

            pe.wait_ge(t_free, T_LN1 + NT)
            for m in range(2):
                project_q(m, NT + m, QL1)
                k = T_PRO + 3 * m
                project_kv(m, k, T[k % 2])
                transpose_qk(m + 1, k + 1, k + 2, T[(k + 1) % 2], T[k % 2])
            for a in range(4):
                if a < 2:
                    pe.wait_ge(exp_done, EX_PRO)
                scores1(0, a, P, a - 1 if a >= 2 else None, T_BASE - 3, S[a % 2])

            def values1(g, i, kb):
                known = 8 * g + i if isinstance(g, int) else i
                pe.wait_ge(t_free, at(g, i, ("T", kb)) + 1)
                if kb == 0:
                    pe.wait_ge(ot_low, g * 8 + i + 2)
                if kb == i % NT:
                    pe.wait_ge(v_split, g * 8 + i + 1)
                o = PT + AT[i, ("PV", kb)] % 3 * 1024
                mm3(VB[:, :], r(VN + kb * P, P), r(VN + TOK + kb * P, P), r(o, 512), r(o + 512, 512),
                    kb == 0, kb == i % NT).then_inc(pv_done, 1)

            def output1(g, count_ot, wait_w, m, first):
                pe.wait_ge(ot_low, count_ot)
                pe.wait_ge(w_free, wait_w)
                for a in range(GRP):
                    if first:
                        pe.wait_ge(split, g * 8 + (QL1 + 5 + a))
                    o = OT + m % 2 * 1024 + a * P
                    w = WOUT + a * 512
                    last = mm3(WB[:, :], r(o, P), r(o + 512, P), r(W_H + w, 512), r(W_L + w, 512), a == 0, a == 3)
                last.then_inc(w_full, 1)

            def slot(g, i):
                known = 8 * g + i if isinstance(g, int) else i
                L = (i + 1) % NT * P + P
                started = False
                for it in slot_items(known):
                    if it[0] == "S":
                        prev = T_BASE if known == 0 and isinstance(g, int) else at(g, i - 1, "KT") + 1
                        u = at(g, i, it)
                        scores1(i + 1, it[1], L, u - (1 + S_PRO), prev, S[AT[known, it] % 2])
                    elif it[0] == "T":
                        kb = it[1]
                        k = at(g, i, it)
                        if not started:
                            pe.wait_ge(probs_ready, (g * 8 + i) * 4 + EX_BASE)
                            started = True
                        ring(k)
                        bank = T[AT[known, it] % 2]
                        for a in range(4):
                            last = e.transpose(bank[:, a * P:(a + 1) * P], PB[:, i % 2, a, kb * P:(kb + 1) * P], IDENT)
                        last.then_inc(t_full, 1)
                        if kb >= 2:
                            values1(g, i, kb - 2)
                    elif it == "WO":
                        output1(g if i <= NT else g, g * 8 + i + 2, at(g, i, "WO"), i - 1, i == 1)
                    elif it == "PQ":
                        project_q(i + 2, at(g, i, "PQ"), (g + (i + 2) // 8) * 8 + QL1)
                    elif it == "PKV":
                        project_kv(i + 2, at(g, i, "PKV"), T[AT[known, "PKV"] % 2])
                    elif it == "QK":
                        transpose_qk(g * 8 + i + 3, at(g, i, "QT"), at(g, i, "KT"),
                                     T[AT[known, "QT"] % 2], T[AT[known, "KT"] % 2])
                    elif it == "E":
                        for kb in range(max(0, i % NT - 1), i % NT + 1):
                            values1(g, i, kb)

            slots(pe, [], slot)
            output1(HKV - 1, STEPS + 2, W_END - 1, STEPS - 1, False)

            pe.wait_ge(split, QFF + NFFC)
            for tg in range(2):
                k = T_END + tg * (FT + 1)
                ring(k)
                for kt in range(KT):
                    last = mm3(T[k % 2][:, :], r(LA_H + kt * P, P), r(LA_L + kt * P, P), xt(0, kt, tg * 512, 512),
                               xt(1, kt, tg * 512, 512), kt == 0, kt == KT - 1)
                last.then_inc(t_full, 1)

                def up(j):
                    u, kk = tg * FT + j, k + 1 + j
                    pe.wait_ge(fw_split, u + 1)
                    ring(kk)
                    w = FW + u % 3 * 2048
                    for kt in range(KT):
                        mm3(T[kk % 2][:, :], r(w + kt * P, P), r(w + 1024 + kt * P, P), xt(0, kt, tg * 512, 512),
                            xt(1, kt, tg * 512, 512), kt == 0, False)
                    if j == 0:
                        pe.wait_ge(t_free, k + 1)
                    mm3(T[kk % 2][:, :], r(LB_H + j * P, P, RANK1), r(LB_L + j * P, P, RANK1), r(XLA, 512, RANK1),
                        r(XLA + 512, 512, RANK1), False, True).then_inc(t_full, 1)

                def down(j):
                    u, kk = tg * FT + j, k + 1 + j
                    pe.wait_ge(t_free, kk + 1)
                    if tg and j == 0:
                        pe.wait_ge(y_ready, NT + 4)
                        pe.wait_ge(z_low, 1)
                    if not tg and j == 0:
                        pe.wait_ge(ot_low, STEPS + 2)
                        pe.wait_ge(s_free, S_END - S_PRO)
                    o, w = X2 + u % 2 * 1024, FW + u % 3 * 2048
                    for tt in range(4):
                        mm3(S[tt // 2][:, tt % 2 * D:(tt % 2 + 1) * D], r(o + tt * P, P), r(o + 512 + tt * P, P),
                            r(w + 512, D), r(w + 1536, D), j == 0, False)
                    mm3(VB[:, :], r(DLA_H + j * P, P), r(DLA_L + j * P, P), r(o, 512), r(o + 512, 512),
                        j == 0, j == FT - 1).then_inc(x2_ready, 1)

                up(0)
                for j in range(FT):
                    if j + 1 < FT:
                        up(j + 1)
                    down(j)
                pe.wait_ge(z_low, tg + 1)
                for tt in range(4):
                    mm3(S[tt // 2][:, tt % 2 * D:(tt % 2 + 1) * D], r(ZT + tt * P, P, RANK1),
                        r(ZT + 512 + tt * P, P, RANK1), r(DLB_H, D, RANK1), r(DLB_L, D, RANK1), False, True)\
                        .then_inc(d_full, 1)


def kernel(**inputs):
    import concourse.bacc as bacc
    from concourse.bass_utils import run_bass_kernel_spmd

    a = {k: np.asarray(v) for k, v in inputs.items()}

    def tiles(w):
        k = w.shape[0] // P
        return w.reshape(k, P, -1).transpose(1, 0, 2).reshape(P, -1)

    qk = a["L0_attn_Wqk_w"].reshape(H0, E0, 2, D)
    bqk = a["L0_attn_Wqk_b"].reshape(H0, E0, 2)
    stacked, bias = [], []
    for w in range(2):
        q = np.broadcast_to(qk[:, None, :, w, :], (H0, 4, E0, D)).reshape(2 * P, D)
        stacked.append(q)
        bias.append(np.broadcast_to(bqk[:, None, :, w], (H0, 4, E0)).reshape(2, P))
    w_qk = np.concatenate(stacked).T
    w_var = np.concatenate([a["L0_attn_Wv_w"], a["L0_ffn_A"].reshape(NEXP * RANK0, D), a["L0_ffn_W_router"]]).T
    w_exp = a["L0_ffn_B"].transpose(0, 2, 1).reshape(P, D)
    w_o = np.broadcast_to(a["L0_attn_Wo_w"].T.reshape(H0, 1, E0, D), (H0, 2, E0, D)).reshape(P, D)
    w0 = np.concatenate([tiles(w_qk), tiles(w_var), tiles(a["L0_ffn_W_base"].T), w_exp, w_o], 1)

    wq = a["L1_attn_Wq"].reshape(HKV, GRP * HD, D)
    wk = a["L1_attn_Wk"].reshape(HKV, HD, D)
    wv = a["L1_attn_Wv"].reshape(HKV, HD, D)
    wo = a["L1_attn_Wo"].T.reshape(HKV, GRP * HD, D)
    w1 = np.concatenate([np.concatenate([tiles(np.concatenate([wq[g], wk[g], wv[g]]).T), tiles(wo[g])], 1)
                         for g in range(HKV)])

    pad = FT * P - FF

    def ff_layout(up, down):
        up = np.pad(up.reshape(FF, D), ((0, pad), (0, 0))).reshape(FT, P, KT, P).transpose(3, 0, 2, 1)
        down = np.pad(down.reshape(D, FF), ((0, 0), (0, pad))).reshape(D, FT, P).transpose(2, 1, 0)
        both = np.concatenate([up.reshape(P, FT, D), down], 2).reshape(P, NDQ, DQN)
        return both.transpose(1, 0, 2).reshape(NDQ * P, DQN)

    codes = ff_layout(a["L1_ffn_w_up_codes"], a["L1_ffn_w_down_codes"])
    absmax = ff_layout(np.repeat(a["L1_ffn_w_up_absmax"], 64), np.repeat(a["L1_ffn_w_down_absmax"], 64))

    def wide(w):
        return np.pad(w, ((0, 0), (0, P - w.shape[1])))

    def tall(w):
        return np.pad(w, ((0, P - w.shape[0]), (0, 0)))

    lora = np.concatenate([
        tiles(wide(a["L1_ffn_w_up_lora_a"])), tall(np.pad(a["L1_ffn_w_up_lora_b"], ((0, 0), (0, pad)))),
        tiles(wide(np.pad(a["L1_ffn_w_down_lora_a"], ((0, pad), (0, 0))))), tall(a["L1_ffn_w_down_lora_b"])], 1)

    p = np.arange(P)
    e = np.arange(NEXP)
    tri = np.broadcast_to((e[None, :] < e[:, None]).reshape(1, -1), (P, NEXP * NEXP))
    copy = p % 32 // E0
    low_q, low_k = copy >= 2, copy % 2 == 1
    masks = np.stack([1 - 2 * low_q, low_q, 1 - 2 * low_k, low_k], 1)
    heads = HKV * GRP
    start = 2 ** (-2 ** (-(math.log2(heads) - 3)))
    slopes = np.array([start * start ** i for i in range(heads)], np.float32)
    inverse = np.concatenate([(1.0 / slopes.astype(np.float64)).reshape(HKV, GRP), np.ones((HKV, 1))], 1)
    consts = np.concatenate([
        np.eye(P), tri, masks, np.stack([*bias[0], *bias[1]], 1),
        np.stack([a["L1_attn_q_norm_w"], a["L1_attn_k_norm_w"]], 1),
        np.pad(a["L1_ffn_b_up"], (0, pad)).reshape(FT, P).T,
        np.broadcast_to(slopes, (P, heads)), np.broadcast_to(inverse.reshape(1, -1), (P, HKV * 5)),
        np.broadcast_to([-0.5] * 5 + [-1.0] * 4, (P, 9)), np.broadcast_to(a["L1_ffn_b_down"], (P, D)),
    ], 1).astype(np.float32)
    rows = np.broadcast_to(np.concatenate([a["L0_attn_Wv_b"], a["L0_attn_Wo_b"], a["L0_ffn_b_base"]]), (P, NROWS))
    gap = np.arange(TOK)[None, :] - (TOK - P) - p[:, None]
    rel = np.where(gap > 0, -1e33, gap).astype(np.float32)

    nc = bacc.Bacc("TRN2", target_bir_lowering=False, num_devices=1)
    arrays = {"x": a["L0_attn_x"].reshape(TOK, D), "w0": w0, "w1": w1, "codes": codes, "absmax": absmax, "lora": lora,
              "consts": consts, "rows": rows, "rel": rel}
    arrays = {k: np.ascontiguousarray(v) for k, v in arrays.items()}
    args = [nc.dram_tensor(k, v.shape, mybir.dt.from_np(v.dtype), kind="ExternalInput").ap() for k, v in arrays.items()]
    out = nc.dram_tensor("out", (TOK, D), F32, kind="ExternalOutput").ap()
    program(nc, *args, out)
    res = run_bass_kernel_spmd(nc, [arrays], core_ids=[0])
    return res.results[0]["out"].reshape(1, TOK, D)
```

```python
import math
import numpy as np
import concourse.bass as bass
from concourse import mybir
from contextlib import ExitStack

F32 = mybir.dt.float32
F32R = mybir.dt.float32r
I32 = mybir.dt.int32
ALU = mybir.AluOpType
ACT = mybir.ActivationFunctionType
AX = mybir.AxisListType

P = 128
TOK, D = 1024, 512
NT, KT = TOK // P, D // P
H0, E0 = 8, 8
NEXP, RANK0 = 8, 16
HKV, GRP, HD = 8, 4, 128
FF, RANK1 = 1376, 16
FT = -(-FF // P)
LN_EPS, RMS_EPS = 1e-5, 1e-6

WQK_H, WQK_L = 0, 2048
WBASE_H, WBASE_L = 4096, 6144
NVAR = 256
WVAR_H, WVAR_L = 8192, 9216
WEXP_H, WEXP_L = 10240, 10752
WO0_H, WO0_L = 11264, 11776
QS, KS = 12288, 14336
VPAD = 0
W_H, W_L = 0, 5120
WOUT = KT * 768
QT = 10240
KTR = 12288
VN = 14336
PT = 16384
OT = 19456
ARENA = 21504
FW = (0, 5120, 2048)
LA_H, LA_L = 7168, 7680
X2 = 8192
LB_H, LB_L = 10240, 11648
DLA_H, DLA_L = 13056, 14464
DLB_H, DLB_L = 15872, 16384
XLA = 16896
ZT = 17920

C_ID = 0
C_TRI = C_ID + P
C_MASK = C_TRI + NEXP * NEXP
C_BQK = C_MASK + 4
C_QKW = C_BQK + 4
C_BUP = C_QKW + 2
C_SLOPE = C_BUP + FT
C_ISL = C_SLOPE + HKV * GRP
C_EXP = C_ISL + HKV * 5
C_BD = C_EXP + 9
NCONST = C_BD + D
R_BV, R_BO, R_BB = 0, 64, 64 + D
NROWS = 64 + 2 * D

NF4 = [-1.0, -0.6961928009986877, -0.5250730514526367, -0.39491748809814453, -0.28444138169288635,
       -0.18477343022823334, -0.09105003625154495, 0.0, 0.07958029955625534, 0.16093020141124725,
       0.24611230194568634, 0.33791524171829224, 0.44070982933044434, 0.5626170039176941,
       0.7229568362236023, 1.0]
LINES = [(NF4[2 * k + 1] - NF4[2 * k], NF4[2 * k] - 2 * k * (NF4[2 * k + 1] - NF4[2 * k])) for k in range(8)]
DQN = 704
NDQ = FT * 1024 // DQN

RAWC = 768


def _cut(src, hi, lo, n, step):
    return [(src + a, hi + a, lo + a, min(step, n - a)) for a in range(0, n, step)]


L0_CHUNKS = (_cut(0, WQK_H, WQK_L, 2048, RAWC) + _cut(2048, WVAR_H, WVAR_L, KT * NVAR, 512)
             + _cut(3072, WBASE_H, WBASE_L, 2048, RAWC) + _cut(5120, WEXP_H, WEXP_L, 512, 512)
             + _cut(5632, WO0_H, WO0_L, 512, 512))
W0_QK, W0_VAR, W0_BASE, W0_EXP, W0_O = 3, 5, 8, 9, 10
NL0 = len(L0_CHUNKS)
QL1 = NL0
QFF = QL1 + 8 * HKV
FF_CHUNKS = ([(True, 0, LA_H, LA_L, 512, P)]
             + [(False, u * 1024 + a, FW[u] + a, FW[u] + 1024 + a, 512, P) for u in (0, 1) for a in (0, 512)]
             + [(True, 512 + a, LB_H + a, LB_L + a, 704, RANK1) for a in (0, 704)]
             + [(True, 1920 + a, DLA_H + a, DLA_L + a, 704, P) for a in (0, 704)]
             + [(True, 3328, DLB_H, DLB_L, 512, RANK1)])
FF_LA, FF_W, FF_LB, FF_DLA, FF_DLB = 1, (3, 5), 7, 9, 10
FF_EARLY = 7
NFFC = len(FF_CHUNKS)

STEPS = NT * HKV


def slot_items(n):
    i = n % NT
    nk = i + 1
    group = {a: [kb for kb in range(nk) if 3 - (nk - 1 - kb) * 4 // nk == a] for a in range(4)}
    s1, s2 = n + 1 < STEPS, n + 2 < STEPS
    seq = []

    def put(*names, when=True):
        if when:
            seq.extend(names)

    put("V")
    for a in range(4):
        put(("S", a), when=s1)
        if a == 1:
            put("PQ", "PKV", when=s2)
        if a == 2:
            put("QN", when=s2)
        if a > 0:
            put(("NR", a - 1), when=s1)
        put(*[("T", kb) for kb in group[a]])
        if a == 0:
            put("WO", when=n > 0)
        put(("EX", a), when=s1)
        if n < STEPS - NT and (i == 5 and a > 0 or i == 6 and a == 0):
            put(("CH", a - 1 if i == 5 else 3))
        if n and i == 0 and a > 0:
            put(("CH", a + 3))
        if n >= STEPS - 2:
            put(("FC", a + 4 * (i - 6)), when=a + 4 * (i - 6) < FF_EARLY)
        if a == 1:
            put("DA")
    put("QK", when=s2)
    put(("CH", 7), when=n and i == 0)
    put(("NR", 3), when=s1)
    put("E", "DB")
    return seq


T_LN0, T_QK, T_VAR, T_HW, T_ATT = 0, 8, 16, 24, 32
T_LN1 = T_ATT + 2 * H0 * NT
T_PRO = T_LN1 + NT
T_BASE = T_PRO + 6
S_ATT, S_PRO = NT, NT + 2 * H0 * 4
S_BASE = S_PRO + 4
W_PRO = NT
W_BASE = W_PRO + 2
PV_BASE = 2 * H0 * NT
OT_BASE = 2
EX_PRO = 2 * H0 * 4
EX_BASE = EX_PRO + 4
P_PER, V_PER = 56, 3


def _tables():
    t, s, w, pv = T_BASE, S_BASE, W_BASE, PV_BASE
    at = {}
    for n in range(STEPS):
        for x in slot_items(n):
            if x in ("PKV",) or x[0] == "T":
                at[n, x] = t
                t += 1
            elif x == "QK":
                at[n, "QT"], at[n, "KT"] = t, t + 1
                t += 2
            elif x[0] == "S":
                at[n, x] = s
                s += 1
            elif x in ("PQ", "WO"):
                at[n, x] = w
                w += 1
        at[n, "last"] = t - 1
        for kb in range(n % NT + 1):
            at[n, ("PV", kb)] = pv
            pv += 1
    at[STEPS, "WO"] = w
    return at, t, s, w + 1, pv


AT, T_END, S_END, W_END, PV_END = _tables()


def w1_place(c):
    return (c * 768, 768) if c < 4 else (WOUT + (c - 4) * 512, 512)


def at(g, i, name):
    if isinstance(g, int):
        return AT[8 * g + i, name]
    return g * (AT[8 + i, name] - AT[i, name]) + AT[i, name]


def hold(eng, sem, value, passed):
    eng.wait_ge(sem, value)
    if not isinstance(value, int):
        eng.sem_inc(passed, 1)


class Tally:

    def __init__(self, eng, sem, passed):
        self.eng, self.sem, self.passed, self.base, self.n = eng, sem, passed, 0, 0

    def done(self, ins):
        ins.then_inc(self.sem, 1)
        self.n += 1

    def settle(self):
        hold(self.eng, self.sem, self.base + self.n, self.passed)

    def link(self, ins):
        self.done(ins)
        self.settle()


def slots(eng, tallies, slot):
    slot(0, 0)
    start = [t.n for t in tallies]
    probe = []
    with eng.Fori(0, HKV - 1) as g:
        for t in tallies:
            t.n = 0
            t.base = t.per * g + start[tallies.index(t)]
        for i in range(1, NT + 1):
            slot(g, i)
        for t in tallies:
            assert t.n == t.per, (t.n, t.per)
            probe.append(t.n)
    for t, s in zip(tallies, start):
        t.base, t.n = 0, s + (HKV - 1) * t.per
    for i in range(1, NT):
        slot(HKV - 1, i)


def program(nc, x, w0, w1, codes, absmax, lora, consts, rows, rel, out):
    with ExitStack() as ctx:
        def sb(name, shape, dt=F32):
            return ctx.enter_context(nc.sbuf_tensor(name, shape, dt))

        def sem(name):
            return ctx.enter_context(nc.semaphore(name))

        x1_dram = nc.dram_tensor("x1_scratch", (TOK, D), F32, kind="Internal").ap()
        wd_dram = nc.dram_tensor("dequantised", (P, FT * 1024), F32, kind="Internal").ap()

        XT = sb("XT", [P, 2, KT, TOK], F32R)
        R = sb("R", [P, ARENA], F32R)
        G = sb("G", [P, NT * D])
        PB = sb("PB", [P, 2, 4, TOK])
        REL = sb("REL", [P, TOK])
        RAW = sb("RAW", [P, 2, RAWC])
        QN = sb("QN", [P, 5 * HD])
        VS = sb("VS", [P, 4, HD])
        DQ = sb("DQ", [P, 4, DQN])
        C = sb("C", [P, NCONST])
        JUNK = sb("JUNK", [P, 10, HD], mybir.dt.bfloat16)
        NM = sb("NM", [P, 8])
        SM = sb("SM", [P, 8])
        RI = sb("RI", [P, 8])
        SQ = sb("SQ", [P, 2, 5])
        SQB = sb("SQB", [P, 2, 5])
        SQC = sb("SQC", [P, 2, 5])
        INV = sb("INV", [P, 2, 5])
        SLC = sb("SLC", [P, 4])
        QKW = sb("QKW", [P, 2])
        ST = sb("ST", [P, 2, 6])
        MV = sb("MV", [P, 2, 2])
        VE = sb("VE", [P, 2])
        RSTD = sb("RSTD", [P, 2])
        CMP = sb("CMP", [P, 2, 512])
        RT = sb("RT", [P, 8, 64])

        LA = DQ[:, :, :].rearrange("p a n -> p (a n)")
        HN = LA[:, 0:1024]
        VN0 = LA[:, 1024:1536]
        ROWS = LA[:, 1536:1536 + NROWS]
        PBF = PB[:, :, :, :].rearrange("p a b n -> p (a b n)")
        XS = [PBF[:, t * D:(t + 1) * D] for t in range(4)]
        XN = [PBF[:, (4 + t) * D:(5 + t) * D] for t in range(4)]
        TMP = [PBF[:, (8 + t) * D:(9 + t) * D] for t in range(6)]
        CODES = DQ[:, 0, :].bitcast(I32)
        Y_AT = (6, 7, 14, 15)
        IDENT = C[:, C_ID:C_ID + P]

        S = [ctx.enter_context(nc.psum_tensor(f"S{k}", [P, 1024], F32)) for k in range(2)]
        T = [ctx.enter_context(nc.psum_tensor(f"T{k}", [P, 512], F32)) for k in range(2)]
        VB = ctx.enter_context(nc.psum_tensor("VB", [P, 512], F32))
        WB = ctx.enter_context(nc.psum_tensor("WB", [P, 512], F32))

        in_const = sem("in_const")
        in_rows = sem("in_rows")
        in_x = [sem(f"in_x{k}") for k in range(4)]
        in_raw = [sem(f"in_raw{k}") for k in range(2)]
        in_codes = sem("in_codes")
        in_absmax = sem("in_absmax")
        in_fw = [sem(f"in_fw{k}") for k in range(2)]
        in_x1 = [sem(f"in_x1{k}") for k in range(4)]
        out_x1 = [sem(f"out_x1{k}") for k in range(4)]
        out_dq = sem("out_dq")
        out_y = [sem(f"out_y{k}") for k in range(4)]
        t_full = sem("t_full")
        t_act = sem("t_act")
        t_free = sem("t_free")
        s_full = sem("s_full")
        s_free = sem("s_free")
        w_full = sem("w_full")
        w_free = sem("w_free")
        pv_done = sem("pv_done")
        ot_high = sem("ot_high")
        ot_low = sem("ot_low")
        max_ready = sem("max_ready")
        exp_done = sem("exp_done")
        probs_ready = sem("probs_ready")
        w_high = sem("w_high")
        split = sem("split")
        vpad_ready = sem("vpad_ready")
        v_split = sem("v_split")
        squares = sem("squares")
        inv_ready = sem("inv_ready")
        qk_ready = sem("qk_ready")
        var_ready = sem("var_ready")
        rstd_ready = sem("rstd_ready")
        xn_ready = sem("xn_ready")
        x1_ready = sem("x1_ready")
        row_ready = sem("row_ready")
        row_exp = sem("row_exp")
        hw_ready = sem("hw_ready")
        y_ready = sem("y_ready")
        y_tanh = sem("y_tanh")
        gate_done = sem("gate_done")
        line = sem("line")
        line_used = sem("line_used")
        dq_selected = sem("dq_selected")
        dq_scaled = sem("dq_scaled")
        fw_high = sem("fw_high")
        fw_split = sem("fw_split")
        x2_ready = sem("x2_ready")
        z_high = sem("z_high")
        z_low = sem("z_low")
        d_full = sem("d_full")
        d_free = sem("d_free")
        out_done = sem("out_done")
        a_chain = sem("a_chain")
        v_chain = sem("v_chain")
        p_chain = sem("p_chain")
        v_passed = sem("v_passed")
        p_passed = sem("p_passed")

        block = ctx.enter_context(nc.Block())

        def r(off, n, p=P):
            return R[0:p, off:off + n]

        def rf(off, n, p=P):
            return R[0:p, off:off + n].bitcast(F32)

        @block.sync
        def _(sp):
            sp.dma_start(C[:, :], consts).then_inc(in_const, 16)
            for t in range(4):
                sp.dma_start(XS[t], x[t * P:(t + 1) * P, :]).then_inc(in_x[t], 16)

            def raw(q, src, rows_=P):
                if q >= 2:
                    sp.wait_ge(split, q - 1)
                n = src.shape[-1]
                sp.dma_start(RAW[0:rows_, q % 2, 0:n], src).then_inc(in_raw[q % 2], 16)

            for q in range(2):
                src, _, _, n = L0_CHUNKS[q]
                raw(q, w0[:, src:src + n])
            sp.dma_start(ROWS, rows).then_inc(in_rows, 16)
            for t in range(4, NT):
                sp.wait_ge(xn_ready, t - 3)
                sp.dma_start(XS[t % 4], x[t * P:(t + 1) * P, :]).then_inc(in_x[t % 4], 16)
                if t >= 5:
                    src, _, _, n = L0_CHUNKS[t - 3]
                    raw(t - 3, w0[:, src:src + n])
            for q in range(5, NL0):
                src, _, _, n = L0_CHUNKS[q]
                raw(q, w0[:, src:src + n])
            sp.dma_start(REL[:, :], rel).then_inc(out_dq, 16)

            def w1_chunk(g, c):
                q = QL1 + c
                a, n = (c * 768, 768) if c < 4 else (WOUT + (c - 4) * 512, 512)
                if isinstance(g, int):
                    raw(q + 8 * g, w1[g * P:(g + 1) * P, a:a + n])
                else:
                    sp.wait_ge(split, g * 8 + q - 1)
                    sp.dma_start(RAW[:, q % 2, 0:n], w1[bass.ds(g * P, P), a:a + n]).then_inc(in_raw[q % 2], 16)

            sp.wait_ge(t_full, T_ATT + (2 * H0 - 1) * NT)
            for t in range(4):
                sp.dma_start(XS[t], x[t * P:(t + 1) * P, :]).then_inc(in_x[t], 16)
            w1_chunk(0, 0)
            w1_chunk(0, 1)
            for t in range(NT):
                sp.wait_ge(x1_ready, t + 1)
                sp.dma_start(x1_dram[t * P:(t + 1) * P, :], XS[t % 4]).then_inc(out_x1[t % 4], 16)
                if t + 4 < NT:
                    sp.wait_ge(xn_ready, NT + t + 1)
                    sp.wait_ge(out_x1[t % 4], 16)
                    sp.dma_start(XS[t % 4], x[(t + 4) * P:(t + 5) * P, :]).then_inc(in_x[t % 4], 16)
                if t >= 2:
                    w1_chunk(0, t)

            def ff_chunk(q):
                lowrank, src, _, _, n, np_ = FF_CHUNKS[q]
                raw(QFF + q, (lora if lowrank else wd_dram)[0:np_, src:src + n], np_)

            def load_codes(g, i):
                if isinstance(g, int):
                    cc = (8 * g + i) // 4
                    if cc:
                        sp.wait_ge(dq_selected, cc)
                    else:
                        sp.wait_ge(xn_ready, 2 * NT)
                        sp.wait_ge(t_free, T_LN1 + NT)
                    sp.dma_start(CODES, codes[cc * P:(cc + 1) * P, :]).then_inc(in_codes, 16)
                else:
                    sp.wait_ge(dq_selected, g * 2 + i // 4)
                    sp.dma_start(CODES, codes[bass.ds(g * (2 * P) + i // 4 * P, P), :]).then_inc(in_codes, 16)

            def slot(g, i):
                jj = i % 4
                if jj == 0:
                    load_codes(g, i)
                if not (isinstance(g, int) and g == HKV - 1):
                    if i == 1:
                        w1_chunk(g + 1, 0)
                        w1_chunk(g + 1, 1)
                    if i == 5:
                        w1_chunk(g + 1, 2)
                        w1_chunk(g + 1, 3)
                    if i == 6:
                        w1_chunk(g + 1, 4)
                        w1_chunk(g + 1, 5)
                    if i == 8:
                        w1_chunk(g + 1, 6)
                        w1_chunk(g + 1, 7)
                elif i >= 5:
                    if i == 5:
                        sp.wait_ge(out_dq, 16 * (2 * 1024 // DQN + 2))
                    for q in {5: (0, 1), 6: (2, 3, 4), 7: (5, 6)}[i]:
                        ff_chunk(q)
                if jj == 0 and not (isinstance(g, int) and 8 * g + i == 0):
                    sp.wait_ge(dq_scaled, g * 2 + (i // 4 + 1))
                    sp.dma_start(wd_dram[:, bass.ds(g * (2 * DQN) + (i // 4 - 1) * DQN, DQN)], DQ[:, 1, :])\
                        .then_inc(out_dq, 16)
                if jj == 3:
                    sp.wait_ge(dq_selected, g * 2 + i // 4 + 1)
                    sp.dma_start(DQ[:, 3, :], absmax[bass.ds(g * (2 * P) + i // 4 * P, P), :]).then_inc(in_absmax, 16)

            slots(sp, [], slot)
            sp.wait_ge(dq_scaled, NDQ + 1)
            sp.dma_start(wd_dram[:, (NDQ - 1) * DQN:NDQ * DQN], DQ[:, 1, :]).then_inc(out_dq, 16)
            for q in range(FF_EARLY, NFFC):
                ff_chunk(q)
            sp.wait_ge(out_dq, 16 * (NDQ + 1))
            sp.wait_ge(t_full, AT[STEPS - 1, "last"] + 1)
            for u in range(2, 2 * FT):
                if u >= 4:
                    sp.wait_ge(fw_split, u - 3)
                sp.dma_start(PBF[:, u % 2 * 1024:(u % 2 + 1) * 1024],
                             wd_dram[:, u % FT * 1024:(u % FT + 1) * 1024]).then_inc(in_fw[u % 2], 16)
                if u in (2, FT + 8):
                    for tt in range(4):
                        t = u // FT * 4 + tt
                        if t >= 4:
                            sp.wait_ge(out_y[tt], 16)
                        sp.dma_start(PBF[:, (8 + tt) * D:(9 + tt) * D], x1_dram[t * P:(t + 1) * P, :])\
                            .then_inc(in_x1[tt], 16)
                if u == FT + 6 or u == 2 * FT - 1:
                    for tt in range(4):
                        t = u // (2 * FT - 1) * 4 + tt
                        sp.wait_ge(out_done, t + 1)
                        sp.dma_start(out[t * P:(t + 1) * P, :], PBF[:, (8 + tt) * D:(9 + tt) * D])\
                            .then_inc(out_y[tt], 16)
            for tt in range(4):
                sp.wait_ge(out_y[tt], 32)

        @block.gpsimd
        def _(pool):
            e = nc.gpsimd
            ch = Tally(pool, p_chain, p_passed)
            ch.per = P_PER

            def low_half(q, hi, lo, n, np_=P):
                hold(pool, w_high, q + 1, p_passed)
                e.tensor_tensor(r(lo, n, np_), RAW[0:np_, q % 2, 0:n], rf(hi, n, np_), ALU.subtract).then_inc(split, 1)

            def rstd(t):
                k = t % 2
                hold(pool, var_ready, t + 1, p_passed)
                ch.link(e.tensor_scalar(VE[:, k:k + 1], MV[:, k, 1:2], 1.0, LN_EPS, ALU.mult, ALU.add))
                e.tensor_tensor(RSTD[:, k:k + 1], VE[:, k:k + 1], C[:, C_EXP:C_EXP + 1], ALU.pow).then_inc(rstd_ready, 1)

            def divide(m, a, L, count, scale):
                k = m % 2 * 4 + a
                hold(pool, exp_done, count, p_passed)
                ch.link(e.tensor_tensor(RI[:, k:k + 1], SM[:, k:k + 1], C[:, C_EXP + 5:C_EXP + 6], ALU.pow))
                e.tensor_scalar(PB[:, m % 2, a, 0:L], PB[:, m % 2, a, 0:L], RI[:, k:k + 1], scale,
                                ALU.mult, ALU.mult).then_inc(probs_ready, 1)

            def inverse_rms(g, m, count):
                k = m % 2
                hold(pool, squares, count, p_passed)
                ch.link(e.tensor_scalar(SQB[:, k, :], SQ[:, k, :], 1.0 / HD, RMS_EPS, ALU.mult, ALU.add))
                ch.link(e.tensor_tensor(SQC[:, k, :], SQB[:, k, :], C[:, C_EXP:C_EXP + 5], ALU.pow))
                e.tensor_tensor(INV[:, k, :], SQC[:, k, :], C[:, bass.ds(g * 5 + C_ISL, 5)], ALU.mult)\
                    .then_inc(inv_ready, 1)

            hold(pool, in_const, 16, p_passed)
            rstd(0)
            rstd(1)
            for q in range(NL0):
                src, hi, lo, n = L0_CHUNKS[q]
                low_half(q, hi, lo, n)
                if 2 + q < NT:
                    rstd(2 + q)
            hold(pool, s_full, NT, p_passed)
            ch.link(e.memset(rf(VPAD, 8192), 0.0))
            hold(pool, t_free, T_VAR + NT, p_passed)
            src = VN0.rearrange("p (b h e) -> p b h e", b=NT, h=H0)

            whole = r(VPAD, 8192).rearrange("p (b n) -> p b n", b=NT)
            for h in range(H0):
                o = h * P + 2 * E0 * h
                hi_ap, lo_ap = whole[:, :, o:o + E0], whole[:, :, o + E0:o + 2 * E0]
                ch.link(e.tensor_copy(hi_ap, src[:, :, h, :]))
                e.tensor_tensor(lo_ap, src[:, :, h, :], hi_ap.bitcast(F32), ALU.subtract).then_inc(vpad_ready, 1)
            for n in range(2 * H0):
                for a in range(4):
                    divide(n, a, TOK, n * 4 + a + 1, 1.0 / math.sqrt(H0 * E0))
            for t in range(NT + 2):
                if t < NT:
                    rstd(NT + t)
                if t >= 2:
                    off, n = w1_place(t - 2)
                    low_half(QL1 + t - 2, W_H + off, W_L + off, n)
            for m in range(2):
                inverse_rms(0, m, 5 * m + 5)
            for a in range(4):
                divide(0, a, P, EX_PRO + a + 1, 1.0)

            def slot(g, i):
                n0 = g * 8 + i
                known = 8 * g + i if isinstance(g, int) else i
                L = (i + 1) % NT * P + P
                for it in slot_items(known if isinstance(g, int) else i):
                    if it == "V":
                        b = i % NT
                        if i < 2:
                            hold(pool, t_act, T_PRO + 3 * i + 1, p_passed)
                        if i >= 2:
                            hold(pool, t_act, at(g, i - 2, "PKV") + 1, p_passed)
                        elif i == 1:
                            hold(pool, t_act, g * 60 + (AT[NT - 1, "PKV"] - 60 + 1), p_passed)
                        if i == NT:
                            hold(pool, pv_done, at(g, NT - 1, ("PV", 0)) + 1, p_passed)
                        elif i:
                            hold(pool, pv_done, g * 36 + (AT[NT - 1, ("PV", b)] - 36 + 1), p_passed)
                        k = i % 4
                        ch.link(e.tensor_copy(r(VN + b * P, P), VS[:, k, :]))
                        e.tensor_tensor(r(VN + TOK + b * P, P), VS[:, k, :], rf(VN + b * P, P), ALU.subtract)\
                            .then_inc(v_split, 1)
                    elif it[0] == "NR":
                        a = it[1]
                        divide(i + 1, a, L, n0 * 4 + (EX_BASE + a + 1), 1.0)
                    elif it == "PKV":
                        inverse_rms(g + (i + 2) // 8, i + 2, n0 * 5 + 15)

            slots(pool, [ch], slot)
            hold(pool, w_full, W_END, p_passed)
            for q in range(FF_EARLY, NFFC):
                _, _, hi, lo, n, np_ = FF_CHUNKS[q]
                low_half(QFF + q, hi, lo, n, np_)
            for u in range(2, 2 * FT):
                hold(pool, fw_high, u - 1, p_passed)
                k = FW[u % 3]
                src = PBF[:, u % 2 * 1024:(u % 2 + 1) * 1024]
                e.tensor_tensor(r(k + 1024, 1024), src, rf(k, 1024), ALU.subtract).then_inc(fw_split, 1)

        @block.scalar
        def _(act):
            e = nc.scalar
            act.wait_ge(in_const, 16)

            def high_xt(k, t):
                act.wait_ge(t_full, k + 1)
                e.activation(XT[:, 0, :, t * P:(t + 1) * P], T[k % 2][:, :].rearrange("p (k n) -> p k n", k=KT),
                             ACT.Copy).then_inc(t_act, 1)

            def high_half(q, hi, n, np_=P, count=None):
                act.wait_ge(in_raw[q % 2], 16 * (q // 2 + 1) if count is None else count)
                e.activation(r(hi, n, np_), RAW[0:np_, q % 2, 0:n], ACT.Copy).then_inc(w_high, 1)

            for t in range(NT):
                high_xt(T_LN0 + t, t)
                high_half(t, L0_CHUNKS[t][1], L0_CHUNKS[t][3])
            for q in range(NT, NL0):
                high_half(q, L0_CHUNKS[q][1], L0_CHUNKS[q][3])
            for u in range(8):
                blk = u // 2
                k = T_QK + u
                act.wait_ge(t_full, k + 1)
                if u >= 2:
                    act.wait_ge(t_free, k - 1)
                e.activation(TMP[u % 2], T[k % 2][:, :], ACT.Identity, bias=C[:, C_BQK + blk:C_BQK + blk + 1])\
                    .then_inc(t_act, 1)
            for t in range(NT):
                k = T_VAR + t
                act.wait_ge(t_full, k + 1)
                e.activation(HN[:, t * P:(t + 1) * P], T[k % 2][:, 64:192], ACT.Copy).then_inc(t_act, 1)
            act.wait_ge(row_ready, 1)
            e.activation(RT[:, 2, :], RT[:, 1, :], ACT.Exp).then_inc(row_exp, 1)
            for t in range(NT):
                k = T_HW + t
                act.wait_ge(t_full, k + 1)
                if t >= 2:
                    act.wait_ge(s_full, t - 1)
                e.activation(r(OT + t % 2 * 256, P), T[k % 2][:, 0:P], ACT.Copy).then_inc(t_act, 1)
                if t >= 1:
                    act.wait_ge(y_ready, t)
                    if t >= 3:
                        act.wait_ge(gate_done, t - 2)
                    e.activation(TMP[2 + (t - 1) % 2], G[:, (t - 1) * D:t * D], ACT.Tanh, scale=0.5)\
                        .then_inc(y_tanh, 1)
            act.wait_ge(y_ready, NT)
            act.wait_ge(gate_done, NT - 2)
            e.activation(TMP[2 + (NT - 1) % 2], G[:, (NT - 1) * D:NT * D], ACT.Tanh, scale=0.5).then_inc(y_tanh, 1)

            def high_pt(k, c):
                act.wait_ge(t_full, k + 1)
                if isinstance(c, int) and c < 3:
                    pass
                else:
                    act.wait_ge(pv_done, c - 2)
                return T[k % 2]

            def exp0(n, a):
                u = n * 4 + a
                act.wait_ge(max_ready, u + 1)
                if n >= 2 and a == 0:
                    act.wait_ge(t_full, T_ATT + (n - 1) * NT)
                if u == 0:
                    act.wait_ge(gate_done, NT)
                k = n % 2 * 4 + a
                e.activation(PB[:, n % 2, a, :], S[u % 2][:, :], ACT.Exp, bias=NM[:, k:k + 1],
                             accum_out=SM[:, k:k + 1]).then_inc(exp_done, 1)

            for a in range(4):
                exp0(0, a)
            for n in range(2 * H0):
                for kb in range(NT):
                    c = n * NT + kb
                    k = T_ATT + c
                    act.wait_ge(t_full, k + 1)
                    if c >= 3:
                        act.wait_ge(pv_done, c - 2)
                    e.activation(r(PT + c % 3 * 1024, 512), T[k % 2][:, :], ACT.Copy).then_inc(t_act, 1)
                    if kb % 2 == 1 and n + 1 < 2 * H0:
                        exp0(n + 1, kb // 2)
                if n % H0 == H0 - 1:
                    qg = n // H0
                    act.wait_ge(pv_done, (n + 1) * NT)
                    e.activation(r(OT + qg * 1024, 512), VB[:, :], ACT.Copy).then_inc(ot_high, 1)
            for t in range(NT):
                high_xt(T_LN1 + t, t)
                high_half(QL1 + t, W_H + w1_place(t)[0], w1_place(t)[1])

            def sum_squares(m, wcount, k):
                act.wait_ge(w_full, wcount)
                for a in range(4):
                    e.activation(JUNK[:, m % 2 * 5 + a, :], WB[:, a * HD:(a + 1) * HD], ACT.Square,
                                 accum_out=SQ[:, m % 2, a:a + 1]).then_inc(squares, 1)
                return k

            def squares_k(m, tcount, tk):
                act.wait_ge(t_full, tcount)
                e.activation(JUNK[:, m % 2 * 5 + 4, :], tk[:, 0:HD], ACT.Square, accum_out=SQ[:, m % 2, 4:5]).then_inc(squares, 1)
                e.activation(VS[:, m % 4, :], tk[:, HD:2 * HD], ACT.Copy).then_inc(t_act, 1)

            def high_qk(m, tq, tk, bq, bk):
                act.wait_ge(t_full, tq)
                e.activation(r(QT + m % 2 * 1024, 512), bq[:, :], ACT.Copy, scale=QKW[:, 0:1]).then_inc(t_act, 1)
                act.wait_ge(t_full, tk)
                e.activation(r(KTR + m % NT * P, P), bk[:, 0:P], ACT.Copy, scale=QKW[:, 1:2]).then_inc(t_act, 1)

            def exp1(m, a, L, count):
                act.wait_ge(s_free, count)
                k = m % 2 * 4 + a
                e.activation(PB[:, m % 2, a, 0:L], PB[:, m % 2, a, 0:L], ACT.Exp, scale=-1.0, bias=NM[:, k:k + 1],
                             accum_out=SM[:, k:k + 1]).then_inc(exp_done, 1)

            for m in range(2):
                sum_squares(m, W_PRO + m + 1, None)
                k = T_PRO + 3 * m
                squares_k(m, k + 1, T[k % 2])
                high_qk(m, k + 2, k + 3, T[(k + 1) % 2], T[k % 2])
            for a in range(4):
                exp1(0, a, P, a + 1)

            def lines(g, i, part):
                jj = i % 4
                todo = {(1, 0): (0, 1), (1, 1): (2,), (2, 0): (3, 4), (2, 1): (5,), (3, 0): (6,), (3, 1): (7,)}
                for ln in todo.get((jj, part), ()):
                    chunk = g * 2 + i // 4
                    to = {0: 1, 4: 2}.get(ln, 3)
                    if ln == 0:
                        act.wait_ge(in_codes, (chunk + 1) * 16)
                        act.wait_ge(out_dq, chunk * 16 + 16)
                    if ln > 1 and to == 3:
                        act.wait_ge(line_used, chunk * 6 + {2: 1, 3: 2, 5: 3, 6: 4, 7: 5}[ln])
                    if ln == 1:
                        act.wait_ge(dq_scaled, chunk + 1)
                    sc, bi = LINES[ln]
                    e.activation(DQ[:, to, :], CODES, ACT.Copy, scale=sc, bias=bi).then_inc(line, 1)

            def slot(g, i):
                known = 8 * g + i if isinstance(g, int) else i
                n0 = g * 8 + i
                L = (i + 1) % NT * P + P
                for it in slot_items(known):
                    if it[0] == "T":
                        kb = it[1]
                        c = at(g, i, ("PV", kb))
                        act.wait_ge(t_full, at(g, i, it) + 1)
                        act.wait_ge(pv_done, c - 2)
                        e.activation(r(PT + AT[i, ("PV", kb)] % 3 * 1024, 512), T[AT[known, it] % 2][:, :],
                                     ACT.Copy).then_inc(t_act, 1)
                    elif it[0] == "EX":
                        exp1(i + 1, it[1], L, at(g, i, ("S", it[1])) + (1 - S_PRO))
                    elif it == "PQ":
                        sum_squares(i + 2, at(g, i, "PQ") + 1, None)
                    elif it == "PKV":
                        squares_k(i + 2, at(g, i, "PKV") + 1, T[AT[known, "PKV"] % 2])
                    elif it == "QK":
                        high_qk(i + 2, at(g, i, "QT") + 1, at(g, i, "KT") + 1,
                                T[AT[known, "QT"] % 2], T[AT[known, "KT"] % 2])
                    elif it == "E":
                        act.wait_ge(pv_done, at(g, i, ("PV", i % NT)) + 1)
                        e.activation(r(OT + i % 2 * 1024, 512), VB[:, :], ACT.Copy).then_inc(ot_high, 1)
                    elif it[0] == "CH":
                        c = it[1]
                        if c == 0:
                            act.wait_ge(t_full, at(g, i, "PKV") + 1)
                        if c == 4:
                            act.wait_ge(w_full, at(g, i, "WO") + 1)
                        q = QL1 + c
                        high_half(q, W_H + w1_place(c)[0], w1_place(c)[1], count=(g + 1) * 64 + 16 * (q // 2 + 1))
                    elif it[0] == "FC":
                        _, _, hi, _, n, np_ = FF_CHUNKS[it[1]]
                        high_half(QFF + it[1], hi, n, np_)
                    elif it == "DA":
                        lines(g, i, 0)
                    elif it == "DB":
                        lines(g, i, 1)

            slots(act, [], slot)
            def high_xla(tg):
                k = T_END + tg * (FT + 1)
                act.wait_ge(t_full, k + 1)
                e.activation(r(XLA, 512, RANK1), T[k % 2][0:RANK1, :], ACT.Copy).then_inc(t_act, 1)

            def high_fw(u):
                act.wait_ge(in_fw[u % 2], 16 * (u // 2))
                if u >= 3:
                    act.wait_ge(x2_ready, u - 2)
                e.activation(r(FW[u % 3], 1024), PBF[:, u % 2 * 1024:(u % 2 + 1) * 1024], ACT.Copy).then_inc(fw_high, 1)

            high_xla(0)
            act.wait_ge(w_full, W_END)
            for q in range(FF_EARLY, NFFC):
                _, _, hi, _, n, np_ = FF_CHUNKS[q]
                high_half(QFF + q, hi, n, np_)
            for tg in range(2):
                k = T_END + tg * (FT + 1)
                for j in range(FT):
                    u = tg * FT + j
                    kk = k + 1 + j
                    act.wait_ge(t_full, kk + 1)
                    if u >= 2:
                        act.wait_ge(t_free, T_END + (u - 2) // FT * (FT + 1) + (u - 2) % FT + 2)
                    e.activation(PBF[:, 2048 + u % 2 * 512:2560 + u % 2 * 512], T[kk % 2][:, :], ACT.Relu,
                                 bias=C[:, C_BUP + j:C_BUP + j + 1]).then_inc(t_act, 1)
                    if u + 2 < 2 * FT:
                        high_fw(u + 2)
                act.wait_ge(x2_ready, (tg + 1) * FT)
                e.activation(r(ZT, 512, RANK1), VB[0:RANK1, :], ACT.Copy).then_inc(z_high, 1)
                if tg == 0:
                    high_xla(1)
                for tt in range(4):
                    act.wait_ge(y_ready, NT + tg * 4 + tt + 1)
                    e.activation(DQ[:, tt, 0:D], PBF[:, Y_AT[tt] * D:(Y_AT[tt] + 1) * D], ACT.Tanh, scale=0.5)\
                        .then_inc(y_tanh, 1)

        @block.vector
        def _(dve):
            e = nc.vector
            ch = Tally(dve, v_chain, v_passed)
            ch.per = V_PER

            def normalise(t, src, slot_):
                k = t % 2
                ch.link(e.bn_stats(ST[:, k, :], src))
                e.bn_aggr(MV[:, k, :], ST[:, k, :]).then_inc(var_ready, 1)
                dve.wait_ge(var_ready, t + 1)
                dve.wait_ge(rstd_ready, t + 1)
                e.tensor_scalar(XN[slot_], src, MV[:, k, 0:1], RSTD[:, k:k + 1], ALU.subtract, ALU.mult)\
                    .then_inc(xn_ready, 1)

            def low_xt(k, t):
                dve.wait_ge(t_act, k + 1)
                e.tensor_tensor(XT[:, 1, :, t * P:(t + 1) * P], T[k % 2][:, :].rearrange("p (k n) -> p k n", k=KT),
                                XT[:, 0, :, t * P:(t + 1) * P].bitcast(F32), ALU.subtract).then_inc(t_free, 1)

            dve.wait_ge(in_const, 16)
            ch.done(e.tensor_scalar(QKW[:, 0:1], C[:, C_QKW:C_QKW + 1], 1.0 / math.sqrt(HD), None, ALU.mult))
            e.memset(CMP[:, 0, 0:8], 0.0).then_inc(dq_scaled, 1)
            ch.done(e.tensor_copy(QKW[:, 1:2], C[:, C_QKW + 1:C_QKW + 2]))
            ch.done(e.tensor_scalar(SLC[:, :], C[:, C_SLOPE:C_SLOPE + 4], -1.0, None, ALU.mult))
            for t in range(NT):
                dve.wait_ge(in_x[t % 4], 16 * (t // 4 + 1))
                if t >= 4:
                    dve.wait_ge(t_full, t - 3)
                normalise(t, XS[t % 4], t % 4)
                if t:
                    low_xt(t - 1, t - 1)
            low_xt(NT - 1, NT - 1)
            for u in range(8):
                blk, nt = u // 2, u % 2
                k = T_QK + u
                dve.wait_ge(t_act, k + 1)
                dve.wait_ge(t_free, k)
                m = C_MASK + 2 * (blk // 2)
                hi = r(PT + u % 2 * 512, 512)
                ch.done(e.tensor_copy(hi, TMP[u % 2]))
                ch.link(e.tensor_scalar(TMP[4], TMP[u % 2], C[:, m + 1:m + 2], None, ALU.mult))
                dst = (QS if blk < 2 else KS) + blk % 2 * 1024 + nt * 512
                e.scalar_tensor_tensor(r(dst, 512), hi.bitcast(F32), C[:, m:m + 1], TMP[4],
                                       ALU.mult, ALU.add).then_inc(t_free, 1)
            dve.wait_ge(in_rows, 16)
            for t in range(NT):
                k = T_VAR + t
                dve.wait_ge(t_act, k + 1)
                ch.done(e.tensor_copy(RT[:, 0, t * 8:t * 8 + 8], T[k % 2][:, 192:200]))
                e.tensor_tensor(VN0[:, t * 64:t * 64 + 64], T[k % 2][:, 0:64], ROWS[:, R_BV:R_BV + 64], ALU.add)\
                    .then_inc(t_free, 1)
            ch.settle()

            def by_e(k):
                return RT[:, k, :].rearrange("p (t e) -> p t e", e=NEXP)

            def over_e(a):
                return a.unsqueeze(2).to_broadcast([P, NT, NEXP])

            ch.link(e.tensor_reduce(RT[:, 3, 0:NT], by_e(0), AX.X, ALU.max))
            e.tensor_tensor(by_e(1), by_e(0), over_e(RT[:, 3, 0:NT]), ALU.subtract).then_inc(row_ready, 1)
            dve.wait_ge(row_exp, 1)
            ch.link(e.tensor_reduce(RT[:, 3, 8:16], by_e(2), AX.X, ALU.add))
            ch.link(e.reciprocal(RT[:, 3, 16:24], RT[:, 3, 8:16]))
            ch.link(e.tensor_tensor(by_e(4), by_e(2), over_e(RT[:, 3, 16:24]), ALU.mult))
            pj = by_e(4).unsqueeze(2).to_broadcast([P, NT, NEXP, NEXP])
            pe_ = by_e(4).unsqueeze(3).to_broadcast([P, NT, NEXP, NEXP])

            def cmp4(k):
                return CMP[:, k, :].rearrange("p (t e j) -> p t e j", e=NEXP, j=NEXP)

            ch.done(e.tensor_tensor(cmp4(0), pj, pe_, ALU.is_gt))
            ch.link(e.tensor_tensor(cmp4(1), pj, pe_, ALU.is_equal))
            tri = C[:, C_TRI:C_TRI + 64].unsqueeze(1).to_broadcast([P, NT, 64])
            c1 = CMP[:, 1, :].rearrange("p (t n) -> p t n", t=NT)
            ch.link(e.tensor_tensor(c1, c1, tri, ALU.mult))
            ch.link(e.tensor_tensor(CMP[:, 0, :], CMP[:, 0, :], CMP[:, 1, :], ALU.add))
            ch.link(e.tensor_reduce(RT[:, 5, :], CMP[:, 0, :].rearrange("p (n j) -> p n j", j=NEXP), AX.X, ALU.add))
            ch.link(e.scalar_tensor_tensor(RT[:, 6, :], RT[:, 5, :], 1.5, RT[:, 4, :], ALU.is_lt, ALU.mult))
            ch.link(e.tensor_reduce(RT[:, 3, 24:32], by_e(6), AX.X, ALU.add))
            ch.link(e.reciprocal(RT[:, 3, 32:40], RT[:, 3, 24:32]))
            ch.link(e.tensor_tensor(by_e(7), by_e(6), over_e(RT[:, 3, 32:40]), ALU.mult))
            ch.link(e.tensor_scalar(RT[:, 7, :], RT[:, 7, :], 2.0, None, ALU.mult))
            hn = HN.rearrange("p (n r) -> p n r", r=RANK0)
            e.tensor_tensor(hn, hn, RT[:, 7, :].unsqueeze(2).to_broadcast([P, 64, RANK0]), ALU.mult)\
                .then_inc(hw_ready, 1)

            def ffn0_out(t):
                dve.wait_ge(s_full, t + 1)
                e.tensor_tensor(G[:, t * D:(t + 1) * D], S[t % 2][:, 0:D], ROWS[:, R_BB:R_BB + D], ALU.add)\
                    .then_inc(y_ready, 1)

            def gate(t):
                dve.wait_ge(y_tanh, t + 1)
                e.scalar_tensor_tensor(G[:, t * D:(t + 1) * D], TMP[2 + t % 2], 1.0, G[:, t * D:(t + 1) * D],
                                       ALU.add, ALU.mult).then_inc(gate_done, 1)

            for t in range(NT):
                k = T_HW + t
                dve.wait_ge(t_act, k + 1)
                o = OT + t % 2 * 256
                e.tensor_tensor(r(o + P, P), T[k % 2][:, 0:P], rf(o, P), ALU.subtract).then_inc(t_free, 1)
                if t:
                    ffn0_out(t - 1)
                if t >= 2:
                    gate(t - 2)
            ffn0_out(NT - 1)
            gate(NT - 2)
            gate(NT - 1)

            def max0(n, a):
                u = n * 4 + a
                dve.wait_ge(s_full, S_ATT + u + 1)
                k = n % 2 * 4 + a
                if n >= 2:
                    dve.wait_ge(exp_done, u - 7)
                e.tensor_reduce(NM[:, k:k + 1], S[u % 2][:, :], AX.X, ALU.max, negate=True).then_inc(max_ready, 1)

            def low_pt(k, c, bank, kc):
                dve.wait_ge(t_act, k)
                o = PT + kc % 3 * 1024
                e.tensor_tensor(r(o + 512, 512), bank[:, :], rf(o, 512), ALU.subtract).then_inc(t_free, 1)

            for a in range(4):
                max0(0, a)
            for n in range(2 * H0):
                for kb in range(NT):
                    c = n * NT + kb
                    if kb % 2 == 0 and n + 1 < 2 * H0:
                        max0(n + 1, kb // 2)
                    low_pt(T_ATT + c + 1, c, T[(T_ATT + c) % 2], c)
                if n % H0 == H0 - 1:
                    o = OT + n // H0 * 1024
                    dve.wait_ge(ot_high, n // H0 + 1)
                    e.tensor_tensor(r(o + 512, 512), VB[:, :], rf(o, 512), ALU.subtract).then_inc(ot_low, 1)
            for t in range(NT):
                dve.wait_ge(w_full, t + 1)
                dve.wait_ge(in_x[t % 4], 16 * (t // 4 + 3))
                if t == 0:
                    dve.wait_ge(t_full, T_LN1)
                tmp = TMP[t % 2]
                e.tensor_tensor(tmp, WB[:, :], ROWS[:, R_BO:R_BO + D], ALU.add).then_inc(w_free, 1)
                dve.wait_ge(w_free, t + 1)
                ch.link(e.scalar_tensor_tensor(tmp, tmp, 0.5, G[:, t * D:(t + 1) * D], ALU.mult, ALU.mult))
                e.tensor_tensor(XS[t % 4], XS[t % 4], tmp, ALU.add).then_inc(x1_ready, 1)
                dve.wait_ge(x1_ready, t + 1)
                if t >= 4:
                    dve.wait_ge(t_full, T_LN1 + t - 3)
                normalise(NT + t, XS[t % 4], t % 4)
                if t:
                    low_xt(T_LN1 + t - 1, t - 1)
            low_xt(T_LN1 + NT - 1, NT - 1)
            ch.link(e.memset(G[:, :], 0.0))
            for k in range(4):
                dve.wait_ge(out_x1[k], 32)

            def copy_k(tcount, tk, tprev):
                dve.wait_ge(t_act, tcount)
                dve.wait_ge(t_full, tprev)
                e.tensor_copy(QN[:, 4 * HD:5 * HD], tk[:, 0:HD]).then_inc(t_free, 1)

            def scale_qk(m, icount, tcopy):
                dve.wait_ge(inv_ready, icount)
                dve.wait_ge(t_free, tcopy)
                k = m % 2
                e.tensor_tensor(QN[:, 0:4 * HD].rearrange("p (a n) -> p a n", a=4),
                                WB[:, :].rearrange("p (a n) -> p a n", a=4),
                                INV[:, k, 0:4].unsqueeze(2).to_broadcast([P, 4, HD]), ALU.mult).then_inc(w_free, 1)
                e.tensor_scalar(QN[:, 4 * HD:5 * HD], QN[:, 4 * HD:5 * HD], INV[:, k, 4:5], None, ALU.mult)\
                    .then_inc(qk_ready, 1)

            def low_qk(m, tq, tk, bq, bk):
                o = QT + m % 2 * 1024
                dve.wait_ge(t_act, tq)
                e.scalar_tensor_tensor(r(o + 512, 512), bq[:, :], QKW[:, 0:1], rf(o, 512), ALU.mult, ALU.subtract)\
                    .then_inc(t_free, 1)
                o = KTR + m % NT * P
                dve.wait_ge(t_act, tk)
                e.scalar_tensor_tensor(r(o + TOK, P), bk[:, 0:P], QKW[:, 1:2], rf(o, P), ALU.mult, ALU.subtract)\
                    .then_inc(t_free, 1)

            def bias_max(m, a, L, scount, bank):
                hold(dve, s_full, scount, v_passed)
                k = m % 2 * 4 + a
                e.tensor_tensor_reduce(out=PB[:, m % 2, a, 0:L], in0=bank[:, 0:L], in1=REL[:, TOK - L:TOK],
                                       scale=SLC[:, a:a + 1], scalar=3.0e38, op0=ALU.add, op1=ALU.min,
                                       accum_out=NM[:, k:k + 1]).then_inc(s_free, 1)

            for m in range(2):
                k = T_PRO + 3 * m
                copy_k(k + 1, T[k % 2], k)
                scale_qk(m, m + 1, k + 1)
                low_qk(m, k + 2, k + 3, T[(k + 1) % 2], T[k % 2])
            for a in range(4):
                bias_max(0, a, P, S_PRO + a + 1, S[a % 2])

            def combine(g, i, part):
                jj = i % 4
                chunk = g * 2 + i // 4
                if jj == 0 and part == 0 and not (isinstance(g, int) and 8 * g + i == 0):
                    dve.wait_ge(in_absmax, chunk * 16)
                    e.tensor_tensor(DQ[:, 1, :], DQ[:, 1, :], DQ[:, 3, :], ALU.mult).then_inc(dq_scaled, 1)
                todo = {(1, 0): (1,), (1, 1): (2,), (2, 0): (3,), (2, 1): (5,), (3, 0): (6,), (3, 1): (7,)}
                for ln in todo.get((jj, part), ()):
                    dve.wait_ge(line, chunk * 8 + ln + 1)
                    b, op = (1, ALU.min) if ln < 4 else (2, ALU.max)
                    if ln not in (1, 5):
                        dve.wait_ge(line_used, chunk * 6 + {2: 1, 3: 2, 6: 4, 7: 5}[ln])
                    e.tensor_tensor(DQ[:, b, :], DQ[:, b, :], DQ[:, 3, :], op).then_inc(line_used, 1)
                if (jj, part) == (3, 1):
                    ch.link(e.tensor_scalar(CODES, CODES, 8, None, ALU.bitwise_and))
                    hold(dve, line_used, chunk * 6 + 6, v_passed)
                    e.copy_predicated(DQ[:, 1, :], CODES, DQ[:, 2, :]).then_inc(dq_selected, 1)
                    dve.wait_ge(dq_selected, chunk + 1)

            def slot(g, i):
                known = 8 * g + i if isinstance(g, int) else i
                n0 = g * 8 + i
                L = (i + 1) % NT * P + P
                for it in slot_items(known):
                    if it[0] == "S":
                        a = it[1]
                        if i == 7 and a == 0:
                            ch.link(e.tensor_scalar(SLC[:, :], C[:, bass.ds(g * 4 + (C_SLOPE + 4), 4)], -1.0, None, ALU.mult))
                        if a == 0 and i > 0:
                            prev = (at(g, i - 1, "last") + 1) if i >= 1 else None
                            dve.wait_ge(t_full, prev)
                        bias_max(i + 1, a, L, at(g, i, it) + 1, S[AT[known, it] % 2])
                    elif it[0] == "T":
                        low_pt(at(g, i, it) + 1, None, T[AT[known, it] % 2], AT[i, ("PV", it[1])])
                    elif it == "WO":
                        dve.wait_ge(w_full, at(g, i, "WO") + 1)
                        t = (i - 1) % NT
                        dve.wait_ge(w_free, at(g, i, "WO"))
                        e.tensor_tensor(G[:, t * D:(t + 1) * D], G[:, t * D:(t + 1) * D], WB[:, :], ALU.add)\
                            .then_inc(w_free, 1)
                    elif it == "PKV":
                        prev = T_BASE if known == 0 and isinstance(g, int) else at(g, i - 1, "KT") + 1
                        copy_k(at(g, i, "PKV") + 1, T[AT[known, "PKV"] % 2], prev)
                    elif it == "QN":
                        scale_qk(i + 2, n0 + 3, at(g, i, "PKV") + 1)
                    elif it == "QK":
                        low_qk(i + 2, at(g, i, "QT") + 1, at(g, i, "KT") + 1,
                               T[AT[known, "QT"] % 2], T[AT[known, "KT"] % 2])
                    elif it == "E":
                        o = OT + i % 2 * 1024
                        dve.wait_ge(ot_high, n0 + 3)
                        e.tensor_tensor(r(o + 512, 512), VB[:, :], rf(o, 512), ALU.subtract).then_inc(ot_low, 1)
                    elif it[0] in ("CH", "FC"):
                        if it[0] == "CH":
                            hi, n = w1_place(it[1])
                            q, np_, hi, lo = QL1 + it[1], P, W_H + hi, W_L + hi
                            dve.wait_ge(w_high, (g + 1) * 8 + q + 1)
                        else:
                            _, _, hi, lo, n, np_ = FF_CHUNKS[it[1]]
                            q = QFF + it[1]
                            dve.wait_ge(w_high, q + 1)
                        e.tensor_tensor(r(lo, n, np_), RAW[0:np_, q % 2, 0:n], rf(hi, n, np_), ALU.subtract)\
                            .then_inc(split, 1)
                    elif it == "DA":
                        combine(g, i, 0)
                    elif it == "DB":
                        combine(g, i, 1)

            slots(dve, [ch], slot)
            dve.wait_ge(in_absmax, NDQ * 16)
            e.tensor_tensor(DQ[:, 1, :], DQ[:, 1, :], DQ[:, 3, :], ALU.mult).then_inc(dq_scaled, 1)
            dve.wait_ge(w_full, W_END)
            dve.wait_ge(w_free, W_END - 1)
            e.tensor_tensor(G[:, 7 * D:8 * D], G[:, 7 * D:8 * D], WB[:, :], ALU.add).then_inc(w_free, 1)
            def low_xla(tg):
                k = T_END + tg * (FT + 1)
                dve.wait_ge(t_act, k + 1)
                e.tensor_tensor(r(XLA + 512, 512, RANK1), T[k % 2][0:RANK1, :], rf(XLA, 512, RANK1), ALU.subtract)\
                    .then_inc(t_free, 1)

            def y_of(u):
                tt = u % 4
                dve.wait_ge(d_full, u + 1)
                y = PBF[:, Y_AT[tt] * D:(Y_AT[tt] + 1) * D]
                e.tensor_tensor(y, S[tt // 2][:, tt % 2 * D:(tt % 2 + 1) * D], C[:, C_BD:C_BD + D], ALU.add)\
                    .then_inc(y_ready, 1)

            def result(u):
                tt = u % 4
                dve.wait_ge(y_ready, NT + u + 1)
                dve.wait_ge(y_tanh, NT + u + 1)
                y = PBF[:, Y_AT[tt] * D:(Y_AT[tt] + 1) * D]
                ch.link(e.scalar_tensor_tensor(y, DQ[:, tt, 0:D], 1.0, y, ALU.add, ALU.mult))
                ch.link(e.scalar_tensor_tensor(y, y, 0.5, G[:, u * D:(u + 1) * D], ALU.mult, ALU.mult))
                dve.wait_ge(in_x1[tt], 16 * (u // 4 + 1))
                xx = PBF[:, (8 + tt) * D:(9 + tt) * D]
                e.tensor_tensor(xx, xx, y, ALU.add).then_inc(out_done, 1)
                dve.wait_ge(out_done, u + 1)

            low_xla(0)
            for tg in range(2):
                k = T_END + tg * (FT + 1)
                for j in range(FT):
                    u = tg * FT + j
                    kk = k + 1 + j
                    o = X2 + u % 2 * 1024
                    src = PBF[:, 2048 + u % 2 * 512:2560 + u % 2 * 512]
                    dve.wait_ge(t_act, kk + 1)
                    if u >= 2:
                        dve.wait_ge(x2_ready, u - 1)
                    ch.link(e.tensor_copy(r(o, 512), src))
                    e.tensor_tensor(r(o + 512, 512), src, rf(o, 512), ALU.subtract).then_inc(t_free, 1)
                    if tg and j < 4:
                        result(j)
                dve.wait_ge(z_high, tg + 1)
                e.tensor_tensor(r(ZT + 512, 512, RANK1), VB[0:RANK1, :], rf(ZT, 512, RANK1), ALU.subtract)\
                    .then_inc(z_low, 1)
                if tg == 0:
                    low_xla(1)
                    for u in range(4):
                        y_of(u)
            y_of(4)
            for u in range(4, 8):
                if u < 7:
                    y_of(u + 1)
                result(u)

        @block.tensor
        def _(pe):
            e = nc.tensor

            def mm3(dst, lh, ll, rh, rl, start, stop):
                e.matmul(dst, lh, rh, start=start, stop=False)
                e.matmul(dst, lh, rl, start=False, stop=False)
                return e.matmul(dst, ll, rh, start=False, stop=stop)

            def xt(half, kt, a, n):
                return XT[:, half, kt, a:a + n]

            def ring(k):
                if isinstance(k, int) and k < 2:
                    return
                pe.wait_ge(t_free, k - 1)

            def transpose_x(k, t, count):
                ring(k)
                pe.wait_ge(xn_ready, count)
                for kt in range(KT):
                    last = e.transpose(T[k % 2][:, kt * P:(kt + 1) * P], XN[t % 4][:, kt * P:(kt + 1) * P], IDENT)
                last.then_inc(t_full, 1)

            pe.wait_ge(in_const, 16)
            for t in range(NT):
                transpose_x(T_LN0 + t, t, t + 1)
            pe.wait_ge(split, W0_QK)
            pe.wait_ge(t_free, NT)
            for u in range(8):
                blk, nt = u // 2, u % 2
                k = T_QK + u
                ring(k)
                for kt in range(KT):
                    c = kt * 512 + blk * P
                    last = mm3(T[k % 2][:, :], r(WQK_H + c, P), r(WQK_L + c, P), xt(0, kt, nt * 512, 512),
                               xt(1, kt, nt * 512, 512), kt == 0, kt == KT - 1)
                last.then_inc(t_full, 1)
            pe.wait_ge(split, W0_VAR)
            for t in range(NT):
                k = T_VAR + t
                ring(k)
                for kt in range(KT):
                    c = kt * NVAR
                    last = mm3(T[k % 2][:, 0:NVAR], xt(0, kt, t * P, P), xt(1, kt, t * P, P), r(WVAR_H + c, NVAR),
                               r(WVAR_L + c, NVAR), kt == 0, kt == KT - 1)
                last.then_inc(t_full, 1)
            pe.wait_ge(split, W0_BASE)

            def base(t):
                if t >= 2:
                    pe.wait_ge(y_ready, t - 1)
                for kt in range(KT):
                    c = kt * 512
                    mm3(S[t % 2][:, 0:D], xt(0, kt, t * P, P), xt(1, kt, t * P, P), r(WBASE_H + c, D),
                        r(WBASE_L + c, D), kt == 0, False)

            base(0)
            base(1)
            pe.wait_ge(hw_ready, 1)
            pe.wait_ge(split, W0_EXP)
            for t in range(NT):
                k = T_HW + t
                ring(k)
                e.transpose(T[k % 2][:, 0:P], HN[:, t * P:(t + 1) * P], IDENT).then_inc(t_full, 1)
                if t >= 2:
                    base(t)
                pe.wait_ge(t_free, k + 1)
                o = OT + t % 2 * 256
                mm3(S[t % 2][:, 0:D], r(o, P), r(o + P, P), r(WEXP_H, D), r(WEXP_L, D), False, True)\
                    .then_inc(s_full, 1)

            def scores0(n, a):
                qg, h = n // H0, n % H0
                u = n * 4 + a
                if u >= 2:
                    pe.wait_ge(exp_done, u - 1)
                else:
                    pe.wait_ge(y_ready, NT - 1 + u)
                b = h % 4 * 32
                qc = QS + h // 4 * 1024 + (qg * 4 + a) * P
                for c in range(2):
                    kc = KS + h // 4 * 1024 + c * 512
                    last = e.matmul(S[u % 2][:, c * 512:(c + 1) * 512], R[b:b + 32, qc:qc + P],
                                    R[b:b + 32, kc:kc + 512], start=True, stop=True)
                last.then_inc(s_full, 1)

            for a in range(4):
                scores0(0, a)
            pe.wait_ge(vpad_ready, H0)

            def values0(c):
                n, kb = c // NT, c % NT
                h = n % H0
                pe.wait_ge(t_free, T_ATT + c + 1)
                if n == H0 and kb == 0:
                    pe.wait_ge(ot_low, 1)
                v = r(VPAD + kb * 1024 + h * P, P)
                o = PT + c % 3 * 1024
                first, end = h == 0 and kb == 0, h == H0 - 1 and kb == NT - 1
                e.matmul(VB[:, :], v, r(o, 512), start=first, stop=False)
                e.matmul(VB[:, :], v, r(o + 512, 512), start=False, stop=end).then_inc(pv_done, 1)

            for n in range(2 * H0):
                for kb in range(NT):
                    c = n * NT + kb
                    k = T_ATT + c
                    if kb % 2 == 0 and n + 1 < 2 * H0:
                        scores0(n + 1, kb // 2)
                    if kb == 0:
                        pe.wait_ge(probs_ready, 4 * (n + 1))
                    ring(k)
                    for a in range(4):
                        last = e.transpose(T[k % 2][:, a * P:(a + 1) * P], PB[:, n % 2, a, kb * P:(kb + 1) * P], IDENT)
                    last.then_inc(t_full, 1)
                    if c >= 2:
                        values0(c - 2)
            values0(2 * H0 * NT - 2)
            values0(2 * H0 * NT - 1)
            for t in range(NT):
                qg = t // 4
                pe.wait_ge(ot_low, qg + 1)
                pe.wait_ge(split, W0_O)
                if t:
                    pe.wait_ge(w_free, t)
                o = OT + qg * 1024 + t % 4 * P
                mm3(WB[:, :], r(o, P), r(o + 512, P), r(WO0_H, D), r(WO0_L, D), True, True).then_inc(w_full, 1)
                if t:
                    transpose_x(T_LN1 + t - 1, t - 1, NT + t)
            transpose_x(T_LN1 + NT - 1, NT - 1, 2 * NT)

            def project_q(m, wait_w, chunks):
                pe.wait_ge(w_free, wait_w)
                for kt in range(KT):
                    pe.wait_ge(split, chunks + kt + 1)
                    c = kt * 768
                    last = mm3(WB[:, :], xt(0, kt, m % NT * P, P), xt(1, kt, m % NT * P, P), r(W_H + c, 512),
                               r(W_L + c, 512), kt == 0, kt == KT - 1)
                last.then_inc(w_full, 1)

            def project_kv(m, k, bank):
                ring(k)
                for kt in range(KT):
                    c = kt * 768 + 512
                    last = mm3(bank[:, 0:256], xt(0, kt, m % NT * P, P), xt(1, kt, m % NT * P, P), r(W_H + c, 256),
                               r(W_L + c, 256), kt == 0, kt == KT - 1)
                last.then_inc(t_full, 1)

            def transpose_qk(count, kq, kk, bq, bk):
                pe.wait_ge(qk_ready, count)
                ring(kq)
                for a in range(4):
                    last = e.transpose(bq[:, a * P:(a + 1) * P], QN[:, a * HD:(a + 1) * HD], IDENT)
                last.then_inc(t_full, 1)
                ring(kk)
                e.transpose(bk[:, 0:P], QN[:, 4 * HD:5 * HD], IDENT).then_inc(t_full, 1)

            def scores1(m, a, L, wait_s, wait_t, bank):
                if a == 0:
                    pe.wait_ge(t_free, wait_t)
                if wait_s is not None:
                    pe.wait_ge(s_free, wait_s)
                q = QT + m % 2 * 1024 + a * P
                for c in range(0, L, 512):
                    w = min(512, max(256, L - c))
                    last = mm3(bank[:, c:c + w], r(q, P), r(q + 512, P), r(KTR + c, w), r(KTR + TOK + c, w), True, True)
                last.then_inc(s_full, 1)

            pe.wait_ge(t_free, T_LN1 + NT)
            for m in range(2):
                project_q(m, NT + m, QL1)
                k = T_PRO + 3 * m
                project_kv(m, k, T[k % 2])
                transpose_qk(m + 1, k + 1, k + 2, T[(k + 1) % 2], T[k % 2])
            for a in range(4):
                if a < 2:
                    pe.wait_ge(exp_done, EX_PRO)
                scores1(0, a, P, a - 1 if a >= 2 else None, T_BASE, S[a % 2])

            def values1(g, i, kb):
                known = 8 * g + i if isinstance(g, int) else i
                pe.wait_ge(t_free, at(g, i, ("T", kb)) + 1)
                if kb == 0:
                    pe.wait_ge(ot_low, g * 8 + i + 2)
                if kb == i % NT:
                    pe.wait_ge(v_split, g * 8 + i + 1)
                o = PT + AT[i, ("PV", kb)] % 3 * 1024
                mm3(VB[:, :], r(VN + kb * P, P), r(VN + TOK + kb * P, P), r(o, 512), r(o + 512, 512),
                    kb == 0, kb == i % NT).then_inc(pv_done, 1)

            def output1(g, count_ot, wait_w, m, first):
                pe.wait_ge(ot_low, count_ot)
                pe.wait_ge(w_free, wait_w)
                for a in range(GRP):
                    if first:
                        pe.wait_ge(split, g * 8 + (QL1 + 5 + a))
                    o = OT + m % 2 * 1024 + a * P
                    w = WOUT + a * 512
                    last = mm3(WB[:, :], r(o, P), r(o + 512, P), r(W_H + w, 512), r(W_L + w, 512), a == 0, a == 3)
                last.then_inc(w_full, 1)

            def slot(g, i):
                known = 8 * g + i if isinstance(g, int) else i
                L = (i + 1) % NT * P + P
                started = False
                for it in slot_items(known):
                    if it[0] == "S":
                        prev = T_BASE if known == 0 and isinstance(g, int) else at(g, i - 1, "KT") + 1
                        u = at(g, i, it)
                        scores1(i + 1, it[1], L, u - (1 + S_PRO), prev, S[AT[known, it] % 2])
                    elif it[0] == "T":
                        kb = it[1]
                        k = at(g, i, it)
                        if not started:
                            pe.wait_ge(probs_ready, (g * 8 + i) * 4 + EX_BASE)
                            started = True
                        ring(k)
                        bank = T[AT[known, it] % 2]
                        for a in range(4):
                            last = e.transpose(bank[:, a * P:(a + 1) * P], PB[:, i % 2, a, kb * P:(kb + 1) * P], IDENT)
                        last.then_inc(t_full, 1)
                        if kb >= 2:
                            values1(g, i, kb - 2)
                    elif it == "WO":
                        output1(g if i <= NT else g, g * 8 + i + 2, at(g, i, "WO"), i - 1, i == 1)
                    elif it == "PQ":
                        project_q(i + 2, at(g, i, "PQ"), (g + (i + 2) // 8) * 8 + QL1)
                    elif it == "PKV":
                        project_kv(i + 2, at(g, i, "PKV"), T[AT[known, "PKV"] % 2])
                    elif it == "QK":
                        transpose_qk(g * 8 + i + 3, at(g, i, "QT"), at(g, i, "KT"),
                                     T[AT[known, "QT"] % 2], T[AT[known, "KT"] % 2])
                    elif it == "E":
                        for kb in range(max(0, i % NT - 1), i % NT + 1):
                            values1(g, i, kb)

            slots(pe, [], slot)
            output1(HKV - 1, STEPS + 2, W_END - 1, STEPS - 1, False)

            def product_xla(tg):
                k = T_END + tg * (FT + 1)
                ring(k)
                for kt in range(KT):
                    last = mm3(T[k % 2][:, :], r(LA_H + kt * P, P), r(LA_L + kt * P, P), xt(0, kt, tg * 512, 512),
                               xt(1, kt, tg * 512, 512), kt == 0, kt == KT - 1)
                last.then_inc(t_full, 1)

            pe.wait_ge(split, QFF + FF_LA)
            product_xla(0)
            for tg in range(2):
                k = T_END + tg * (FT + 1)

                def up(j):
                    u, kk = tg * FT + j, k + 1 + j
                    if u < 2:
                        pe.wait_ge(split, QFF + FF_W[u])
                    else:
                        pe.wait_ge(fw_split, u - 1)
                    ring(kk)
                    w = FW[u % 3]
                    for kt in range(KT):
                        mm3(T[kk % 2][:, :], r(w + kt * P, P), r(w + 1024 + kt * P, P), xt(0, kt, tg * 512, 512),
                            xt(1, kt, tg * 512, 512), kt == 0, False)
                    if j == 0:
                        pe.wait_ge(t_free, k + 1)
                        pe.wait_ge(split, QFF + FF_LB)
                    mm3(T[kk % 2][:, :], r(LB_H + j * P, P, RANK1), r(LB_L + j * P, P, RANK1), r(XLA, 512, RANK1),
                        r(XLA + 512, 512, RANK1), False, True).then_inc(t_full, 1)

                def down(j):
                    u, kk = tg * FT + j, k + 1 + j
                    pe.wait_ge(t_free, kk + 1)
                    if tg and j == 0:
                        pe.wait_ge(y_ready, NT + 4)
                        pe.wait_ge(z_low, 1)
                    if not tg and j == 0:
                        pe.wait_ge(ot_low, STEPS + 2)
                        pe.wait_ge(s_free, S_END - S_PRO)
                        pe.wait_ge(split, QFF + FF_DLA)
                    o, w = X2 + u % 2 * 1024, FW[u % 3]
                    for tt in range(4):
                        mm3(S[tt // 2][:, tt % 2 * D:(tt % 2 + 1) * D], r(o + tt * P, P), r(o + 512 + tt * P, P),
                            r(w + 512, D), r(w + 1536, D), j == 0, False)
                    mm3(VB[:, :], r(DLA_H + j * P, P), r(DLA_L + j * P, P), r(o, 512), r(o + 512, 512),
                        j == 0, j == FT - 1).then_inc(x2_ready, 1)

                up(0)
                for j in range(FT):
                    if j + 1 < FT:
                        up(j + 1)
                    down(j)
                if tg == 0:
                    product_xla(1)
                pe.wait_ge(split, QFF + FF_DLB)
                pe.wait_ge(z_low, tg + 1)
                for tt in range(4):
                    mm3(S[tt // 2][:, tt % 2 * D:(tt % 2 + 1) * D], r(ZT + tt * P, P, RANK1),
                        r(ZT + 512 + tt * P, P, RANK1), r(DLB_H, D, RANK1), r(DLB_L, D, RANK1), False, True)\
                        .then_inc(d_full, 1)


def kernel(**inputs):
    import concourse.bacc as bacc
    from concourse.bass_utils import run_bass_kernel_spmd

    a = {k: np.asarray(v) for k, v in inputs.items()}

    def tiles(w):
        k = w.shape[0] // P
        return w.reshape(k, P, -1).transpose(1, 0, 2).reshape(P, -1)

    qk = a["L0_attn_Wqk_w"].reshape(H0, E0, 2, D)
    bqk = a["L0_attn_Wqk_b"].reshape(H0, E0, 2)
    stacked, bias = [], []
    for w in range(2):
        q = np.broadcast_to(qk[:, None, :, w, :], (H0, 4, E0, D)).reshape(2 * P, D)
        stacked.append(q)
        bias.append(np.broadcast_to(bqk[:, None, :, w], (H0, 4, E0)).reshape(2, P))
    w_qk = np.concatenate(stacked).T
    w_var = np.concatenate([a["L0_attn_Wv_w"], a["L0_ffn_A"].reshape(NEXP * RANK0, D), a["L0_ffn_W_router"]])
    w_var = np.pad(w_var, ((0, NVAR - len(w_var)), (0, 0))).T
    w_exp = a["L0_ffn_B"].transpose(0, 2, 1).reshape(P, D)
    w_o = np.broadcast_to(a["L0_attn_Wo_w"].T.reshape(H0, 1, E0, D), (H0, 2, E0, D)).reshape(P, D)
    w0 = np.concatenate([tiles(w_qk), tiles(w_var), tiles(a["L0_ffn_W_base"].T), w_exp, w_o], 1)

    wq = a["L1_attn_Wq"].reshape(HKV, GRP * HD, D)
    wk = a["L1_attn_Wk"].reshape(HKV, HD, D)
    wv = a["L1_attn_Wv"].reshape(HKV, HD, D)
    wo = a["L1_attn_Wo"].T.reshape(HKV, GRP * HD, D)
    w1 = np.concatenate([np.concatenate([tiles(np.concatenate([wq[g], wk[g], wv[g]]).T), tiles(wo[g])], 1)
                         for g in range(HKV)])

    pad = FT * P - FF

    def ff_layout(up, down):
        up = np.pad(up.reshape(FF, D), ((0, pad), (0, 0))).reshape(FT, P, KT, P).transpose(3, 0, 2, 1)
        down = np.pad(down.reshape(D, FF), ((0, 0), (0, pad))).reshape(D, FT, P).transpose(2, 1, 0)
        both = np.concatenate([up.reshape(P, FT, D), down], 2).reshape(P, NDQ, DQN)
        return both.transpose(1, 0, 2).reshape(NDQ * P, DQN)

    codes = ff_layout(a["L1_ffn_w_up_codes"], a["L1_ffn_w_down_codes"])
    absmax = ff_layout(np.repeat(a["L1_ffn_w_up_absmax"], 64), np.repeat(a["L1_ffn_w_down_absmax"], 64))

    def wide(w):
        return np.pad(w, ((0, 0), (0, P - w.shape[1])))

    def tall(w):
        return np.pad(w, ((0, P - w.shape[0]), (0, 0)))

    lora = np.concatenate([
        tiles(wide(a["L1_ffn_w_up_lora_a"])), tall(np.pad(a["L1_ffn_w_up_lora_b"], ((0, 0), (0, pad)))),
        tiles(wide(np.pad(a["L1_ffn_w_down_lora_a"], ((0, pad), (0, 0))))), tall(a["L1_ffn_w_down_lora_b"])], 1)

    p = np.arange(P)
    e = np.arange(NEXP)
    tri = np.broadcast_to((e[None, :] < e[:, None]).reshape(1, -1), (P, NEXP * NEXP))
    copy = p % 32 // E0
    low_q, low_k = copy >= 2, copy % 2 == 1
    masks = np.stack([1 - 2 * low_q, low_q, 1 - 2 * low_k, low_k], 1)
    heads = HKV * GRP
    start = 2 ** (-2 ** (-(math.log2(heads) - 3)))
    slopes = np.array([start * start ** i for i in range(heads)], np.float32)
    inverse = np.concatenate([(1.0 / slopes.astype(np.float64)).reshape(HKV, GRP), np.ones((HKV, 1))], 1)
    consts = np.concatenate([
        np.eye(P), tri, masks, np.stack([*bias[0], *bias[1]], 1),
        np.stack([a["L1_attn_q_norm_w"], a["L1_attn_k_norm_w"]], 1),
        np.pad(a["L1_ffn_b_up"], (0, pad)).reshape(FT, P).T,
        np.broadcast_to(slopes, (P, heads)), np.broadcast_to(inverse.reshape(1, -1), (P, HKV * 5)),
        np.broadcast_to([-0.5] * 5 + [-1.0] * 4, (P, 9)), np.broadcast_to(a["L1_ffn_b_down"], (P, D)),
    ], 1).astype(np.float32)
    rows = np.broadcast_to(np.concatenate([a["L0_attn_Wv_b"], a["L0_attn_Wo_b"], a["L0_ffn_b_base"]]), (P, NROWS))
    gap = np.arange(TOK)[None, :] - (TOK - P) - p[:, None]
    rel = np.where(gap > 0, -1e33, gap).astype(np.float32)

    nc = bacc.Bacc("TRN2", target_bir_lowering=False, num_devices=1)
    arrays = {"x": a["L0_attn_x"].reshape(TOK, D), "w0": w0, "w1": w1, "codes": codes, "absmax": absmax, "lora": lora,
              "consts": consts, "rows": rows, "rel": rel}
    arrays = {k: np.ascontiguousarray(v) for k, v in arrays.items()}
    args = [nc.dram_tensor(k, v.shape, mybir.dt.from_np(v.dtype), kind="ExternalInput").ap() for k, v in arrays.items()]
    out = nc.dram_tensor("out", (TOK, D), F32, kind="ExternalOutput").ap()
    program(nc, *args, out)
    res = run_bass_kernel_spmd(nc, [arrays], core_ids=[0])
    return res.results[0]["out"].reshape(1, TOK, D)
```

```python
import math
import numpy as np
import concourse.bass as bass
from concourse import mybir
from contextlib import ExitStack

F32 = mybir.dt.float32
F32R = mybir.dt.float32r
I32 = mybir.dt.int32
ALU = mybir.AluOpType
ACT = mybir.ActivationFunctionType
AX = mybir.AxisListType

P = 128
TOK, D = 1024, 512
NT, KT = TOK // P, D // P
H0, E0 = 8, 8
NEXP, RANK0 = 8, 16
HKV, GRP, HD = 8, 4, 128
FF, RANK1 = 1376, 16
FT = -(-FF // P)
LN_EPS, RMS_EPS = 1e-5, 1e-6

WQK_H, WQK_L = 0, 2048
WBASE_H, WBASE_L = 4096, 6144
NVAR = 256
WVAR_H, WVAR_L = 8192, 9216
WEXP_H, WEXP_L = 10240, 10752
WO0_H, WO0_L = 11264, 11776
QS, KS = 12288, 14336
VPAD_AT = (0, 1024, 2048, 3072, 8192, 9216, 4096, 5120)
W_H, W_L = 0, 5120
WOUT = KT * 768
QT = 10240
KTR = 12288
VN = 14336
PT = 16384
OT = 19456
ARENA = 21504
FW = (0, 5120, 2048)
LA_H, LA_L = 7168, 7680
X2 = 8192
LB_H, LB_L = 10240, 11648
DLA_H, DLA_L = 13056, 14464
DLB_H, DLB_L = 15872, 16384
XLA = 16896
ZT = 17920

C_ID = 0
C_TRI = C_ID + P
C_MASK = C_TRI + NEXP * NEXP
C_BQK = C_MASK + 4
C_QKW = C_BQK + 4
C_BUP = C_QKW + 2
C_SLOPE = C_BUP + FT
C_ISL = C_SLOPE + HKV * GRP
C_EXP = C_ISL + HKV * 5
NCONST = C_EXP + 9
R_BV, R_BO, R_BB = 0, 64, 64 + D
NROWS = 64 + 2 * D

NF4 = [-1.0, -0.6961928009986877, -0.5250730514526367, -0.39491748809814453, -0.28444138169288635,
       -0.18477343022823334, -0.09105003625154495, 0.0, 0.07958029955625534, 0.16093020141124725,
       0.24611230194568634, 0.33791524171829224, 0.44070982933044434, 0.5626170039176941,
       0.7229568362236023, 1.0]
LINES = [(NF4[2 * k + 1] - NF4[2 * k], NF4[2 * k] - 2 * k * (NF4[2 * k + 1] - NF4[2 * k])) for k in range(8)]
DQN = 704
NDQ = FT * 1024 // DQN

RAWC = 768


def _cut(src, hi, lo, n, step):
    return [(src + a, hi + a, lo + a, min(step, n - a)) for a in range(0, n, step)]


L0_CHUNKS = (_cut(0, WQK_H, WQK_L, 2048, RAWC) + _cut(2048, WVAR_H, WVAR_L, KT * NVAR, 512)
             + _cut(3072, WBASE_H, WBASE_L, 2048, RAWC) + _cut(5120, WEXP_H, WEXP_L, 512, 512)
             + _cut(5632, WO0_H, WO0_L, 512, 512))
W0_QK, W0_VAR, W0_BASE, W0_EXP, W0_O = 3, 5, 8, 9, 10
NL0 = len(L0_CHUNKS)
QL1 = NL0
QFF = QL1 + 8 * HKV
FF_CHUNKS = ([(True, 0, LA_H, LA_L, 512, P)]
             + [(False, u * 1024 + a, FW[u] + a, FW[u] + 1024 + a, 512, P) for u in (0, 1) for a in (0, 512)]
             + [(True, 512 + a, LB_H + a, LB_L + a, 704, RANK1) for a in (0, 704)]
             + [(True, 1920 + a, DLA_H + a, DLA_L + a, 704, P) for a in (0, 704)]
             + [(True, 3328, DLB_H, DLB_L, 512, RANK1 + 1)])
FF_LA, FF_W, FF_LB, FF_DLA, FF_DLB = 1, (3, 5), 7, 9, 10
FF_EARLY = 7
NFFC = len(FF_CHUNKS)

SCORE_AT = {0: 0, 1: 1, 2: 2, 4: 3}
EXP_AT = {0: 0, 2: 1, 3: 2, 5: 3}

STEPS = NT * HKV
HIGH_AT = {2: 0, 3: 1, 6: 2, 7: 3}
LOW_AT = {4: 0, 5: 1, 7: 2, 8: 3}
T_WITH = {1: (0, 0, 0, 1), 2: (0, 1, 0, 1), 3: (1, 0, 1, 1), 4: (1, 1, 0, 2), 5: (1, 1, 0, 3), 6: (1, 2, 1, 2),
          7: (1, 2, 1, 3), 8: (2, 2, 1, 3)}


def slot_items(n):
    i = n % NT
    nk = i + 1
    cuts = [sum(T_WITH[nk][:a]) for a in range(5)]
    s1, s2 = n + 1 < STEPS, n + 2 < STEPS
    seq = []

    def put(*names, when=True):
        if when:
            seq.extend(names)

    put("V")
    for a in range(4):
        if a == 3:
            put("WO", when=i != 0)
        if a == 0:
            put("PQ", when=s2)
        put(("S", a), when=s1)
        if a == 0:
            put("PKV", when=s2)
            put("WO", when=n > 0 and i == 0)
        if a > 0:
            put(("NR", a - 1), when=s1)
        put(*[("T", kb) for kb in range(cuts[a], cuts[a + 1])])
        if a == 2 and nk <= 4:
            put("QN", when=s2)
        put(("EX", a), when=s1)
        put(("CH", a + 3), when=i == 0 and a > 0)
        put(("CH", a), when=n < STEPS - NT and i == 5)
        if n >= STEPS - 2:
            put(("FC", a + 4 * (i - 6)), when=a + 4 * (i - 6) < FF_EARLY)
        if a == 1 and nk > 4:
            put("QN", when=s2)
        if a == (1 if nk > 4 else 3):
            put("DA")
    put("QK", when=s2)
    put(("CH", 7), when=i == 0)
    put(("NR", 3), when=s1)
    put("DB", "E")
    return seq


T_LN0, T_QK, T_VAR, T_HW, T_ATT = 0, 8, 16, 24, 32
T_LN1 = T_ATT + 2 * H0 * NT
T_PRO = T_LN1 + NT
T_BASE = T_PRO + 6
S_ATT, S_PRO = NT, NT + 2 * H0 * 4
S_BASE = S_PRO + 4
W_PRO = NT
W_BASE = W_PRO + 2
PV_BASE = 2 * H0 * NT
OT_BASE = 2
EX_PRO = 2 * H0 * 4
EX_BASE = EX_PRO + 4
P_PER, V_PER = 56, 3


def _tables():
    t, s, w, pv = T_BASE, S_BASE, W_BASE, PV_BASE
    at = {}
    for n in range(STEPS):
        for x in slot_items(n):
            if x in ("PKV", "WO") or x[0] == "T":
                at[n, x] = t
                t += 1
            elif x == "QK":
                at[n, "QT"], at[n, "KT"] = t, t + 1
                t += 2
            elif x[0] == "S":
                at[n, x] = s
                s += 1
            elif x == "PQ":
                at[n, x] = w
                w += 1
        at[n, "last"] = t - 1
        for kb in range(n % NT + 1):
            at[n, ("PV", kb)] = pv
            pv += 1
    return at, t, s, w, pv


AT, T_LAST, S_END, W_END, PV_END = _tables()
T_END = T_LAST + 1
T_PER = AT[9, "PKV"] - AT[1, "PKV"]


def w1_place(c):
    return (c * 768, 768) if c < 4 else (WOUT + (c - 4) * 512, 512)


def at(g, i, name):
    if isinstance(g, int):
        return AT[8 * g + i, name]
    return g * (AT[8 + i, name] - AT[i, name]) + AT[i, name]


def hold(eng, sem, value, passed):
    eng.wait_ge(sem, value)
    if not isinstance(value, int):
        eng.sem_inc(passed, 1)


class Tally:

    def __init__(self, eng, sem, passed):
        self.eng, self.sem, self.passed, self.base, self.n = eng, sem, passed, 0, 0

    def done(self, ins):
        ins.then_inc(self.sem, 1)
        self.n += 1

    def settle(self):
        hold(self.eng, self.sem, self.base + self.n, self.passed)

    def link(self, ins):
        self.done(ins)
        self.settle()


def slots(eng, tallies, slot):
    slot(0, 0)
    start = [t.n for t in tallies]
    probe = []
    with eng.Fori(0, HKV - 1) as g:
        for t in tallies:
            t.n = 0
            t.base = t.per * g + start[tallies.index(t)]
        for i in range(1, NT + 1):
            slot(g, i)
        for t in tallies:
            assert t.n == t.per, (t.n, t.per)
            probe.append(t.n)
    for t, s in zip(tallies, start):
        t.base, t.n = 0, s + (HKV - 1) * t.per
    for i in range(1, NT):
        slot(HKV - 1, i)


def program(nc, x, w0, w1, codes, absmax, lora, consts, rows, rel, out):
    with ExitStack() as ctx:
        def sb(name, shape, dt=F32):
            return ctx.enter_context(nc.sbuf_tensor(name, shape, dt))

        def sem(name):
            return ctx.enter_context(nc.semaphore(name))

        x1_dram = nc.dram_tensor("x1_scratch", (TOK, D), F32, kind="Internal").ap()
        wd_dram = nc.dram_tensor("dequantised", (P, FT * 1024), F32, kind="Internal").ap()

        XT = sb("XT", [P, 2, KT, TOK], F32R)
        R = sb("R", [P, ARENA], F32R)
        G = sb("G", [P, NT * D])
        PB = sb("PB", [P, 2, 4, TOK])
        REL = sb("REL", [P, TOK])
        RAW = sb("RAW", [P, 2, RAWC])
        QN = sb("QN", [P, 5 * HD])
        VS = sb("VS", [P, 4, HD])
        DQ = sb("DQ", [P, 4, DQN])
        C = sb("C", [P, NCONST])
        JUNK = sb("JUNK", [P, 10, HD], mybir.dt.bfloat16)
        NM = sb("NM", [P, 8])
        SM = sb("SM", [P, 8])
        RI = sb("RI", [P, 8])
        SQ = sb("SQ", [P, 2, 5])
        SQB = sb("SQB", [P, 2, 5])
        SQC = sb("SQC", [P, 2, 5])
        INV = sb("INV", [P, 2, 5])
        SLC = sb("SLC", [P, 4])
        QKW = sb("QKW", [P, 2])
        ST = sb("ST", [P, 2, 6])
        MV = sb("MV", [P, 2, 2])
        VE = sb("VE", [P, 2])
        RSTD = sb("RSTD", [P, 2])
        CMP = sb("CMP", [P, 2, 512])
        RT = sb("RT", [P, 8, 64])

        LA = DQ[:, :, :].rearrange("p a n -> p (a n)")
        HN = LA[:, 0:1024]
        VN0 = LA[:, 1024:1536]
        ROWS = LA[:, 1536:1536 + NROWS]
        PBF = PB[:, :, :, :].rearrange("p a b n -> p (a b n)")
        XS = [PBF[:, t * D:(t + 1) * D] for t in range(4)]
        XN = [PBF[:, (4 + t) * D:(5 + t) * D] for t in range(4)]
        TMP = [PBF[:, (8 + t) * D:(9 + t) * D] for t in range(6)]
        CODES = DQ[:, 0, :].bitcast(I32)
        Y_AT = (6, 7, 14, 15)
        IDENT = C[:, C_ID:C_ID + P]

        S = [ctx.enter_context(nc.psum_tensor(f"S{k}", [P, 1024], F32)) for k in range(2)]
        T = [ctx.enter_context(nc.psum_tensor(f"T{k}", [P, 512], F32)) for k in range(2)]
        VB = ctx.enter_context(nc.psum_tensor("VB", [P, 512], F32))
        WB = ctx.enter_context(nc.psum_tensor("WB", [P, 512], F32))

        in_const = sem("in_const")
        in_rows = sem("in_rows")
        in_x = [sem(f"in_x{k}") for k in range(4)]
        in_raw = [sem(f"in_raw{k}") for k in range(2)]
        in_codes = sem("in_codes")
        in_absmax = sem("in_absmax")
        in_fw = [sem(f"in_fw{k}") for k in range(2)]
        in_x1 = [sem(f"in_x1{k}") for k in range(4)]
        out_x1 = [sem(f"out_x1{k}") for k in range(4)]
        out_dq = sem("out_dq")
        out_y = [sem(f"out_y{k}") for k in range(4)]
        t_full = sem("t_full")
        t_act = sem("t_act")
        t_free = sem("t_free")
        s_full = sem("s_full")
        s_free = sem("s_free")
        w_full = sem("w_full")
        w_free = sem("w_free")
        pv_done = sem("pv_done")
        ot_high = sem("ot_high")
        ot_low = sem("ot_low")
        max_ready = sem("max_ready")
        exp_done = sem("exp_done")
        probs_ready = sem("probs_ready")
        w_high = sem("w_high")
        split = sem("split")
        vpad_ready = sem("vpad_ready")
        v_split = sem("v_split")
        squares = sem("squares")
        inv_ready = sem("inv_ready")
        qk_ready = sem("qk_ready")
        var_ready = sem("var_ready")
        rstd_ready = sem("rstd_ready")
        xn_ready = sem("xn_ready")
        tmp_ready = sem("tmp_ready")
        x1_ready = sem("x1_ready")
        row_ready = sem("row_ready")
        row_exp = sem("row_exp")
        hw_ready = sem("hw_ready")
        y_ready = sem("y_ready")
        y_tanh = sem("y_tanh")
        gate_done = sem("gate_done")
        line = sem("line")
        line_used = sem("line_used")
        dq_selected = sem("dq_selected")
        dq_scaled = sem("dq_scaled")
        fw_high = sem("fw_high")
        fw_split = sem("fw_split")
        x2_ready = sem("x2_ready")
        z_ones = sem("z_ones")
        z_high = sem("z_high")
        z_low = sem("z_low")
        d_full = sem("d_full")
        d_free = sem("d_free")
        y_scaled = sem("y_scaled")
        out_done = sem("out_done")
        v_chain = sem("v_chain")
        p_chain = sem("p_chain")
        v_passed = sem("v_passed")
        p_passed = sem("p_passed")

        block = ctx.enter_context(nc.Block())

        def y_psum(tt):
            return S[tt // 2][:, tt % 2 * D:(tt % 2 + 1) * D]

        def y_bank(t):
            return S[t // 2 % 2][:, t % 2 * 512:(t % 2 + 1) * 512]

        def r(off, n, p=P):
            return R[0:p, off:off + n]

        def rf(off, n, p=P):
            return R[0:p, off:off + n].bitcast(F32)

        @block.sync
        def _(sp):
            sp.dma_start(C[:, :], consts).then_inc(in_const, 16)
            for t in range(4):
                sp.dma_start(XS[t], x[t * P:(t + 1) * P, :]).then_inc(in_x[t], 16)

            def raw(q, src, rows_=P):
                if q >= 2:
                    sp.wait_ge(split, q - 1)
                n = src.shape[-1]
                sp.dma_start(RAW[0:rows_, q % 2, 0:n], src).then_inc(in_raw[q % 2], 16)

            for q in range(2):
                src, _, _, n = L0_CHUNKS[q]
                raw(q, w0[:, src:src + n])
            sp.dma_start(ROWS, rows).then_inc(in_rows, 16)
            for t in range(4, NT):
                sp.wait_ge(xn_ready, t - 3)
                sp.dma_start(XS[t % 4], x[t * P:(t + 1) * P, :]).then_inc(in_x[t % 4], 16)
                if t >= 5:
                    src, _, _, n = L0_CHUNKS[t - 3]
                    raw(t - 3, w0[:, src:src + n])
            for q in range(5, NL0):
                src, _, _, n = L0_CHUNKS[q]
                raw(q, w0[:, src:src + n])
            sp.dma_start(REL[:, :], rel).then_inc(out_dq, 16)

            def w1_chunk(g, c):
                q = QL1 + c
                a, n = w1_place(c)
                if isinstance(g, int):
                    raw(q + 8 * g, w1[g * P:(g + 1) * P, a:a + n])
                else:
                    sp.wait_ge(split, g * 8 + q - 1)
                    sp.dma_start(RAW[:, q % 2, 0:n], w1[bass.ds(g * P, P), a:a + n]).then_inc(in_raw[q % 2], 16)

            sp.wait_ge(t_full, T_ATT + (2 * H0 - 1) * NT)
            for t in range(4):
                sp.dma_start(XS[t], x[t * P:(t + 1) * P, :]).then_inc(in_x[t], 16)
            w1_chunk(0, 0)
            w1_chunk(0, 1)
            for t in range(NT):
                sp.wait_ge(x1_ready, t + 1)
                sp.dma_start(x1_dram[t * P:(t + 1) * P, :], XS[t % 4]).then_inc(out_x1[t % 4], 16)
                if t + 4 < NT:
                    sp.wait_ge(xn_ready, NT + t + 1)
                    sp.wait_ge(out_x1[t % 4], 16)
                    sp.dma_start(XS[t % 4], x[(t + 4) * P:(t + 5) * P, :]).then_inc(in_x[t % 4], 16)
                if t in (4, 5):
                    w1_chunk(0, t - 2)

            for c in (4, 5):
                w1_chunk(0, c)

            def ff_chunk(q):
                lowrank, src, _, _, n, np_ = FF_CHUNKS[q]
                raw(QFF + q, (lora if lowrank else wd_dram)[0:np_, src:src + n], np_)

            def load_codes(g, i):
                if isinstance(g, int):
                    cc = (8 * g + i) // 4
                    if cc:
                        sp.wait_ge(dq_selected, cc)
                    else:
                        sp.wait_ge(xn_ready, 2 * NT)
                        sp.wait_ge(t_free, T_LN1 + NT)
                    sp.dma_start(CODES, codes[cc * P:(cc + 1) * P, :]).then_inc(in_codes, 16)
                else:
                    sp.wait_ge(dq_selected, g * 2 + i // 4)
                    sp.dma_start(CODES, codes[bass.ds(g * (2 * P) + i // 4 * P, P), :]).then_inc(in_codes, 16)

            def slot(g, i):
                jj = i % 4
                if jj == 0:
                    load_codes(g, i)
                if isinstance(g, int) and g == i == 0:
                    w1_chunk(0, 6)
                    w1_chunk(0, 7)
                if not (isinstance(g, int) and g == HKV - 1):
                    if i == 2:
                        w1_chunk(g + 1, 0)
                        w1_chunk(g + 1, 1)
                    if i == 5:
                        w1_chunk(g + 1, 2)
                        w1_chunk(g + 1, 3)
                    if i == 6:
                        w1_chunk(g + 1, 4)
                        w1_chunk(g + 1, 5)
                    if i == 8:
                        w1_chunk(g + 1, 6)
                        w1_chunk(g + 1, 7)
                elif i >= 5:
                    if i == 5:
                        sp.wait_ge(out_dq, 16 * (2 * 1024 // DQN + 2))
                    for q in {5: (0, 1), 6: (2, 3, 4), 7: (5, 6)}[i]:
                        ff_chunk(q)
                if jj == 0 and not (isinstance(g, int) and 8 * g + i == 0):
                    sp.wait_ge(dq_scaled, g * 2 + (i // 4 + 1))
                    sp.dma_start(wd_dram[:, bass.ds(g * (2 * DQN) + (i // 4 - 1) * DQN, DQN)], DQ[:, 1, :])\
                        .then_inc(out_dq, 16)
                if jj == 3:
                    sp.wait_ge(dq_selected, g * 2 + i // 4 + 1)
                    sp.dma_start(DQ[:, 3, :], absmax[bass.ds(g * (2 * P) + i // 4 * P, P), :]).then_inc(in_absmax, 16)

            slots(sp, [], slot)
            for q in range(FF_EARLY, NFFC - 1):
                ff_chunk(q)
            sp.wait_ge(dq_scaled, NDQ + 1)
            sp.dma_start(wd_dram[:, (NDQ - 1) * DQN:NDQ * DQN], DQ[:, 1, :]).then_inc(out_dq, 16)
            ff_chunk(NFFC - 1)
            sp.wait_ge(out_dq, 16 * (NDQ + 1))
            sp.wait_ge(t_full, AT[STEPS - 1, "last"] + 1)
            for u in range(2, 2 * FT):
                if u >= 4:
                    sp.wait_ge(fw_split, u - 3)
                sp.dma_start(PBF[:, u % 2 * 1024:(u % 2 + 1) * 1024],
                             wd_dram[:, u % FT * 1024:(u % FT + 1) * 1024]).then_inc(in_fw[u % 2], 16)
                if u in (2, FT + 8):
                    for tt in range(4):
                        t = u // FT * 4 + tt
                        if t >= 4:
                            sp.wait_ge(out_y[tt], 16)
                        sp.dma_start(PBF[:, (8 + tt) * D:(9 + tt) * D], x1_dram[t * P:(t + 1) * P, :])\
                            .then_inc(in_x1[tt], 16)
                if u == FT + 6 or u == 2 * FT - 1:
                    for tt in range(4):
                        t = u // (2 * FT - 1) * 4 + tt
                        sp.wait_ge(out_done, t + 1)
                        sp.dma_start(out[t * P:(t + 1) * P, :], PBF[:, (8 + tt) * D:(9 + tt) * D])\
                            .then_inc(out_y[tt], 16)
            for tt in range(4):
                sp.wait_ge(out_y[tt], 32)

        @block.gpsimd
        def _(pool):
            e = nc.gpsimd
            ch = Tally(pool, p_chain, p_passed)
            ch.per = P_PER

            def low_half(q, hi, lo, n, np_=P):
                hold(pool, w_high, q + 1, p_passed)
                e.tensor_tensor(r(lo, n, np_), RAW[0:np_, q % 2, 0:n], rf(hi, n, np_), ALU.subtract).then_inc(split, 1)

            def rstd(t):
                k = t % 2
                hold(pool, var_ready, t + 1, p_passed)
                ch.link(e.tensor_scalar(VE[:, k:k + 1], MV[:, k, 1:2], 1.0, LN_EPS, ALU.mult, ALU.add))
                e.tensor_tensor(RSTD[:, k:k + 1], VE[:, k:k + 1], C[:, C_EXP:C_EXP + 1], ALU.pow).then_inc(rstd_ready, 1)

            def divide(m, a, L, count, scale):
                k = m % 2 * 4 + a
                hold(pool, exp_done, count, p_passed)
                ch.link(e.tensor_tensor(RI[:, k:k + 1], SM[:, k:k + 1], C[:, C_EXP + 5:C_EXP + 6], ALU.pow))
                e.tensor_scalar(PB[:, m % 2, a, 0:L], PB[:, m % 2, a, 0:L], RI[:, k:k + 1], scale,
                                ALU.mult, ALU.mult).then_inc(probs_ready, 1)

            def inverse_rms(g, m, count):
                k = m % 2
                hold(pool, squares, count, p_passed)
                ch.link(e.tensor_scalar(SQB[:, k, :], SQ[:, k, :], 1.0 / HD, RMS_EPS, ALU.mult, ALU.add))
                ch.link(e.tensor_tensor(SQC[:, k, :], SQB[:, k, :], C[:, C_EXP:C_EXP + 5], ALU.pow))
                e.tensor_tensor(INV[:, k, :], SQC[:, k, :], C[:, bass.ds(g * 5 + C_ISL, 5)], ALU.mult)\
                    .then_inc(inv_ready, 1)

            hold(pool, in_const, 16, p_passed)
            rstd(0)
            rstd(1)
            rstd(2)
            for q in range(NL0):
                src, hi, lo, n = L0_CHUNKS[q]
                low_half(q, hi, lo, n)
                if 3 + q < NT:
                    rstd(3 + q)
            src = VN0.rearrange("p (b h e) -> p b h e", b=NT, h=H0)

            def pad_values(b, nb):
                whole = r(VPAD_AT[b], nb * 1024).rearrange("p (b n) -> p b n", b=nb)
                for h in range(H0):
                    o = h * P + 2 * E0 * h
                    hi_ap, lo_ap = whole[:, :, o:o + E0], whole[:, :, o + E0:o + 2 * E0]
                    ch.link(e.tensor_copy(hi_ap, src[:, b:b + nb, h, :]))
                    e.tensor_tensor(lo_ap, src[:, b:b + nb, h, :], hi_ap.bitcast(F32), ALU.subtract)\
                        .then_inc(vpad_ready, 1)

            hold(pool, t_full, T_QK + 8, p_passed)
            ch.link(e.memset(rf(VPAD_AT[0], 4096), 0.0))
            hold(pool, t_full, T_VAR + NT, p_passed)
            ch.link(e.memset(rf(VPAD_AT[4], 2048), 0.0))
            hold(pool, t_free, T_VAR + NT, p_passed)
            pad_values(0, 4)
            pad_values(4, 2)
            hold(pool, s_full, NT, p_passed)
            ch.link(e.memset(rf(VPAD_AT[6], 2048), 0.0))
            for n in range(2 * H0):
                for a in range(4):
                    divide(n, a, TOK, n * 4 + a + 1, 1.0 / math.sqrt(H0 * E0))
                if n == 0:
                    pad_values(6, 2)
            def w1_low(c):
                off, n = w1_place(c)
                low_half(QL1 + c, W_H + off, W_L + off, n)

            for t in range(NT + 1):
                if t < NT:
                    hold(pool, tmp_ready, t + 1, p_passed)
                    hold(pool, in_x[t % 4], 16 * (t // 4 + 3), p_passed)
                    e.tensor_tensor(XS[t % 4], XS[t % 4], TMP[t % 4], ALU.add).then_inc(x1_ready, 1)
                if t:
                    rstd(NT + t - 1)
                if t in LOW_AT:
                    w1_low(LOW_AT[t])
            for m in range(2):
                inverse_rms(0, m, 5 * m + 5)
            for a in range(4):
                divide(0, a, P, EX_PRO + a + 1, 1.0)

            def slot(g, i):
                n0 = g * 8 + i
                known = 8 * g + i if isinstance(g, int) else i
                L = (i + 1) % NT * P + P
                for it in slot_items(known if isinstance(g, int) else i):
                    if it == "V":
                        b = i % NT
                        if i < 2:
                            hold(pool, t_act, T_PRO + 3 * i + 1, p_passed)
                        if i >= 2:
                            hold(pool, t_act, at(g, i - 2, "PKV") + 1, p_passed)
                        elif i == 1:
                            hold(pool, t_act, g * T_PER + (AT[NT - 1, "PKV"] - T_PER + 1), p_passed)
                        if i == NT:
                            hold(pool, pv_done, at(g, NT - 1, ("PV", 0)) + 1, p_passed)
                        elif i:
                            hold(pool, pv_done, g * 36 + (AT[NT - 1, ("PV", b)] - 36 + 1), p_passed)
                        k = i % 4
                        ch.link(e.tensor_copy(r(VN + b * P, P), VS[:, k, :]))
                        e.tensor_tensor(r(VN + TOK + b * P, P), VS[:, k, :], rf(VN + b * P, P), ALU.subtract)\
                            .then_inc(v_split, 1)
                    elif it[0] == "NR":
                        a = it[1]
                        divide(i + 1, a, L, n0 * 4 + (EX_BASE + a + 1), 1.0)
                    elif it == "PKV":
                        inverse_rms(g + (i + 2) // 8, i + 2, n0 * 5 + 15)

            slots(pool, [ch], slot)
            hold(pool, t_full, T_END, p_passed)
            def ff_low(q):
                _, _, hi, lo, n, np_ = FF_CHUNKS[q]
                low_half(QFF + q, hi, lo, n, np_)

            for q in range(FF_EARLY, NFFC - 1):
                ff_low(q)
            e.memset(rf(ZT, 512, RANK1 + 1), 1.0).then_inc(z_ones, 1)
            e.memset(rf(ZT + 512, 512, RANK1 + 1), 0.0).then_inc(z_ones, 1)

            def add_x1(u):
                tt = u % 4
                pool.wait_ge(y_scaled, u + 1)
                hold(pool, in_x1[tt], 16 * (u // 4 + 1), p_passed)
                xx = PBF[:, (8 + tt) * D:(9 + tt) * D]
                e.tensor_tensor(xx, xx, PBF[:, Y_AT[tt] * D:(Y_AT[tt] + 1) * D], ALU.add).then_inc(out_done, 1)

            for u in range(2, 2 * FT):
                if u == 4:
                    ff_low(NFFC - 1)
                if FT + 3 <= u < FT + 7:
                    add_x1(u - FT - 3)
                hold(pool, fw_high, u - 1, p_passed)
                k = FW[u % 3]
                src = PBF[:, u % 2 * 1024:(u % 2 + 1) * 1024]
                e.tensor_tensor(r(k + 1024, 1024), src, rf(k, 1024), ALU.subtract).then_inc(fw_split, 1)
            for u in range(4, 8):
                add_x1(u)

        @block.scalar
        def _(act):
            e = nc.scalar
            act.wait_ge(in_const, 16)

            def high_xt(k, t):
                act.wait_ge(t_full, k + 1)
                e.activation(XT[:, 0, :, t * P:(t + 1) * P], T[k % 2][:, :].rearrange("p (k n) -> p k n", k=KT),
                             ACT.Copy).then_inc(t_act, 1)

            def high_half(q, hi, n, np_=P, count=None):
                act.wait_ge(in_raw[q % 2], 16 * (q // 2 + 1) if count is None else count)
                e.activation(r(hi, n, np_), RAW[0:np_, q % 2, 0:n], ACT.Copy).then_inc(w_high, 1)

            for t in range(NT):
                high_xt(T_LN0 + t, t)
                high_half(t, L0_CHUNKS[t][1], L0_CHUNKS[t][3])
            for q in range(NT, NL0):
                high_half(q, L0_CHUNKS[q][1], L0_CHUNKS[q][3])
            for u in range(8):
                blk = u // 2
                k = T_QK + u
                act.wait_ge(t_full, k + 1)
                if u >= 2:
                    act.wait_ge(t_free, k - 1)
                e.activation(TMP[u % 2], T[k % 2][:, :], ACT.Identity, bias=C[:, C_BQK + blk:C_BQK + blk + 1])\
                    .then_inc(t_act, 1)
            for t in range(NT):
                k = T_VAR + t
                act.wait_ge(t_full, k + 1)
                e.activation(HN[:, t * P:(t + 1) * P], T[k % 2][:, 64:192], ACT.Copy).then_inc(t_act, 1)
            act.wait_ge(row_ready, 1)
            e.activation(RT[:, 2, :], RT[:, 1, :], ACT.Exp).then_inc(row_exp, 1)
            for t in range(NT):
                k = T_HW + t
                act.wait_ge(t_full, k + 1)
                if t >= 2:
                    act.wait_ge(s_full, t - 1)
                e.activation(r(OT + t % 2 * 256, P), T[k % 2][:, 0:P], ACT.Copy).then_inc(t_act, 1)
                if t >= 1:
                    act.wait_ge(y_ready, t)
                    if t >= 3:
                        act.wait_ge(gate_done, t - 2)
                    e.activation(TMP[2 + (t - 1) % 2], G[:, (t - 1) * D:t * D], ACT.Tanh, scale=0.5)\
                        .then_inc(y_tanh, 1)
            act.wait_ge(y_ready, NT)
            act.wait_ge(gate_done, NT - 2)
            e.activation(TMP[2 + (NT - 1) % 2], G[:, (NT - 1) * D:NT * D], ACT.Tanh, scale=0.5).then_inc(y_tanh, 1)

            def exp0(n, a):
                u = n * 4 + a
                act.wait_ge(max_ready, u + 1)
                if n >= 2 and a == 0:
                    act.wait_ge(t_full, T_ATT + (n - 1) * NT)
                if u == 4:
                    act.wait_ge(gate_done, NT)
                k = n % 2 * 4 + a
                e.activation(PB[:, n % 2, a, :], S[u % 2][:, :], ACT.Exp, bias=NM[:, k:k + 1],
                             accum_out=SM[:, k:k + 1]).then_inc(exp_done, 1)

            for a in range(4):
                exp0(0, a)
            for n in range(2 * H0):
                for kb in range(NT):
                    c = n * NT + kb
                    k = T_ATT + c
                    act.wait_ge(t_full, k + 1)
                    if c >= 3:
                        act.wait_ge(pv_done, c - 2)
                    e.activation(r(PT + c % 3 * 1024, 512), T[k % 2][:, :], ACT.Copy).then_inc(t_act, 1)
                    if kb in EXP_AT and n + 1 < 2 * H0:
                        exp0(n + 1, EXP_AT[kb])
                if n % H0 == H0 - 1:
                    qg = n // H0
                    act.wait_ge(pv_done, (n + 1) * NT)
                    e.activation(r(OT + qg * 1024, 512), VB[:, :], ACT.Copy).then_inc(ot_high, 1)
            for t in range(NT):
                high_xt(T_LN1 + t, t)
                if t in HIGH_AT:
                    c = HIGH_AT[t]
                    high_half(QL1 + c, W_H + w1_place(c)[0], w1_place(c)[1])

            def sum_squares(m, wcount, k):
                act.wait_ge(w_full, wcount)
                for a in range(4):
                    e.activation(JUNK[:, m % 2 * 5 + a, :], WB[:, a * HD:(a + 1) * HD], ACT.Square,
                                 accum_out=SQ[:, m % 2, a:a + 1]).then_inc(squares, 1)
                return k

            def squares_k(m, tcount, tk):
                act.wait_ge(t_full, tcount)
                e.activation(JUNK[:, m % 2 * 5 + 4, :], tk[:, 0:HD], ACT.Square, accum_out=SQ[:, m % 2, 4:5]).then_inc(squares, 1)
                e.activation(VS[:, m % 4, :], tk[:, HD:2 * HD], ACT.Copy).then_inc(t_act, 1)

            def high_qk(m, tq, tk, bq, bk):
                act.wait_ge(t_full, tq)
                e.activation(r(QT + m % 2 * 1024, 512), bq[:, :], ACT.Copy, scale=QKW[:, 0:1]).then_inc(t_act, 1)
                act.wait_ge(t_full, tk)
                e.activation(r(KTR + m % NT * P, P), bk[:, 0:P], ACT.Copy, scale=QKW[:, 1:2]).then_inc(t_act, 1)

            def exp1(m, a, L, count):
                act.wait_ge(s_free, count)
                k = m % 2 * 4 + a
                e.activation(PB[:, m % 2, a, 0:L], PB[:, m % 2, a, 0:L], ACT.Exp, scale=-1.0, bias=NM[:, k:k + 1],
                             accum_out=SM[:, k:k + 1]).then_inc(exp_done, 1)

            for m in range(2):
                sum_squares(m, W_PRO + m + 1, None)
                k = T_PRO + 3 * m
                squares_k(m, k + 1, T[k % 2])
                high_qk(m, k + 2, k + 3, T[(k + 1) % 2], T[k % 2])
            for a in range(4):
                exp1(0, a, P, a + 1)

            def lines(g, i, part):
                jj = i % 4
                todo = {(1, 0): (0, 1), (1, 1): (2,), (2, 0): (3, 4), (2, 1): (5,), (3, 0): (6,), (3, 1): (7,)}
                for ln in todo.get((jj, part), ()):
                    chunk = g * 2 + i // 4
                    to = {0: 1, 4: 2}.get(ln, 3)
                    if ln == 0:
                        act.wait_ge(in_codes, (chunk + 1) * 16)
                        act.wait_ge(out_dq, chunk * 16 + 16)
                    if ln > 1 and to == 3:
                        act.wait_ge(line_used, chunk * 6 + {2: 1, 3: 2, 5: 3, 6: 4, 7: 5}[ln])
                    if ln == 1:
                        act.wait_ge(dq_scaled, chunk + 1)
                    sc, bi = LINES[ln]
                    e.activation(DQ[:, to, :], CODES, ACT.Copy, scale=sc, bias=bi).then_inc(line, 1)

            def slot(g, i):
                known = 8 * g + i if isinstance(g, int) else i
                n0 = g * 8 + i
                L = (i + 1) % NT * P + P
                for it in slot_items(known):
                    if it[0] == "T":
                        kb = it[1]
                        c = at(g, i, ("PV", kb))
                        act.wait_ge(t_full, at(g, i, it) + 1)
                        act.wait_ge(pv_done, c - 2)
                        e.activation(r(PT + AT[i, ("PV", kb)] % 3 * 1024, 512), T[AT[known, it] % 2][:, :],
                                     ACT.Copy).then_inc(t_act, 1)
                    elif it[0] == "EX":
                        exp1(i + 1, it[1], L, at(g, i, ("S", it[1])) + (1 - S_PRO))
                    elif it == "PQ":
                        sum_squares(i + 2, at(g, i, "PQ") + 1, None)
                    elif it == "WO":
                        act.wait_ge(t_act, at(g, i, "WO"))
                        act.sem_inc(t_act, 1)
                    elif it == "PKV":
                        squares_k(i + 2, at(g, i, "PKV") + 1, T[AT[known, "PKV"] % 2])
                    elif it == "QK":
                        high_qk(i + 2, at(g, i, "QT") + 1, at(g, i, "KT") + 1,
                                T[AT[known, "QT"] % 2], T[AT[known, "KT"] % 2])
                    elif it == "E":
                        act.wait_ge(pv_done, at(g, i, ("PV", i % NT)) + 1)
                        e.activation(r(OT + i % 2 * 1024, 512), VB[:, :], ACT.Copy).then_inc(ot_high, 1)
                    elif it[0] == "CH":
                        c = it[1]
                        if c == 0:
                            act.wait_ge(t_full, at(g, i, "PKV") + 1)
                        if c == 4 and i:
                            act.wait_ge(t_full, at(g, i, "WO") + 1)
                        q = QL1 + c
                        high_half(q, W_H + w1_place(c)[0], w1_place(c)[1],
                                  count=(g + (i >= 5)) * 64 + 16 * (q // 2 + 1))
                    elif it[0] == "FC":
                        _, _, hi, _, n, np_ = FF_CHUNKS[it[1]]
                        high_half(QFF + it[1], hi, n, np_)
                    elif it == "DA":
                        lines(g, i, 0)
                    elif it == "DB":
                        lines(g, i, 1)

            slots(act, [], slot)
            def high_xla(tg):
                k = T_END + tg * (FT + 1)
                act.wait_ge(t_full, k + 1)
                e.activation(r(XLA, 512, RANK1), T[k % 2][0:RANK1, :], ACT.Copy).then_inc(t_act, 1)

            def high_fw(u):
                act.wait_ge(in_fw[u % 2], 16 * (u // 2))
                if u >= 3:
                    act.wait_ge(x2_ready, u - 2)
                e.activation(r(FW[u % 3], 1024), PBF[:, u % 2 * 1024:(u % 2 + 1) * 1024], ACT.Copy).then_inc(fw_high, 1)

            def ff_high(q):
                _, _, hi, _, n, np_ = FF_CHUNKS[q]
                high_half(QFF + q, hi, n, np_)

            act.wait_ge(t_act, T_LAST)
            act.sem_inc(t_act, 1)
            act.wait_ge(t_full, T_END)
            for q in range(FF_EARLY, NFFC - 1):
                ff_high(q)
            high_xla(0)
            for tg in range(2):
                k = T_END + tg * (FT + 1)
                for j in range(FT):
                    u = tg * FT + j
                    kk = k + 1 + j
                    act.wait_ge(t_full, kk + 1)
                    if u >= 2:
                        act.wait_ge(t_free, T_END + (u - 2) // FT * (FT + 1) + (u - 2) % FT + 2)
                    e.activation(PBF[:, 2048 + u % 2 * 512:2560 + u % 2 * 512], T[kk % 2][:, :], ACT.Relu,
                                 bias=C[:, C_BUP + j:C_BUP + j + 1]).then_inc(t_act, 1)
                    if u + 2 < 2 * FT:
                        high_fw(u + 2)
                    if u == 1:
                        ff_high(NFFC - 1)
                act.wait_ge(x2_ready, (tg + 1) * FT)
                act.wait_ge(z_ones, 2)
                e.activation(r(ZT, 512, RANK1), VB[0:RANK1, :], ACT.Copy).then_inc(z_high, 1)
                if tg == 0:
                    high_xla(1)
                for tt in range(4):
                    act.wait_ge(d_full, tg * 4 + tt + 1)
                    e.activation(DQ[:, tt, 0:D], y_psum(tt), ACT.Tanh, scale=0.5)\
                        .then_inc(y_tanh, 1)

        @block.vector
        def _(dve):
            e = nc.vector
            ch = Tally(dve, v_chain, v_passed)
            ch.per = V_PER

            def stats(t, src):
                k = t % 2
                ch.link(e.bn_stats(ST[:, k, :], src))
                e.bn_aggr(MV[:, k, :], ST[:, k, :]).then_inc(var_ready, 1)

            def apply(t, src, slot_):
                k = t % 2
                dve.wait_ge(var_ready, t + 1)
                dve.wait_ge(rstd_ready, t + 1)
                e.tensor_scalar(XN[slot_], src, MV[:, k, 0:1], RSTD[:, k:k + 1], ALU.subtract, ALU.mult)\
                    .then_inc(xn_ready, 1)

            def low_xt(k, t):
                dve.wait_ge(t_act, k + 1)
                e.tensor_tensor(XT[:, 1, :, t * P:(t + 1) * P], T[k % 2][:, :].rearrange("p (k n) -> p k n", k=KT),
                                XT[:, 0, :, t * P:(t + 1) * P].bitcast(F32), ALU.subtract).then_inc(t_free, 1)

            dve.wait_ge(in_const, 16)
            ch.done(e.tensor_scalar(QKW[:, 0:1], C[:, C_QKW:C_QKW + 1], 1.0 / math.sqrt(HD), None, ALU.mult))
            e.memset(CMP[:, 0, 0:8], 0.0).then_inc(dq_scaled, 1)
            ch.done(e.tensor_copy(QKW[:, 1:2], C[:, C_QKW + 1:C_QKW + 2]))
            ch.done(e.tensor_scalar(SLC[:, :], C[:, C_SLOPE:C_SLOPE + 4], -1.0, None, ALU.mult))
            for t in range(NT + 2):
                if t < NT:
                    dve.wait_ge(in_x[t % 4], 16 * (t // 4 + 1))
                    if t >= 2:
                        dve.wait_ge(xn_ready, t - 1)
                    stats(t, XS[t % 4])
                if 1 <= t <= NT:
                    if t >= 5:
                        dve.wait_ge(t_full, t - 4)
                    apply(t - 1, XS[(t - 1) % 4], (t - 1) % 4)
                if t >= 2:
                    low_xt(t - 2, t - 2)
            for u in range(8):
                blk, nt = u // 2, u % 2
                k = T_QK + u
                dve.wait_ge(t_act, k + 1)
                dve.wait_ge(t_free, k)
                m = C_MASK + 2 * (blk // 2)
                hi = r(PT + u % 2 * 512, 512)
                ch.done(e.tensor_copy(hi, TMP[u % 2]))
                ch.link(e.tensor_scalar(TMP[4], TMP[u % 2], C[:, m + 1:m + 2], None, ALU.mult))
                dst = (QS if blk < 2 else KS) + blk % 2 * 1024 + nt * 512
                e.scalar_tensor_tensor(r(dst, 512), hi.bitcast(F32), C[:, m:m + 1], TMP[4],
                                       ALU.mult, ALU.add).then_inc(t_free, 1)
            dve.wait_ge(in_rows, 16)
            for t in range(NT):
                k = T_VAR + t
                dve.wait_ge(t_act, k + 1)
                ch.done(e.tensor_copy(RT[:, 0, t * 8:t * 8 + 8], T[k % 2][:, 192:200]))
                e.tensor_tensor(VN0[:, t * 64:t * 64 + 64], T[k % 2][:, 0:64], ROWS[:, R_BV:R_BV + 64], ALU.add)\
                    .then_inc(t_free, 1)
            ch.settle()

            def by_e(k):
                return RT[:, k, :].rearrange("p (t e) -> p t e", e=NEXP)

            def over_e(a):
                return a.unsqueeze(2).to_broadcast([P, NT, NEXP])

            ch.link(e.tensor_reduce(RT[:, 3, 0:NT], by_e(0), AX.X, ALU.max))
            e.tensor_tensor(by_e(1), by_e(0), over_e(RT[:, 3, 0:NT]), ALU.subtract).then_inc(row_ready, 1)
            dve.wait_ge(row_exp, 1)
            ch.link(e.tensor_reduce(RT[:, 3, 8:16], by_e(2), AX.X, ALU.add))
            ch.link(e.reciprocal(RT[:, 3, 16:24], RT[:, 3, 8:16]))
            ch.link(e.tensor_tensor(by_e(4), by_e(2), over_e(RT[:, 3, 16:24]), ALU.mult))
            pj = by_e(4).unsqueeze(2).to_broadcast([P, NT, NEXP, NEXP])
            pe_ = by_e(4).unsqueeze(3).to_broadcast([P, NT, NEXP, NEXP])

            def cmp4(k):
                return CMP[:, k, :].rearrange("p (t e j) -> p t e j", e=NEXP, j=NEXP)

            ch.done(e.tensor_tensor(cmp4(0), pj, pe_, ALU.is_gt))
            ch.link(e.tensor_tensor(cmp4(1), pj, pe_, ALU.is_equal))
            tri = C[:, C_TRI:C_TRI + 64].unsqueeze(1).to_broadcast([P, NT, 64])
            c1 = CMP[:, 1, :].rearrange("p (t n) -> p t n", t=NT)
            ch.link(e.tensor_tensor(c1, c1, tri, ALU.mult))
            ch.link(e.tensor_tensor(CMP[:, 0, :], CMP[:, 0, :], CMP[:, 1, :], ALU.add))
            ch.link(e.tensor_reduce(RT[:, 5, :], CMP[:, 0, :].rearrange("p (n j) -> p n j", j=NEXP), AX.X, ALU.add))
            ch.link(e.scalar_tensor_tensor(RT[:, 6, :], RT[:, 5, :], 1.5, RT[:, 4, :], ALU.is_lt, ALU.mult))
            ch.link(e.tensor_reduce(RT[:, 3, 24:32], by_e(6), AX.X, ALU.add))
            ch.link(e.reciprocal(RT[:, 3, 32:40], RT[:, 3, 24:32]))
            ch.link(e.tensor_tensor(by_e(7), by_e(6), over_e(RT[:, 3, 32:40]), ALU.mult))
            ch.link(e.tensor_scalar(RT[:, 7, :], RT[:, 7, :], 2.0, None, ALU.mult))
            hn = HN.rearrange("p (n r) -> p n r", r=RANK0)
            e.tensor_tensor(hn, hn, RT[:, 7, :].unsqueeze(2).to_broadcast([P, 64, RANK0]), ALU.mult)\
                .then_inc(hw_ready, 1)

            def ffn0_out(t):
                dve.wait_ge(s_full, t + 1)
                e.tensor_tensor(G[:, t * D:(t + 1) * D], y_bank(t), ROWS[:, R_BB:R_BB + D], ALU.add)\
                    .then_inc(y_ready, 1)

            def gate(t):
                dve.wait_ge(y_tanh, t + 1)
                e.scalar_tensor_tensor(G[:, t * D:(t + 1) * D], TMP[2 + t % 2], 1.0, G[:, t * D:(t + 1) * D],
                                       ALU.add, ALU.mult).then_inc(gate_done, 1)

            for t in range(NT):
                k = T_HW + t
                dve.wait_ge(t_act, k + 1)
                o = OT + t % 2 * 256
                e.tensor_tensor(r(o + P, P), T[k % 2][:, 0:P], rf(o, P), ALU.subtract).then_inc(t_free, 1)
                if t:
                    ffn0_out(t - 1)
                if t >= 2:
                    gate(t - 2)
            ffn0_out(NT - 1)
            gate(NT - 2)
            gate(NT - 1)

            def max0(n, a):
                u = n * 4 + a
                dve.wait_ge(s_full, S_ATT + u + 1)
                k = n % 2 * 4 + a
                if n >= 2:
                    dve.wait_ge(exp_done, u - 7)
                e.tensor_reduce(NM[:, k:k + 1], S[u % 2][:, :], AX.X, ALU.max, negate=True).then_inc(max_ready, 1)

            def low_pt(k, c, bank, kc):
                dve.wait_ge(t_act, k)
                o = PT + kc % 3 * 1024
                e.tensor_tensor(r(o + 512, 512), bank[:, :], rf(o, 512), ALU.subtract).then_inc(t_free, 1)

            for a in range(4):
                max0(0, a)
            for n in range(2 * H0):
                for kb in range(NT):
                    c = n * NT + kb
                    if kb in SCORE_AT and n + 1 < 2 * H0:
                        max0(n + 1, SCORE_AT[kb])
                    low_pt(T_ATT + c + 1, c, T[(T_ATT + c) % 2], c)
                if n % H0 == H0 - 1:
                    o = OT + n // H0 * 1024
                    dve.wait_ge(ot_high, n // H0 + 1)
                    e.tensor_tensor(r(o + 512, 512), VB[:, :], rf(o, 512), ALU.subtract).then_inc(ot_low, 1)
            for s in range(NT + 3):
                if s < NT:
                    dve.wait_ge(w_full, s + 1)
                    if s == 0:
                        dve.wait_ge(t_full, T_LN1)
                    if s >= 4:
                        dve.wait_ge(x1_ready, s - 3)
                    tmp = TMP[s % 4]
                    e.tensor_tensor(tmp, WB[:, :], ROWS[:, R_BO:R_BO + D], ALU.add).then_inc(w_free, 1)
                    dve.wait_ge(w_free, s + 1)
                    e.scalar_tensor_tensor(tmp, tmp, 0.5, G[:, s * D:(s + 1) * D], ALU.mult, ALU.mult)\
                        .then_inc(tmp_ready, 1)
                if 1 <= s <= NT:
                    t = s - 1
                    dve.wait_ge(x1_ready, t + 1)
                    if t >= 2:
                        dve.wait_ge(xn_ready, NT + t - 1)
                    stats(NT + t, XS[t % 4])
                if 2 <= s <= NT + 1:
                    t = s - 2
                    if t >= 4:
                        dve.wait_ge(t_full, T_LN1 + t - 3)
                    apply(NT + t, XS[t % 4], t % 4)
                if s >= 3:
                    low_xt(T_LN1 + s - 3, s - 3)
            for k in range(4):
                dve.wait_ge(out_x1[k], 32)

            def copy_k(tcount, tk, tprev):
                dve.wait_ge(t_act, tcount)
                dve.wait_ge(t_full, tprev)
                e.tensor_copy(QN[:, 4 * HD:5 * HD], tk[:, 0:HD]).then_inc(t_free, 1)

            def scale_qk(m, icount, tcopy):
                dve.wait_ge(inv_ready, icount)
                dve.wait_ge(t_free, tcopy)
                k = m % 2
                e.tensor_tensor(QN[:, 0:4 * HD].rearrange("p (a n) -> p a n", a=4),
                                WB[:, :].rearrange("p (a n) -> p a n", a=4),
                                INV[:, k, 0:4].unsqueeze(2).to_broadcast([P, 4, HD]), ALU.mult).then_inc(w_free, 1)
                e.tensor_scalar(QN[:, 4 * HD:5 * HD], QN[:, 4 * HD:5 * HD], INV[:, k, 4:5], None, ALU.mult)\
                    .then_inc(qk_ready, 1)

            def low_qk(m, tq, tk, bq, bk):
                o = QT + m % 2 * 1024
                dve.wait_ge(t_act, tq)
                e.scalar_tensor_tensor(r(o + 512, 512), bq[:, :], QKW[:, 0:1], rf(o, 512), ALU.mult, ALU.subtract)\
                    .then_inc(t_free, 1)
                o = KTR + m % NT * P
                dve.wait_ge(t_act, tk)
                e.scalar_tensor_tensor(r(o + TOK, P), bk[:, 0:P], QKW[:, 1:2], rf(o, P), ALU.mult, ALU.subtract)\
                    .then_inc(t_free, 1)

            def bias_max(m, a, L, scount, bank):
                hold(dve, s_full, scount, v_passed)
                k = m % 2 * 4 + a
                e.tensor_tensor_reduce(out=PB[:, m % 2, a, 0:L], in0=bank[:, 0:L], in1=REL[:, TOK - L:TOK],
                                       scale=SLC[:, a:a + 1], scalar=3.0e38, op0=ALU.add, op1=ALU.min,
                                       accum_out=NM[:, k:k + 1]).then_inc(s_free, 1)

            def clear_output(k):
                ch.done(e.memset(G[:, k * 1024:(k + 1) * 1024], 0.0))

            for m in range(2):
                k = T_PRO + 3 * m
                copy_k(k + 1, T[k % 2], k)
                scale_qk(m, m + 1, k + 1)
                low_qk(m, k + 2, k + 3, T[(k + 1) % 2], T[k % 2])
                clear_output(2 * m)
                clear_output(2 * m + 1)
            for a in range(4):
                bias_max(0, a, P, S_PRO + a + 1, S[a % 2])

            def combine(g, i, part):
                jj = i % 4
                chunk = g * 2 + i // 4
                if jj == 0 and part == 0 and not (isinstance(g, int) and 8 * g + i == 0):
                    dve.wait_ge(in_absmax, chunk * 16)
                    e.tensor_tensor(DQ[:, 1, :], DQ[:, 1, :], DQ[:, 3, :], ALU.mult).then_inc(dq_scaled, 1)
                todo = {(1, 0): (1,), (1, 1): (2,), (2, 0): (3,), (2, 1): (5,), (3, 0): (6,), (3, 1): (7,)}
                for ln in todo.get((jj, part), ()):
                    dve.wait_ge(line, chunk * 8 + ln + 1)
                    b, op = (1, ALU.min) if ln < 4 else (2, ALU.max)
                    if ln not in (1, 5):
                        dve.wait_ge(line_used, chunk * 6 + {2: 1, 3: 2, 6: 4, 7: 5}[ln])
                    e.tensor_tensor(DQ[:, b, :], DQ[:, b, :], DQ[:, 3, :], op).then_inc(line_used, 1)
                if (jj, part) == (3, 1):
                    ch.link(e.tensor_scalar(CODES, CODES, 8, None, ALU.bitwise_and))
                    hold(dve, line_used, chunk * 6 + 6, v_passed)
                    e.copy_predicated(DQ[:, 1, :], CODES, DQ[:, 2, :]).then_inc(dq_selected, 1)
                    dve.wait_ge(dq_selected, chunk + 1)

            def slot(g, i):
                known = 8 * g + i if isinstance(g, int) else i
                n0 = g * 8 + i
                L = (i + 1) % NT * P + P
                for it in slot_items(known):
                    if it[0] == "S":
                        a = it[1]
                        if i == 7 and a == 0:
                            ch.link(e.tensor_scalar(SLC[:, :], C[:, bass.ds(g * 4 + (C_SLOPE + 4), 4)], -1.0, None, ALU.mult))
                        if a == 0 and i > 0:
                            prev = (at(g, i - 1, "last") + 1) if i >= 1 else None
                            dve.wait_ge(t_full, prev)
                        bias_max(i + 1, a, L, at(g, i, it) + 1, S[AT[known, it] % 2])
                    elif it[0] == "T":
                        low_pt(at(g, i, it) + 1, None, T[AT[known, it] % 2], AT[i, ("PV", it[1])])
                    elif it == "WO":
                        dve.wait_ge(t_full, at(g, i, "WO") + 1)
                        t = (i - 1) % NT
                        dve.wait_ge(t_free, at(g, i, "WO"))
                        e.tensor_tensor(G[:, t * D:(t + 1) * D], G[:, t * D:(t + 1) * D],
                                        T[AT[known, "WO"] % 2][:, :], ALU.add).then_inc(t_free, 1)
                    elif it == "PKV":
                        prev = T_BASE if known == 0 and isinstance(g, int) else at(g, i - 1, "KT") + 1
                        copy_k(at(g, i, "PKV") + 1, T[AT[known, "PKV"] % 2], prev)
                    elif it == "QN":
                        scale_qk(i + 2, n0 + 3, at(g, i, "PKV") + 1)
                    elif it == "QK":
                        low_qk(i + 2, at(g, i, "QT") + 1, at(g, i, "KT") + 1,
                               T[AT[known, "QT"] % 2], T[AT[known, "KT"] % 2])
                    elif it == "E":
                        o = OT + i % 2 * 1024
                        dve.wait_ge(ot_high, n0 + 3)
                        e.tensor_tensor(r(o + 512, 512), VB[:, :], rf(o, 512), ALU.subtract).then_inc(ot_low, 1)
                    elif it[0] in ("CH", "FC"):
                        if it[0] == "CH":
                            hi, n = w1_place(it[1])
                            q, np_, hi, lo = QL1 + it[1], P, W_H + hi, W_L + hi
                            dve.wait_ge(w_high, (g + (i >= 5)) * 8 + q + 1)
                        else:
                            _, _, hi, lo, n, np_ = FF_CHUNKS[it[1]]
                            q = QFF + it[1]
                            dve.wait_ge(w_high, q + 1)
                        e.tensor_tensor(r(lo, n, np_), RAW[0:np_, q % 2, 0:n], rf(hi, n, np_), ALU.subtract)\
                            .then_inc(split, 1)
                    elif it == "DA":
                        combine(g, i, 0)
                    elif it == "DB":
                        combine(g, i, 1)

            slots(dve, [ch], slot)
            dve.wait_ge(t_full, T_LAST + 1)
            dve.wait_ge(t_free, T_LAST)
            e.tensor_tensor(G[:, 7 * D:8 * D], G[:, 7 * D:8 * D], T[T_LAST % 2][:, :], ALU.add).then_inc(t_free, 1)
            def low_xla(tg):
                k = T_END + tg * (FT + 1)
                dve.wait_ge(t_act, k + 1)
                e.tensor_tensor(r(XLA + 512, 512, RANK1), T[k % 2][0:RANK1, :], rf(XLA, 512, RANK1), ALU.subtract)\
                    .then_inc(t_free, 1)

            def gate1(u):
                tt = u % 4
                dve.wait_ge(y_tanh, NT + u + 1)
                if u >= 4:
                    dve.wait_ge(out_done, u - 3)
                e.scalar_tensor_tensor(PBF[:, Y_AT[tt] * D:(Y_AT[tt] + 1) * D], DQ[:, tt, 0:D], 1.0, y_psum(tt),
                                       ALU.add, ALU.mult).then_inc(y_ready, 1)

            def result(u):
                dve.wait_ge(y_ready, NT + u + 1)
                y = PBF[:, Y_AT[u % 4] * D:(Y_AT[u % 4] + 1) * D]
                e.scalar_tensor_tensor(y, y, 0.5, G[:, u * D:(u + 1) * D], ALU.mult, ALU.mult).then_inc(y_scaled, 1)

            dve.wait_ge(in_absmax, NDQ * 16)
            e.tensor_tensor(DQ[:, 1, :], DQ[:, 1, :], DQ[:, 3, :], ALU.mult).then_inc(dq_scaled, 1)
            low_xla(0)
            for tg in range(2):
                k = T_END + tg * (FT + 1)
                for j in range(FT):
                    u = tg * FT + j
                    kk = k + 1 + j
                    o = X2 + u % 2 * 1024
                    src = PBF[:, 2048 + u % 2 * 512:2560 + u % 2 * 512]
                    dve.wait_ge(t_act, kk + 1)
                    if u >= 2:
                        dve.wait_ge(x2_ready, u - 1)
                    ch.link(e.tensor_copy(r(o, 512), src))
                    e.tensor_tensor(r(o + 512, 512), src, rf(o, 512), ALU.subtract).then_inc(t_free, 1)
                    if tg and j < 4:
                        result(j)
                dve.wait_ge(z_high, tg + 1)
                e.tensor_tensor(r(ZT + 512, 512, RANK1), VB[0:RANK1, :], rf(ZT, 512, RANK1), ALU.subtract)\
                    .then_inc(z_low, 1)
                if tg == 0:
                    low_xla(1)
                    for u in range(4):
                        gate1(u)
            for u in range(4, 8):
                gate1(u)
                result(u)

        @block.tensor
        def _(pe):
            e = nc.tensor

            def mm3(dst, lh, ll, rh, rl, start, stop):
                e.matmul(dst, lh, rh, start=start, stop=False)
                e.matmul(dst, lh, rl, start=False, stop=False)
                return e.matmul(dst, ll, rh, start=False, stop=stop)

            def xt(half, kt, a, n):
                return XT[:, half, kt, a:a + n]

            def ring(k):
                if isinstance(k, int) and k < 2:
                    return
                pe.wait_ge(t_free, k - 1)

            def transpose_x(k, t, count):
                ring(k)
                pe.wait_ge(xn_ready, count)
                for kt in range(KT):
                    last = e.transpose(T[k % 2][:, kt * P:(kt + 1) * P], XN[t % 4][:, kt * P:(kt + 1) * P], IDENT)
                last.then_inc(t_full, 1)

            pe.wait_ge(in_const, 16)
            for t in range(NT):
                transpose_x(T_LN0 + t, t, t + 1)
            pe.wait_ge(split, W0_QK)
            pe.wait_ge(t_free, NT)
            for u in range(8):
                blk, nt = u // 2, u % 2
                k = T_QK + u
                ring(k)
                for kt in range(KT):
                    c = kt * 512 + blk * P
                    last = mm3(T[k % 2][:, :], r(WQK_H + c, P), r(WQK_L + c, P), xt(0, kt, nt * 512, 512),
                               xt(1, kt, nt * 512, 512), kt == 0, kt == KT - 1)
                last.then_inc(t_full, 1)
            pe.wait_ge(split, W0_VAR)
            for t in range(NT):
                k = T_VAR + t
                ring(k)
                for kt in range(KT):
                    c = kt * NVAR
                    last = mm3(T[k % 2][:, 0:NVAR], xt(0, kt, t * P, P), xt(1, kt, t * P, P), r(WVAR_H + c, NVAR),
                               r(WVAR_L + c, NVAR), kt == 0, kt == KT - 1)
                last.then_inc(t_full, 1)
            pe.wait_ge(split, W0_BASE)

            def base(t):
                if t >= 4:
                    pe.wait_ge(y_ready, t - 3)
                for kt in range(KT):
                    c = kt * 512
                    mm3(y_bank(t), xt(0, kt, t * P, P), xt(1, kt, t * P, P), r(WBASE_H + c, D),
                        r(WBASE_L + c, D), kt == 0, False)

            for t in range(3):
                base(t)
            pe.wait_ge(hw_ready, 1)
            pe.wait_ge(split, W0_EXP)

            def transpose_hn(t):
                k = T_HW + t
                ring(k)
                e.transpose(T[k % 2][:, 0:P], HN[:, t * P:(t + 1) * P], IDENT).then_inc(t_full, 1)

            transpose_hn(0)
            for t in range(NT):
                if t + 1 < NT:
                    transpose_hn(t + 1)
                if 3 <= t + 2 < NT:
                    base(t + 2)
                pe.wait_ge(t_free, T_HW + t + 1)
                o = OT + t % 2 * 256
                mm3(y_bank(t), r(o, P), r(o + P, P), r(WEXP_H, D), r(WEXP_L, D), False, True)\
                    .then_inc(s_full, 1)

            def scores0(n, a):
                qg, h = n // H0, n % H0
                u = n * 4 + a
                if u >= 2:
                    pe.wait_ge(exp_done, u - 1)
                else:
                    pe.wait_ge(y_ready, NT - 2 + 2 * u)
                b = h % 4 * 32
                qc = QS + h // 4 * 1024 + (qg * 4 + a) * P
                for c in range(2):
                    kc = KS + h // 4 * 1024 + c * 512
                    last = e.matmul(S[u % 2][:, c * 512:(c + 1) * 512], R[b:b + 32, qc:qc + P],
                                    R[b:b + 32, kc:kc + 512], start=True, stop=True)
                last.then_inc(s_full, 1)

            for a in range(4):
                scores0(0, a)

            def values0(c):
                n, kb = c // NT, c % NT
                h = n % H0
                pe.wait_ge(t_free, T_ATT + c + 1)
                if n == H0 and kb == 0:
                    pe.wait_ge(ot_low, 1)
                v = r(VPAD_AT[kb] + h * P, P)
                if n == 0 and kb in (0, 4, 6):
                    pe.wait_ge(vpad_ready, {0: 1, 4: 2, 6: 3}[kb] * H0)
                o = PT + c % 3 * 1024
                first, end = h == 0 and kb == 0, h == H0 - 1 and kb == NT - 1
                e.matmul(VB[:, :], v, r(o, 512), start=first, stop=False)
                e.matmul(VB[:, :], v, r(o + 512, 512), start=False, stop=end).then_inc(pv_done, 1)

            for n in range(2 * H0):
                for kb in range(NT):
                    c = n * NT + kb
                    k = T_ATT + c
                    if kb in SCORE_AT and n + 1 < 2 * H0:
                        scores0(n + 1, SCORE_AT[kb])
                    if kb == 0:
                        pe.wait_ge(probs_ready, 4 * (n + 1))
                    ring(k)
                    for a in range(4):
                        last = e.transpose(T[k % 2][:, a * P:(a + 1) * P], PB[:, n % 2, a, kb * P:(kb + 1) * P], IDENT)
                    last.then_inc(t_full, 1)
                    if c >= 2:
                        values0(c - 2)
            values0(2 * H0 * NT - 2)
            values0(2 * H0 * NT - 1)
            for t in range(NT):
                qg = t // 4
                pe.wait_ge(ot_low, qg + 1)
                pe.wait_ge(split, W0_O)
                if t:
                    pe.wait_ge(w_free, t)
                o = OT + qg * 1024 + t % 4 * P
                mm3(WB[:, :], r(o, P), r(o + 512, P), r(WO0_H, D), r(WO0_L, D), True, True).then_inc(w_full, 1)
                if t >= 3:
                    transpose_x(T_LN1 + t - 3, t - 3, NT + t - 2)
            for t in range(NT - 3, NT):
                transpose_x(T_LN1 + t, t, NT + t + 1)

            def project_q(m, wait_w, chunks):
                pe.wait_ge(w_free, wait_w)
                for kt in range(KT):
                    pe.wait_ge(split, chunks + kt + 1)
                    c = kt * 768
                    last = mm3(WB[:, :], xt(0, kt, m % NT * P, P), xt(1, kt, m % NT * P, P), r(W_H + c, 512),
                               r(W_L + c, 512), kt == 0, kt == KT - 1)
                last.then_inc(w_full, 1)

            def project_kv(m, k, bank):
                ring(k)
                for kt in range(KT):
                    c = kt * 768 + 512
                    last = mm3(bank[:, 0:256], xt(0, kt, m % NT * P, P), xt(1, kt, m % NT * P, P), r(W_H + c, 256),
                               r(W_L + c, 256), kt == 0, kt == KT - 1)
                last.then_inc(t_full, 1)

            def transpose_qk(count, kq, kk, bq, bk):
                pe.wait_ge(qk_ready, count)
                ring(kq)
                for a in range(4):
                    last = e.transpose(bq[:, a * P:(a + 1) * P], QN[:, a * HD:(a + 1) * HD], IDENT)
                last.then_inc(t_full, 1)
                ring(kk)
                e.transpose(bk[:, 0:P], QN[:, 4 * HD:5 * HD], IDENT).then_inc(t_full, 1)

            def scores1(m, a, L, wait_s, wait_t, bank):
                if a == 0:
                    pe.wait_ge(t_free, wait_t)
                if wait_s is not None:
                    pe.wait_ge(s_free, wait_s)
                q = QT + m % 2 * 1024 + a * P
                for c in range(0, L, 512):
                    w = min(512, max(256, L - c))
                    last = mm3(bank[:, c:c + w], r(q, P), r(q + 512, P), r(KTR + c, w), r(KTR + TOK + c, w), True, True)
                last.then_inc(s_full, 1)

            pe.wait_ge(t_free, T_LN1 + NT)
            for m in range(2):
                project_q(m, NT + m, QL1)
                k = T_PRO + 3 * m
                project_kv(m, k, T[k % 2])
                transpose_qk(m + 1, k + 1, k + 2, T[(k + 1) % 2], T[k % 2])
            for a in range(4):
                if a < 2:
                    pe.wait_ge(exp_done, EX_PRO)
                scores1(0, a, P, a - 1 if a >= 2 else None, T_BASE, S[a % 2])

            def values1(g, i, kb):
                known = 8 * g + i if isinstance(g, int) else i
                pe.wait_ge(t_free, at(g, i, ("T", kb)) + 1)
                if kb == 0:
                    pe.wait_ge(ot_low, g * 8 + i + 2)
                if kb == i % NT:
                    pe.wait_ge(v_split, g * 8 + i + 1)
                o = PT + AT[i, ("PV", kb)] % 3 * 1024
                mm3(VB[:, :], r(VN + kb * P, P), r(VN + TOK + kb * P, P), r(o, 512), r(o + 512, 512),
                    kb == 0, kb == i % NT).then_inc(pv_done, 1)

            def output1(g, count_ot, k, bank, m, first):
                pe.wait_ge(ot_low, count_ot)
                ring(k)
                for a in range(GRP):
                    if first:
                        pe.wait_ge(split, g * 8 + (QL1 + 5 + a))
                    o = OT + m % 2 * 1024 + a * P
                    w = WOUT + a * 512
                    last = mm3(bank[:, :], r(o, P), r(o + 512, P), r(W_H + w, 512), r(W_L + w, 512), a == 0, a == 3)
                last.then_inc(t_full, 1)

            def slot(g, i):
                known = 8 * g + i if isinstance(g, int) else i
                L = (i + 1) % NT * P + P
                started = False
                for it in slot_items(known):
                    if it[0] == "S":
                        prev = T_BASE if known == 0 and isinstance(g, int) else at(g, i - 1, "KT") + 1
                        u = at(g, i, it)
                        scores1(i + 1, it[1], L, u - (1 + S_PRO), prev, S[AT[known, it] % 2])
                    elif it[0] == "T":
                        kb = it[1]
                        k = at(g, i, it)
                        if not started:
                            pe.wait_ge(probs_ready, (g * 8 + i) * 4 + EX_BASE)
                            started = True
                        ring(k)
                        bank = T[AT[known, it] % 2]
                        for a in range(4):
                            last = e.transpose(bank[:, a * P:(a + 1) * P], PB[:, i % 2, a, kb * P:(kb + 1) * P], IDENT)
                        last.then_inc(t_full, 1)
                        if kb >= 2:
                            values1(g, i, kb - 2)
                    elif it == "WO":
                        output1(g, g * 8 + i + 2, at(g, i, "WO"), T[AT[known, "WO"] % 2], i - 1, i == 1)
                    elif it == "PQ":
                        project_q(i + 2, at(g, i, "PQ"), (g + (i + 2) // 8) * 8 + QL1)
                    elif it == "PKV":
                        project_kv(i + 2, at(g, i, "PKV"), T[AT[known, "PKV"] % 2])
                    elif it == "QK":
                        transpose_qk(g * 8 + i + 3, at(g, i, "QT"), at(g, i, "KT"),
                                     T[AT[known, "QT"] % 2], T[AT[known, "KT"] % 2])
                    elif it == "E":
                        for kb in range(max(0, i % NT - 1), i % NT + 1):
                            values1(g, i, kb)

            slots(pe, [], slot)
            output1(HKV - 1, STEPS + 2, T_LAST, T[T_LAST % 2], STEPS - 1, False)

            def product_xla(tg):
                k = T_END + tg * (FT + 1)
                ring(k)
                for kt in range(KT):
                    last = mm3(T[k % 2][:, :], r(LA_H + kt * P, P), r(LA_L + kt * P, P), xt(0, kt, tg * 512, 512),
                               xt(1, kt, tg * 512, 512), kt == 0, kt == KT - 1)
                last.then_inc(t_full, 1)

            pe.wait_ge(split, QFF + FF_LA)
            product_xla(0)
            for tg in range(2):
                k = T_END + tg * (FT + 1)

                def up(j):
                    u, kk = tg * FT + j, k + 1 + j
                    if u < 2:
                        pe.wait_ge(split, QFF + FF_W[u])
                    else:
                        pe.wait_ge(fw_split, u - 1)
                    ring(kk)
                    w = FW[u % 3]
                    for kt in range(KT):
                        mm3(T[kk % 2][:, :], r(w + kt * P, P), r(w + 1024 + kt * P, P), xt(0, kt, tg * 512, 512),
                            xt(1, kt, tg * 512, 512), kt == 0, False)
                    if j == 0:
                        pe.wait_ge(t_free, k + 1)
                        pe.wait_ge(split, QFF + FF_LB)
                    mm3(T[kk % 2][:, :], r(LB_H + j * P, P, RANK1), r(LB_L + j * P, P, RANK1), r(XLA, 512, RANK1),
                        r(XLA + 512, 512, RANK1), False, True).then_inc(t_full, 1)

                def down(j):
                    u, kk = tg * FT + j, k + 1 + j
                    pe.wait_ge(t_free, kk + 1)
                    if tg and j == 0:
                        pe.wait_ge(y_ready, NT + 4)
                        pe.wait_ge(z_low, 1)
                    if not tg and j == 0:
                        pe.wait_ge(ot_low, STEPS + 2)
                        pe.wait_ge(s_free, S_END - S_PRO)
                        pe.wait_ge(split, QFF + FF_DLA)
                    o, w = X2 + u % 2 * 1024, FW[u % 3]
                    for tt in range(4):
                        mm3(S[tt // 2][:, tt % 2 * D:(tt % 2 + 1) * D], r(o + tt * P, P), r(o + 512 + tt * P, P),
                            r(w + 512, D), r(w + 1536, D), j == 0, False)
                    mm3(VB[:, :], r(DLA_H + j * P, P), r(DLA_L + j * P, P), r(o, 512), r(o + 512, 512),
                        j == 0, j == FT - 1).then_inc(x2_ready, 1)

                up(0)
                for j in range(FT):
                    if j + 1 < FT:
                        up(j + 1)
                    down(j)
                if tg == 0:
                    product_xla(1)
                pe.wait_ge(split, QFF + FF_DLB)
                pe.wait_ge(z_low, tg + 1)
                for tt in range(4):
                    mm3(y_psum(tt), r(ZT + tt * P, P, RANK1 + 1), r(ZT + 512 + tt * P, P, RANK1 + 1),
                        r(DLB_H, D, RANK1 + 1), r(DLB_L, D, RANK1 + 1), False, True)\
                        .then_inc(d_full, 1)


def kernel(**inputs):
    import concourse.bacc as bacc
    from concourse.bass_utils import run_bass_kernel_spmd

    a = {k: np.asarray(v) for k, v in inputs.items()}

    def tiles(w):
        k = w.shape[0] // P
        return w.reshape(k, P, -1).transpose(1, 0, 2).reshape(P, -1)

    qk = a["L0_attn_Wqk_w"].reshape(H0, E0, 2, D)
    bqk = a["L0_attn_Wqk_b"].reshape(H0, E0, 2)
    stacked, bias = [], []
    for w in range(2):
        q = np.broadcast_to(qk[:, None, :, w, :], (H0, 4, E0, D)).reshape(2 * P, D)
        stacked.append(q)
        bias.append(np.broadcast_to(bqk[:, None, :, w], (H0, 4, E0)).reshape(2, P))
    w_qk = np.concatenate(stacked).T
    w_var = np.concatenate([a["L0_attn_Wv_w"], a["L0_ffn_A"].reshape(NEXP * RANK0, D), a["L0_ffn_W_router"]])
    w_var = np.pad(w_var, ((0, NVAR - len(w_var)), (0, 0))).T
    w_exp = a["L0_ffn_B"].transpose(0, 2, 1).reshape(P, D)
    w_o = np.broadcast_to(a["L0_attn_Wo_w"].T.reshape(H0, 1, E0, D), (H0, 2, E0, D)).reshape(P, D)
    w0 = np.concatenate([tiles(w_qk), tiles(w_var), tiles(a["L0_ffn_W_base"].T), w_exp, w_o], 1)

    wq = a["L1_attn_Wq"].reshape(HKV, GRP * HD, D)
    wk = a["L1_attn_Wk"].reshape(HKV, HD, D)
    wv = a["L1_attn_Wv"].reshape(HKV, HD, D)
    wo = a["L1_attn_Wo"].T.reshape(HKV, GRP * HD, D)
    w1 = np.concatenate([np.concatenate([tiles(np.concatenate([wq[g], wk[g], wv[g]]).T), tiles(wo[g])], 1)
                         for g in range(HKV)])

    pad = FT * P - FF

    def ff_layout(up, down):
        up = np.pad(up.reshape(FF, D), ((0, pad), (0, 0))).reshape(FT, P, KT, P).transpose(3, 0, 2, 1)
        down = np.pad(down.reshape(D, FF), ((0, 0), (0, pad))).reshape(D, FT, P).transpose(2, 1, 0)
        both = np.concatenate([up.reshape(P, FT, D), down], 2).reshape(P, NDQ, DQN)
        return both.transpose(1, 0, 2).reshape(NDQ * P, DQN)

    codes = ff_layout(a["L1_ffn_w_up_codes"], a["L1_ffn_w_down_codes"])
    absmax = ff_layout(np.repeat(a["L1_ffn_w_up_absmax"], 64), np.repeat(a["L1_ffn_w_down_absmax"], 64))

    def wide(w):
        return np.pad(w, ((0, 0), (0, P - w.shape[1])))

    def tall(w):
        return np.pad(w, ((0, P - w.shape[0]), (0, 0)))

    lora = np.concatenate([
        tiles(wide(a["L1_ffn_w_up_lora_a"])), tall(np.pad(a["L1_ffn_w_up_lora_b"], ((0, 0), (0, pad)))),
        tiles(wide(np.pad(a["L1_ffn_w_down_lora_a"], ((0, pad), (0, 0))))), 
        tall(np.concatenate([a["L1_ffn_w_down_lora_b"], a["L1_ffn_b_down"][None, :]]))], 1)

    p = np.arange(P)
    e = np.arange(NEXP)
    tri = np.broadcast_to((e[None, :] < e[:, None]).reshape(1, -1), (P, NEXP * NEXP))
    copy = p % 32 // E0
    low_q, low_k = copy >= 2, copy % 2 == 1
    masks = np.stack([1 - 2 * low_q, low_q, 1 - 2 * low_k, low_k], 1)
    heads = HKV * GRP
    start = 2 ** (-2 ** (-(math.log2(heads) - 3)))
    slopes = np.array([start * start ** i for i in range(heads)], np.float32)
    inverse = np.concatenate([(1.0 / slopes.astype(np.float64)).reshape(HKV, GRP), np.ones((HKV, 1))], 1)
    consts = np.concatenate([
        np.eye(P), tri, masks, np.stack([*bias[0], *bias[1]], 1),
        np.stack([a["L1_attn_q_norm_w"], a["L1_attn_k_norm_w"]], 1),
        np.pad(a["L1_ffn_b_up"], (0, pad)).reshape(FT, P).T,
        np.broadcast_to(slopes, (P, heads)), np.broadcast_to(inverse.reshape(1, -1), (P, HKV * 5)),
        np.broadcast_to([-0.5] * 5 + [-1.0] * 4, (P, 9)),
    ], 1).astype(np.float32)
    rows = np.broadcast_to(np.concatenate([a["L0_attn_Wv_b"], a["L0_attn_Wo_b"], a["L0_ffn_b_base"]]), (P, NROWS))
    gap = np.arange(TOK)[None, :] - (TOK - P) - p[:, None]
    rel = np.where(gap > 0, -1e33, gap).astype(np.float32)

    nc = bacc.Bacc("TRN2", target_bir_lowering=False, num_devices=1)
    arrays = {"x": a["L0_attn_x"].reshape(TOK, D), "w0": w0, "w1": w1, "codes": codes, "absmax": absmax, "lora": lora,
              "consts": consts, "rows": rows, "rel": rel}
    arrays = {k: np.ascontiguousarray(v) for k, v in arrays.items()}
    args = [nc.dram_tensor(k, v.shape, mybir.dt.from_np(v.dtype), kind="ExternalInput").ap() for k, v in arrays.items()]
    out = nc.dram_tensor("out", (TOK, D), F32, kind="ExternalOutput").ap()
    program(nc, *args, out)
    res = run_bass_kernel_spmd(nc, [arrays], core_ids=[0])
    return res.results[0]["out"].reshape(1, TOK, D)
```
